# Optimizing a Trainium2 kernel written in Bass

```python
import numpy as np
import jax
import jax.numpy as jnp

def _softmax(x, axis=-1):
    return jax.nn.softmax(x, axis=axis)

def _gelu(x):
    return jax.nn.gelu(x, approximate=True)

def _silu(x):
    return jax.nn.silu(x)

def _sigmoid(x):
    return jax.nn.sigmoid(x)

def _layernorm(x, axis=-1, eps=1e-05):
    m = jnp.mean(x, axis=axis, keepdims=True)
    v = jnp.var(x, axis=axis, keepdims=True)
    return (x - m) / jnp.sqrt(v + eps)

def _scatter_add(tgt, idx, src, axis=0):
    return tgt.at[idx].add(src)

def _segment_sum(src, seg, n):
    return jax.ops.segment_sum(src, seg, n)
kernel_name = 'mk_seq_preln_d1_jaxref_r8_197ccc'

def setup_inputs(seed: int=0):
    np.random.seed(seed)
    _w = jnp.asarray

    def _L0_attn_setup():
        import jax, jax.numpy as jnp
        import numpy as np
        import math
        H = 8
        D = 32
        DEPTH = 1
        LAMBDA_INIT = 0.8 - 0.6 * math.exp(-0.3 * DEPTH)
        EPS = 1e-08
        key = jax.random.key(seed)
        ks = jax.random.split(key, 9)
        B, T, IN_DIM, OUT_DIM = (2, 256, 128, 128)
        E = 2 * H * D
        inp = {'x': jax.random.normal(ks[0], (B, T, IN_DIM), dtype=jnp.float32), 'Wq': jax.random.normal(ks[1], (IN_DIM, E), dtype=jnp.float32) * IN_DIM ** (-0.5), 'Wkv': jax.random.normal(ks[2], (IN_DIM, 2 * E), dtype=jnp.float32) * IN_DIM ** (-0.5), 'Wout': jax.random.normal(ks[3], (E, OUT_DIM), dtype=jnp.float32) * E ** (-0.5), 'lambda_q1': 0.1 * jax.random.normal(ks[4], (D,), dtype=jnp.float32), 'lambda_k1': 0.1 * jax.random.normal(ks[5], (D,), dtype=jnp.float32), 'lambda_q2': 0.1 * jax.random.normal(ks[6], (D,), dtype=jnp.float32), 'lambda_k2': 0.1 * jax.random.normal(ks[7], (D,), dtype=jnp.float32), 'gamma': jnp.ones((2 * D,), dtype=jnp.float32)}
        return inp
    _L0_attn_in = _L0_attn_setup()

    def _L0_ffn_setup():
        import jax, jax.numpy as jnp
        import numpy as np
        HIDDEN = 128
        HEAD_DIM = 64
        N_EXPERTS = 16
        MIN_EXPERTS = 2
        B, T = (4, 256)

        def _normalize(x, axis):
            n = jnp.sqrt(jnp.sum(x * x, axis=axis, keepdims=True))
            return x / jnp.maximum(n, 1e-12)

        def _ste(x):
            hard = jax.lax.stop_gradient((x > 0).astype(x.dtype))
            return hard + x - jax.lax.stop_gradient(x)

        def _gating(hidden_states, sim_matrix, gates):
            b, t, c = hidden_states.shape
            flat = hidden_states.reshape(b * t, c)
            logits = _normalize(flat, -1) @ _normalize(sim_matrix, 0) - jax.nn.sigmoid(gates)
            gated = jax.nn.relu(logits)
            mask = _ste(gated)
            inactive = jnp.sum(mask, axis=1) == 0
            _, fb_idx = jax.lax.top_k(logits, MIN_EXPERTS)
            fb = jnp.zeros_like(mask).at[jnp.arange(b * t)[:, None], fb_idx].set(1.0)
            fb_applied = inactive[:, None] & (fb > 0)
            mask = jnp.where(fb_applied, 1.0, mask)
            masked_logits = jnp.where(mask > 0, gated, -jnp.inf)
            return jax.nn.softmax(masked_logits, axis=-1).reshape(b, t, -1)
        key = jax.random.key(seed)
        ks = jax.random.split(key, 6)
        xav_qkv = float(np.sqrt(6.0 / (HIDDEN + HEAD_DIM)))
        return {'hidden_states': jax.random.normal(ks[0], (B, T, HIDDEN), dtype=jnp.float32), 'sim_matrix': jax.random.normal(ks[1], (HIDDEN, N_EXPERTS), dtype=jnp.float32), 'gates': jnp.zeros((N_EXPERTS,), dtype=jnp.float32), 'q_proj': jax.random.uniform(ks[2], (N_EXPERTS, HIDDEN, HEAD_DIM), jnp.float32, -xav_qkv, xav_qkv), 'k_proj': jax.random.uniform(ks[3], (N_EXPERTS, HIDDEN, HEAD_DIM), jnp.float32, -xav_qkv, xav_qkv), 'v_proj': jax.random.uniform(ks[4], (N_EXPERTS, HIDDEN, HEAD_DIM), jnp.float32, -xav_qkv, xav_qkv), 'o_proj': jax.random.uniform(ks[5], (N_EXPERTS, HEAD_DIM, HIDDEN), jnp.float32, -xav_qkv, xav_qkv)}
    _L0_ffn_in = _L0_ffn_setup()
    _d = {'L0_attn_x': _L0_attn_in['x'], 'L0_attn_Wq': _L0_attn_in['Wq'], 'L0_attn_Wkv': _L0_attn_in['Wkv'], 'L0_attn_Wout': _L0_attn_in['Wout'], 'L0_attn_lambda_q1': _L0_attn_in['lambda_q1'], 'L0_attn_lambda_k1': _L0_attn_in['lambda_k1'], 'L0_attn_lambda_q2': _L0_attn_in['lambda_q2'], 'L0_attn_lambda_k2': _L0_attn_in['lambda_k2'], 'L0_attn_gamma': _L0_attn_in['gamma'], 'L0_ffn_sim_matrix': _L0_ffn_in['sim_matrix'], 'L0_ffn_gates': _L0_ffn_in['gates'], 'L0_ffn_q_proj': _L0_ffn_in['q_proj'], 'L0_ffn_k_proj': _L0_ffn_in['k_proj'], 'L0_ffn_v_proj': _L0_ffn_in['v_proj'], 'L0_ffn_o_proj': _L0_ffn_in['o_proj']}
    _x0 = _d['L0_attn_x']
    _d['L0_attn_x'] = jax.random.normal(jax.random.fold_in(jax.random.key(seed), 1), (4, 1024, 128), dtype=_x0.dtype)
    del _x0
    return _d

def reference(L0_attn_x, L0_attn_Wq, L0_attn_Wkv, L0_attn_Wout, L0_attn_lambda_q1, L0_attn_lambda_k1, L0_attn_lambda_q2, L0_attn_lambda_k2, L0_attn_gamma, L0_ffn_sim_matrix, L0_ffn_gates, L0_ffn_q_proj, L0_ffn_k_proj, L0_ffn_v_proj, L0_ffn_o_proj):

    def _L0_attn_ref(x, Wq, Wkv, Wout, lambda_q1, lambda_k1, lambda_q2, lambda_k2, gamma):
        import jax, jax.numpy as jnp
        import numpy as np
        import math
        H = 8
        D = 32
        DEPTH = 1
        LAMBDA_INIT = 0.8 - 0.6 * math.exp(-0.3 * DEPTH)
        EPS = 1e-08
        B, T, _ = x.shape
        scaling = D ** (-0.5)
        q = (x @ Wq).reshape(B, T, 2 * H, D).transpose(0, 2, 1, 3) * scaling
        kv = x @ Wkv
        k, v = jnp.split(kv, 2, axis=-1)
        k = k.reshape(B, T, 2 * H, D).transpose(0, 2, 1, 3)
        v = v.reshape(B, T, H, 2 * D).transpose(0, 2, 1, 3)
        dots = jnp.einsum('bhqd,bhkd->bhqk', q, k)
        attn_w = jax.nn.softmax(dots.astype(jnp.float32), axis=-1).astype(dots.dtype)
        lam1 = jnp.exp(jnp.sum(lambda_q1 * lambda_k1))
        lam2 = jnp.exp(jnp.sum(lambda_q2 * lambda_k2))
        lam = lam1 - lam2 + LAMBDA_INIT
        attn_w = attn_w.reshape(B, H, 2, T, T)
        attn_w = attn_w[:, :, 0] - lam * attn_w[:, :, 1]
        attn = jnp.einsum('bhqk,bhkd->bhqd', attn_w, v)
        rms = jnp.sqrt(jnp.mean(attn * attn, axis=-1, keepdims=True))
        attn = gamma * (attn / (rms + EPS))
        attn = attn * (1.0 - LAMBDA_INIT)
        attn = attn.transpose(0, 2, 1, 3).reshape(B, T, 2 * H * D)
        return attn @ Wout

    def _L0_ffn_ref(hidden_states, sim_matrix, gates, q_proj, k_proj, v_proj, o_proj):
        import jax, jax.numpy as jnp
        import numpy as np
        HIDDEN = 128
        HEAD_DIM = 64
        N_EXPERTS = 16
        MIN_EXPERTS = 2
        B, T = (4, 256)

        def _normalize(x, axis):
            n = jnp.sqrt(jnp.sum(x * x, axis=axis, keepdims=True))
            return x / jnp.maximum(n, 1e-12)

        def _ste(x):
            hard = jax.lax.stop_gradient((x > 0).astype(x.dtype))
            return hard + x - jax.lax.stop_gradient(x)

        def _gating(hidden_states, sim_matrix, gates):
            b, t, c = hidden_states.shape
            flat = hidden_states.reshape(b * t, c)
            logits = _normalize(flat, -1) @ _normalize(sim_matrix, 0) - jax.nn.sigmoid(gates)
            gated = jax.nn.relu(logits)
            mask = _ste(gated)
            inactive = jnp.sum(mask, axis=1) == 0
            _, fb_idx = jax.lax.top_k(logits, MIN_EXPERTS)
            fb = jnp.zeros_like(mask).at[jnp.arange(b * t)[:, None], fb_idx].set(1.0)
            fb_applied = inactive[:, None] & (fb > 0)
            mask = jnp.where(fb_applied, 1.0, mask)
            masked_logits = jnp.where(mask > 0, gated, -jnp.inf)
            return jax.nn.softmax(masked_logits, axis=-1).reshape(b, t, -1)
        b, t, c = hidden_states.shape
        rw = _gating(hidden_states, sim_matrix, gates)
        q = jnp.einsum('bte,bted->btd', rw, jnp.einsum('btc,ecd->bted', hidden_states, q_proj))
        k = jnp.einsum('bte,bted->btd', rw, jnp.einsum('btc,ecd->bted', hidden_states, k_proj))
        v = jnp.einsum('bte,bted->btd', rw, jnp.einsum('btc,ecd->bted', hidden_states, v_proj))
        scale = 1.0 / jnp.sqrt(jnp.asarray(HEAD_DIM, dtype=q.dtype))
        scores = jnp.einsum('bqd,bkd->bqk', q, k) * scale
        causal = jnp.tril(jnp.ones((t, t), dtype=bool))
        scores = jnp.where(causal, scores, -jnp.inf)
        attn = jnp.einsum('bqk,bkd->bqd', jax.nn.softmax(scores, axis=-1), v)
        mixed = attn[:, :, None, :] * rw[..., None]
        return jnp.einsum('bted,edc->btc', mixed, o_proj)
    x = L0_attn_x
    x = x + _L0_attn_ref(_layernorm(x, axis=-1), L0_attn_Wq, L0_attn_Wkv, L0_attn_Wout, L0_attn_lambda_q1, L0_attn_lambda_k1, L0_attn_lambda_q2, L0_attn_lambda_k2, L0_attn_gamma)
    x = x + _L0_ffn_ref(_layernorm(x, axis=-1), L0_ffn_sim_matrix, L0_ffn_gates, L0_ffn_q_proj, L0_ffn_k_proj, L0_ffn_v_proj, L0_ffn_o_proj)
    return x

_drawn_inputs = setup_inputs


def setup_inputs(seed=0):
    import zlib

    import numpy as np

    out = dict(_drawn_inputs(seed))
    spreads = {'L0_attn_gamma': (1.0, 0.2), 'L0_ffn_gates': (0.0, 0.1)}
    factors = {'L0_attn_lambda_q2': 4.454, 'L0_attn_lambda_k2': 4.239}
    for name, (base, spread) in spreads.items():
        noise = np.random.default_rng([zlib.crc32(name.encode()), seed]).standard_normal(out[name].shape)
        drawn = base * np.exp(spread * noise) if base else spread * noise
        out[name] = jnp.asarray(drawn.astype(out[name].dtype))
    for name, factor in factors.items():
        out[name] = (out[name] * factor).astype(out[name].dtype)
    return out
```

```python
import math
from contextlib import ExitStack

import numpy as np
import concourse.bass as bass
from concourse import mybir

F32 = mybir.dt.float32
F16 = mybir.dt.float16
BF16 = mybir.dt.bfloat16
U32 = mybir.dt.uint32
ALU = mybir.AluOpType
ACT = mybir.ActivationFunctionType
AX = mybir.AxisListType

P = 128
B, T, C = 4, 1024, 128
NT = T // P
H, D = 8, 32
DV = 2 * D
G = H // 2
STEPS = B * G
UNITS = 16
ITERS = STEPS // 2
SLOTS = 2 * UNITS
HALF = T // 2
LAMBDA_INIT = 0.8 - 0.6 * math.exp(-0.3)
QSCALE = D ** -0.5
RMS_EPS = 1e-8
LN_EPS = 1e-5

TRANS_LAG = 2
PV_LAG = 10
PV_END = PV_LAG + NT - 1
COPY_LAG = PV_END + 1
ROWS_LAG = COPY_LAG + 1
STAT_LAG = ROWS_LAG + 2
NORM_LAG = STAT_LAG + 2
COLS_LAG = NORM_LAG
PROJECT_LAG = COLS_LAG + 1
TAIL_SLOTS = PROJECT_LAG + 3
PROJ_SLOTS = {1: ("k0", 1), 4: ("v1", 0), 5: ("k1", 1), 9: ("q0", 2), 12: ("v0", 1), 13: ("q1", 2)}
PARTS = ("q0", "q1", "k0", "k1", "v0", "v1")
AHEAD = [("q0", 0), ("q1", 0), ("k0", 0), ("k1", 0), ("v0", 0), ("q0", 1), ("q1", 1)]

E, DE = 16, 64
MASKED = -1e30
GATE_LEAST = 1e-12
PART2_LAG = 3
RSQ_SHIFT = 2.0 ** 30
RSQ_LEAST = 2.0 ** -64


def unit_of(s):
    j, u = divmod(s, UNITS)
    return j, j % 2, u // 8, (u // 4) % 2, u % 4, u % 8


def present(half, first, last):
    return not (first and half < 0) and not (last and half > 3)


def half_at(s, lag, first, last):
    half, rest = divmod(s - lag, 8)
    return half if rest == 0 and present(half, first, last) else None


def misc_fill(s, first, last):
    for stage, lag in (("rows", ROWS_LAG), ("cols", COLS_LAG), ("project", PROJECT_LAG)):
        if (s - lag) % 8 == 0:
            half = half_at(s, lag, first, last)
            return None if half is None else (stage, half)
    if s % UNITS not in PROJ_SLOTS or (first and s < 0):
        return None
    part, ahead = PROJ_SLOTS[s % UNITS]
    step = s // UNITS + ahead
    return None if last and step > 1 else (part, step)


def misc_fill_before(s, first, last):
    for r in range(s - 1, s - UNITS - 1, -1):
        if first and r < 0:
            return ("q1", 1)
        if found := misc_fill(r, first, last):
            return found


def block_kernel(nc, x, wq, wkv, wout, lq1, lk1, lq2, lk2, gamma, sim, gates, eq, ek, ev, eo, out):
    ctx = ExitStack()
    with ctx:
        stack_of = {"memory": ctx}

        def sb(name, shape, dt=F32):
            return stack_of["memory"].enter_context(nc.sbuf_tensor(name, shape, dt))

        def ps(name, shape, dt=F32):
            return stack_of["memory"].enter_context(nc.psum_tensor(name, shape, dt))

        def sem(name):
            return ctx.enter_context(nc.semaphore(name))

        resid = sb("resid", [P, B * NT, C])
        xnT = sb("xnT", [P, B * T])
        wo_sb = sb("wo_sb", [P, G, C])
        gcol = sb("gcol", [P, 1])
        ident = sb("ident", [P, P])
        lam_in = sb("lam_in", [P, 4, D])
        lam_pr = sb("lam_pr", [P, 2, D])
        lam = sb("lam", [P, 6])
        stat = sb("stat", [P, 8, NT])
        simn = sb("simn", [P, E])
        sgate = sb("sgate", [P, E])
        small = sb("small", [P, 8, E])
        iota = sb("iota", [P, E])
        ones = sb("ones", [P, P])
        identb = sb("identb", [P, P], BF16)
        identh = sb("identh", [P, P], F16)
        causal = sb("causal", [P, P], BF16)

        part1 = ExitStack()
        stack_of["memory"] = part1
        xg = sb("xg", [P, 2, T])
        wg = sb("wg", [P, 2, 3, P])
        split = sb("split", [P, 4, T], F16)
        qa = sb("qa", [P, 2, 4, T], F16)
        ka = sb("ka", [P, 2, 4, T], F16)
        v_sb = sb("v_sb", [P, 2, NT, P])
        prob = sb("prob", [P, 2, 2, T])
        mixed = sb("mixed", [P, 2, T])
        probT = sb("probT", [P, 2, NT, 2, HALF])
        negmax = sb("negmax", [P, 2, 2])
        sums = sb("sums", [P, 4, 2, 8])
        recip2 = sb("recip2", [P, 2])
        ccol = sb("ccol", [P, 2])
        attnT = sb("attnT", [P, HALF])
        attn = sb("attn", [P, 4, 2, DV])
        attn_sq = sb("attn_sq", [P, 4, 2, DV])
        attn_n = sb("attn_n", [P, 4, 2, DV])
        attn_nT = sb("attn_nT", [P, 4, P])
        tl = sb("tl", [P, 12, 8])
        xc = probT[:, 0, 0:2, :, :].rearrange("p a b c -> p (a b c)")[:, 0:T]
        xsq = probT[:, 0, 2:4, :, :].rearrange("p a b c -> p (a b c)")[:, 0:T]
        xn = probT[:, 0, 4:6, :, :].rearrange("p a b c -> p (a b c)")[:, 0:T]

        score_ps = ps("score_ps", [P, 2, T])
        trans_ps = ps("trans_ps", [P, 2, 512])
        attn_ps = ps("attn_ps", [P, HALF])
        misc_ps = ps("misc_ps", [P, 512])

        part1.close()
        stack_of["memory"] = ctx
        ew = sb("ew", [P, E, 3 * DE])
        eow = sb("eow", [P, E // 2, C])
        x2T_all = sb("x2T_all", [P, B * T])
        x2c = sb("x2c", [P, T])
        x2sq = sb("x2sq", [P, T])
        x2n = sb("x2n", [P, T])
        x2T = sb("x2T", [P, T])
        gs = sb("gs", [P, 8, NT])
        gl = sb("gl", [P, 10, NT, E])
        top8 = sb("top8", [P, NT, 8])
        top8i = sb("top8i", [P, NT, 8], U32)
        top2f = sb("top2f", [P, NT, 2])
        rw_all = sb("rw_all", [P, B * NT, E])
        rw = sb("rw", [P, NT, E])
        xr = sb("xr", [P, 4, P])
        acc = sb("acc", [P, 2, 3 * DE])
        kv2 = sb("kv2", [P, NT, 2 * DE])
        qs = sb("qs", [P, 2, 3, P], F16)
        qkT = sb("qkT", [P, 3, T], F16)
        p2 = sb("p2", [P, 2, T])
        p2T = sb("p2T", [P, NT, P])
        nm2 = sb("nm2", [P, 2])
        sum2 = sb("sum2", [P, 2])
        rec2 = sb("rec2", [P, 2])
        mx = sb("mx", [P, 2, E, DE])
        mxT = sb("mxT", [P, E // 2, P])
        yo = sb("yo", [P, 2, C])

        exp_ps = ps("exp_ps", [P, 2, 512])
        s2_ps = ps("s2_ps", [P, T])
        t2_ps = ps("t2_ps", [P, 2, 512])
        qk_ps = ps("qk_ps", [P, 1024], F16)
        o2_ps = ps("o2_ps", [P, 512])

        x_in, w_in, const_in = sem("x_in"), sem("w_in"), sem("const_in")
        ident_ok, lam_ok, wo_ok, lam_chain, lam_exp = (sem(n) for n in ("ident_ok", "lam_ok", "wo_ok", "lam_chain", "lam_exp"))
        ln_v, ln_sq, ln_y, ln_T, ln_evA, ln_evV = (sem(n) for n in ("ln_v", "ln_sq", "ln_y", "ln_T", "ln_evA", "ln_evV"))
        step_in = (sem("step_in_even"), sem("step_in_odd"))
        stacked = {"q": sem("q_stacked"), "k": sem("k_stacked")}
        filled = {part: sem("filled_" + part) for part in PARTS}
        high_ok = {"q": sem("q_high_ok"), "k": sem("k_high_ok")}
        low_ok = {"q": sem("q_low_ok"), "k": sem("k_low_ok")}
        v_ok, begun, scaled = sem("v_ok"), sem("begun"), sem("scaled")
        score_ok, max_ok, exp_ok, rec_ok, c_ok, mix_ok = (sem(n) for n in ("score_ok", "max_ok", "exp_ok", "rec_ok", "c_ok", "mix_ok"))
        trans_ok, probT_A, probT_V, pv_ok, attnT_ok = (sem(n) for n in ("trans_ok", "probT_A", "probT_V", "pv_ok", "attnT_ok"))
        rows_ok, attn_copied, tail_v, ln_ok, y_ok = (sem(n) for n in ("rows_ok", "attn_copied", "tail_v", "ln_ok", "y_ok"))
        cols_ok, attn_nT_ok, out_ok, resid_ok = (sem(n) for n in ("cols_ok", "attn_nT_ok", "out_ok", "resid_ok"))
        done = sem("done")
        experts_in = sem("experts_in")
        const2_in, iota_ok, mask_ok = sem("const2_in"), sem("iota_ok"), sem("mask_ok")
        c2_v, c2_a, c2_p = sem("c2_v"), sem("c2_a"), sem("c2_p")
        g_v, g_sq, g_y, g_T, g_evA, g_evV, g_lg, g_exp, g_copied = (
            sem("g_" + n) for n in ("v", "sq", "y", "T", "evA", "evV", "lg", "exp", "copied"))
        xr_in = [sem(f"xr_in{r}") for r in range(4)]
        (e_ps, e_v, rw_ok, hi2, lo2, qkt_ps, qkt_ok, s2_ok, max2, exp2, t2_ok, t2_A, t2_V, pv2, rec2_ok, mx_ok,
         mt_ok, mt_A, mt_V, o_ok, y_done, kv_ok, q_out) = (sem("p2_" + n) for n in (
            "e_ps", "e_v", "rw_ok", "hi", "lo", "qkt_ps", "qkt_ok", "s_ok", "max", "exp", "t_ok", "t_A", "t_V", "pv",
            "rec", "mx_ok", "mt_ok", "mt_A", "mt_V", "o_ok", "y_done", "kv_ok", "q_out"))
        stored = [sem("stored0"), sem("stored1")]

        LNV = 10
        GV, GEXP = 50, 46
        C2V = 10
        TLV = 13

        def misc_free(eng, s, it, first, last):
            kind, which = misc_fill_before(s, first, last)
            if kind in PARTS:
                read(eng, kind, 2 * it + which)
            elif kind == "rows":
                eng.wait_ge(attn_copied, 2 * (4 * it + which + 1))
            elif kind == "cols":
                eng.wait_ge(attn_nT_ok, 4 * it + which + 1)
            else:
                eng.wait_ge(resid_ok, 4 * it + which + 1)

        def read(eng, part, j):
            eng.wait_ge(v_ok if part[0] == "v" else low_ok[part[0]], 2 * j + int(part[1]) + 1)

        block = ctx.enter_context(nc.Block())

        @block.sync
        def _(sp):
            for b in range(B):
                sp.dma_start(resid[:, b * NT:(b + 1) * NT, :],
                             x[b].rearrange("(t p) c -> p t c", p=P)).then_inc(x_in, 16)
            for n, v in enumerate((lq1, lk1, lq2, lk2)):
                sp.dma_start(lam_in[:, n, :], v.rearrange("(a d) -> a d", a=1).to_broadcast([P, D])).then_inc(const_in, 16)
            sp.dma_start(gcol[0:DV, :], gamma.rearrange("(d a) -> d a", a=1)).then_inc(const_in, 16)
            sp.dma_start(gcol[DV:P, :], gamma.rearrange("(d a) -> d a", a=1)).then_inc(const_in, 16)
            sp.dma_start(wo_sb[:, :, :], wout.rearrange("(g p) c -> p g c", p=P)).then_inc(const_in, 16)

            sp.dma_start(simn[:, :], sim).then_inc(const2_in, 16)
            sp.dma_start(sgate[:, :], gates.rearrange("(a e) -> a e", a=1).to_broadcast([P, E])).then_inc(const2_in, 16)
            out_rows = out.rearrange("b (t p) c -> p (b t) c", p=P)

            def load_step(par, b, g):
                for n, w in enumerate((wq[:, bass.ds(g * P, P)], wkv[:, bass.ds(g * P, P)],
                                       wkv[:, bass.ds(g * P + H * DV, P)])):
                    sp.dma_start(wg[:, par, n, :], w).then_inc(step_in[par], 16)
                sp.dma_start(xg[:, par, :], xnT[:, bass.ds(b * T, T)]).then_inc(step_in[par], 16)

            def stack(kind, par, j):
                dst, base, order = {"q": (qa, 0, (0, 0, 1, 1)), "k": (ka, 2, (0, 1, 0, 1))}[kind]
                sp.wait_ge(low_ok[kind], 2 * (j + 1))
                for row, part in enumerate(order):
                    for sub in range(4):
                        sp.dma_start(dst[D * row:D * row + D, par, sub, :],
                                     split[D * sub:D * sub + D, base + part, :]).then_inc(stacked[kind], 16)

            sp.wait_ge(ln_evA, B)
            sp.wait_ge(ln_evV, B)
            load_step(0, 0, 0)
            load_step(1, 0, 1)
            stack("q", 0, 0)
            stack("k", 0, 0)
            stack("q", 1, 1)

            def two_steps(it, first, last):
                for k in range(2):
                    j = 2 * it + k
                    if not (last and k == 1):
                        if not (first and k == 0):
                            sp.wait_ge(score_ok, 2 * UNITS * j)
                        stack("k", (k + 1) % 2, j + 1)
                    if not last:
                        sp.wait_ge(filled["v1"], j + 1)
                        load_step(k, (j + 2) // G, (j + 2) % G)
                        sp.wait_ge(score_ok, 2 * UNITS * (j + 1))
                        stack("q", k, j + 2)

            two_steps(0, True, False)
            with sp.Fori(1, ITERS - 1) as it:
                two_steps(it, False, False)
            two_steps(ITERS - 1, False, True)
            sp.wait_ge(resid_ok, 2 * STEPS)
            for n, w in enumerate((eq, ek, ev)):
                sp.dma_start(ew[:, :, n * DE:(n + 1) * DE], w.rearrange("e c d -> c e d")).then_inc(experts_in, 16)
            for half in range(2):
                sp.dma_start(eow[half * DE:(half + 1) * DE, :, :],
                             eo.rearrange("(g two) d c -> two d g c", two=2)[half]).then_inc(experts_in, 16)
            for b in range(B):
                sp.wait_ge(g_evA, b + 1)
                sp.wait_ge(g_evV, b + 1)
                sp.dma_start(x2T_all[:, b * T:(b + 1) * T], x2T[:, :]).then_inc(g_copied, 16)
            sp.wait_ge(g_copied, 16 * B)

            def tiles2(it, first, last):
                for t in range(NT + PART2_LAG if last else NT):
                    m = NT * it + t
                    if t < NT:
                        if not (first and t < 4):
                            sp.wait_ge(e_ps, 8 * (m - 3))
                        sp.dma_start(xr[:, t % 4, :], x2T_all[:, bass.ds(m * P, P)]).then_inc(xr_in[t % 4], 16)
                    v = t - PART2_LAG
                    if not (first and v < 0):
                        sp.wait_ge(y_done, m - PART2_LAG + 1)
                        tile = m - PART2_LAG
                        sp.dma_start(out_rows[:, bass.ds(tile, 1), :], yo[:, v % 2:v % 2 + 1, :]).then_inc(stored[v % 2], 16)

            tiles2(0, True, False)
            with sp.Fori(1, B - 1) as it:
                tiles2(it, False, False)
            tiles2(B - 1, False, True)
            for r in range(2):
                sp.wait_ge(stored[r], 16 * B * NT // 2)

        @block.gpsimd
        def _(pool):
            pool.memset(ident[:, :], 0.0).then_inc(ident_ok, 1)
            pool.wait_ge(ident_ok, 1)
            pool.affine_select(out=ident[:, :], in_=ident[:, :], compare_op=ALU.not_equal, fill=1.0, base=0,
                               pattern=[[-1, P]], channel_multiplier=1).then_inc(ident_ok, 1)

            pool.memset(ones[:, :], 1.0).then_inc(iota_ok, 1)
            for e in range(E):
                pool.memset(iota[:, e:e + 1], float(e)).then_inc(iota_ok, 1)
            pool.memset(causal[:, :], 0.0).then_inc(mask_ok, 1)
            pool.wait_ge(mask_ok, 1)
            pool.affine_select(out=causal[:, :], in_=causal[:, :], compare_op=ALU.is_ge, fill=MASKED, base=0,
                               pattern=[[-1, P]], channel_multiplier=1).then_inc(mask_ok, 1)
            for i in (identb, identh):
                pool.memset(i[:, :], 0.0).then_inc(mask_ok, 1)
            pool.wait_ge(mask_ok, 4)
            for i in (identb, identh):
                pool.affine_select(out=i[:, :], in_=i[:, :], compare_op=ALU.not_equal, fill=1.0, base=0,
                                   pattern=[[-1, P]], channel_multiplier=1).then_inc(mask_ok, 1)

            def mix(n, r, peeled):
                pool.wait_ge(c_ok, n + 1)
                pool.sem_inc(begun, 1)
                pool.tensor_scalar(prob[:, r, 1, :], prob[:, r, 1, :], ccol[:, r:r + 1], None, ALU.mult).then_inc(scaled, 1)
                pool.wait_ge(scaled, n + 1)
                if not (peeled and n < 2):
                    pool.wait_ge(trans_ok, 2 * (n - 1))
                pool.tensor_tensor(mixed[:, r, :], prob[:, r, 0, :], prob[:, r, 1, :], ALU.add).then_inc(mix_ok, 1)
            mix(0, 0, True)
            mix(1, 1, True)
            with pool.Fori(1, STEPS * UNITS // 2) as pair:
                mix(2 * pair, 0, False)
                mix(2 * pair + 1, 1, False)

        @block.tensor
        def _(pe):
            pe.wait_ge(ident_ok, 2)

            def ln_transposes(b):
                pe.wait_ge(ln_v, LNV * (b + 1))
                if b > 0:
                    pe.wait_ge(ln_evA, b)
                    pe.wait_ge(ln_evV, b)
                for t in range(NT):
                    mm = pe.transpose(score_ps[:, 0, t * P:(t + 1) * P], xn[:, t * P:(t + 1) * P], ident[:, :])
                    if t % 4 == 3:
                        mm.then_inc(ln_T, 1)
            for b in range(B):
                ln_transposes(b)

            def proj_fill(part, j, par, pair):
                if part == "q0":
                    pe.wait_ge(step_in[par], 64 * (pair + 1))
                half = int(part[1])
                if part[0] != "v":
                    mm = pe.matmul(misc_ps[:, :], wg[:, par, "qk".index(part[0]), :],
                                   xg[:, par, half * HALF:(half + 1) * HALF], start=True, stop=True)
                else:
                    for t in range(4):
                        tile = half * 4 + t
                        mm = pe.matmul(misc_ps[:, t * P:(t + 1) * P], xg[:, par, tile * P:(tile + 1) * P],
                                       wg[:, par, 2, :], start=True, stop=True)
                mm.then_inc(filled[part], 1)

            before = None
            for part, j in AHEAD:
                if before:
                    read(pe, *before)
                proj_fill(part, j, j, 0)
                before = (part, j)

            def scores(n, s, sub, peeled):
                j, par, half, head, qt, _ = unit_of(s)
                if not (peeled and n < 1):
                    pe.wait_ge(exp_ok, 2 * n - 1 + sub)
                q0 = (half * 4 + qt) * P
                for kh in range(2):
                    mm = pe.matmul(score_ps[:, sub, kh * HALF:(kh + 1) * HALF],
                                   qa[:, par, head * 2 + sub, q0:q0 + P],
                                   ka[:, par, head * 2 + sub, kh * HALF:(kh + 1) * HALF], start=True, stop=True)
                mm.then_inc(score_ok, 1)

            def slots(it, first, last):
                peeled = first or last
                end = SLOTS - 8 + TAIL_SLOTS if last else SLOTS
                if first:
                    pe.wait_ge(stacked["q"], 256)
                    pe.wait_ge(stacked["k"], 256)
                    scores(0, 0, 0, True)
                    scores(0, 0, 1, True)
                for s in range(end):
                    n = SLOTS * it + s
                    ahead = not (last and s + 1 >= SLOTS)
                    if ahead and (s + 1) % UNITS == 0:
                        j = 2 * it + (s + 1) // UNITS
                        pe.wait_ge(stacked["q"], 256 * (j + 1))
                        pe.wait_ge(stacked["k"], 256 * (j + 1))
                    if ahead:
                        scores(n + 1, s + 1, 0, peeled)
                    u = s - TRANS_LAG
                    if not (first and u < 0) and not (last and u >= SLOTS):
                        pe.wait_ge(mix_ok, n - TRANS_LAG + 1)
                        for kb in range(2):
                            if not (first and u == 0):
                                pe.wait_ge((probT_A, probT_V)[kb], n - TRANS_LAG)
                            for t in range(4):
                                k0 = (kb * 4 + t) * P
                                mm = pe.transpose(trans_ps[:, kb, t * P:(t + 1) * P], mixed[:, u % 2, k0:k0 + P], ident[:, :])
                            mm.then_inc(trans_ok, 1)
                    if ahead:
                        scores(n + 1, s + 1, 1, peeled)
                    half, kt = divmod(s - PV_LAG, 8)
                    if present(half, first, last):
                        par = (half // 2) % 2
                        if kt == 0:
                            pe.wait_ge(probT_A, 8 * (4 * it + half + 1))
                            pe.wait_ge(probT_V, 8 * (4 * it + half + 1))
                            if not (first and half == 0):
                                pe.wait_ge(attnT_ok, 4 * it + half)
                        if half % 2 == 0 and kt in (0, 4):
                            pe.wait_ge(v_ok, 2 * (2 * it + half // 2) + kt // 4 + 1)
                        for head in range(2):
                            mm = pe.matmul(attn_ps[head * DV:(head + 1) * DV, :],
                                           v_sb[:, par, kt, head * DV:(head + 1) * DV],
                                           probT[:, half % 2, kt, head, :], start=kt == 0, stop=kt == 7)
                        mm.then_inc(pv_ok, 1)
                    fill = misc_fill(s, first, last)
                    if fill:
                        misc_free(pe, s, it, first, last)
                        kind, which = fill
                        if kind in PARTS:
                            proj_fill(kind, 2 * it + which, which % 2, it + which // 2)
                        elif kind == "rows":
                            pe.wait_ge(attnT_ok, 4 * it + which + 1)
                            for t in range(4):
                                mm = pe.transpose(misc_ps[:, t * P:(t + 1) * P], attnT[:, t * P:(t + 1) * P], ident[:, :])
                            mm.then_inc(rows_ok, 1)
                        elif kind == "cols":
                            pe.wait_ge(tail_v, TLV * (4 * it + which + 1))
                            for t in range(4):
                                mm = pe.transpose(misc_ps[:, t * P:(t + 1) * P],
                                                  attn_n[:, t, :, :].rearrange("p h d -> p (h d)"), ident[:, :])
                            mm.then_inc(cols_ok, 1)
                        else:
                            pe.wait_ge(attn_nT_ok, 4 * it + which + 1)
                            if which == 0 and first:
                                pe.wait_ge(wo_ok, 1)
                            step = 2 * it + which // 2
                            wo_g = wo_sb[:, bass.ds(step % G, 1), :].rearrange("p a c -> p (a c)")
                            for t in range(4):
                                mm = pe.matmul(misc_ps[:, t * P:(t + 1) * P], attn_nT[:, t, :], wo_g,
                                               start=True, stop=True)
                            mm.then_inc(out_ok, 1)

            slots(0, True, False)
            with pe.Fori(1, ITERS - 1) as it:
                slots(it, False, False)
            slots(ITERS - 1, False, True)

            pe.wait_ge(resid_ok, 2 * STEPS)
            pe.wait_ge(c2_v, 1)
            pe.wait_ge(iota_ok, 1)
            pe.wait_ge(mask_ok, 6)
            pe.matmul(exp_ps[:, 0, 0:E], ones[:, :], small[:, 0, :], start=True, stop=True).then_inc(c2_p, 1)
            for b in range(B):
                pe.wait_ge(g_v, GV * b + 10)
                for t in range(NT):
                    mm = pe.transpose(t2_ps[:, t // 4, t % 4 * P:(t % 4 + 1) * P], x2n[:, t * P:(t + 1) * P], ident[:, :])
                    if t % 4 == 3:
                        mm.then_inc(g_T, 1)
                pe.wait_ge(g_evA, b + 1)
                pe.wait_ge(g_evV, b + 1)
                pe.wait_ge(c2_v, C2V)
                for t in range(NT):
                    mm = pe.matmul(exp_ps[:, 0, t * E:(t + 1) * E], x2T[:, t * P:(t + 1) * P], simn[:, :],
                                   start=True, stop=True)
                mm.then_inc(g_lg, 1)
            pe.wait_ge(experts_in, 16 * 5)
            pe.wait_ge(g_v, GV * B)

            def tiles2(it, first, last):
                for t in range(NT + PART2_LAG if last else NT):
                    m = NT * it + t

                    def live(lag):
                        return not (first and t < lag) and not (last and t - lag >= NT)

                    def experts(c):
                        if not live(0):
                            return
                        if c == 0:
                            pe.wait_ge(xr_in[t % 4], 16 * (2 * it + t // 4 + 1))
                        if not (first and t == 0 and c < 2):
                            pe.wait_ge(e_v, 8 * m + c - 1)
                        pe.matmul(exp_ps[:, c % 2, 0:6 * DE], xr[:, t % 4, :],
                                  ew[:, 2 * c:2 * c + 2, :].rearrange("p e d -> p (e d)"),
                                  start=True, stop=True).then_inc(e_ps, 1)

                    experts(0)
                    if live(1):
                        v = (t - 1) % NT
                        pe.wait_ge(hi2, 2 * m)
                        pe.wait_ge(lo2, 2 * m)
                        if not (first and t == 1):
                            pe.wait_ge(qkt_ok, m - 1)
                        for n in range(3):
                            mm = pe.transpose(qk_ps[:, n * P:(n + 1) * P], qs[:, v % 2, n, :], identh[:, :])
                        mm.then_inc(qkt_ps, 1)
                    experts(1)
                    if live(2):
                        v = (t - 2) % NT
                        pe.wait_ge(exp2, m - 1)
                        if not (first and t < 4):
                            pe.wait_ge(mt_A, m - 3)
                            pe.wait_ge(mt_V, m - 3)
                        elif t == 3:
                            pe.wait_ge(t2_A, m - 2)
                            pe.wait_ge(t2_V, m - 2)
                        for kb in range(v + 1):
                            mm = pe.transpose(t2_ps[:, kb // 4, kb % 4 * P:(kb % 4 + 1) * P],
                                              p2[:, v % 2, kb * P:(kb + 1) * P], ident[:, :])
                        mm.then_inc(t2_ok, 1)
                    experts(2)
                    if live(3):
                        v = (t - 3) % NT
                        pe.wait_ge(mx_ok, m - 2)
                        if live(2):
                            pe.wait_ge(t2_A, m - 1)
                            pe.wait_ge(t2_V, m - 1)
                        elif last:
                            pe.wait_ge(mt_A, m - 3)
                            pe.wait_ge(mt_V, m - 3)
                        for g in range(8):
                            mm = pe.transpose(t2_ps[:, g // 4, g % 4 * P:(g % 4 + 1) * P],
                                              mx[:, v % 2, 2 * g:2 * g + 2, :].rearrange("p e d -> p (e d)"), ident[:, :])
                            if g % 4 == 3:
                                mm.then_inc(mt_ok, 1)
                    experts(3)
                    if live(1):
                        v = (t - 1) % NT
                        pe.wait_ge(qkt_ok, m)
                        if not (first and t == 1):
                            pe.wait_ge(exp2, m - 1)
                        keys = (v + 1) * P
                        for k0 in range(0, keys, 512):
                            k1 = min(k0 + 512, keys)
                            diag = k1 == keys
                            pe.matmul(s2_ps[:, k0:k1], qkT[:, 0, v * P:(v + 1) * P], qkT[:, 1, k0:k1], start=True, stop=False)
                            mm = pe.matmul(s2_ps[:, k0:k1], qkT[:, 0, v * P:(v + 1) * P], qkT[:, 2, k0:k1], start=False, stop=not diag)
                            if diag:
                                mm = pe.matmul(s2_ps[:, k1 - P:k1], identb[:, :], causal[:, :], start=False, stop=True)
                        mm.then_inc(s2_ok, 1)
                    experts(4)
                    if live(2):
                        v = (t - 2) % NT
                        pe.wait_ge(t2_A, m - 1)
                        pe.wait_ge(t2_V, m - 1)
                        pe.wait_ge(kv_ok, m - 1)
                        if not (first and t < 4):
                            pe.wait_ge(y_done, m - 3)
                        elif not (first and t == 2):
                            pe.wait_ge(mx_ok, m - 2)
                        for kb in range(v + 1):
                            mm = pe.matmul(o2_ps[:, 0:2 * DE], p2T[:, kb, :], kv2[:, kb, :], start=kb == 0, stop=kb == v)
                        mm.then_inc(pv2, 1)
                    experts(5)
                    if live(3):
                        pe.wait_ge(mt_A, m - 2)
                        pe.wait_ge(mt_V, m - 2)
                        if live(2):
                            pe.wait_ge(mx_ok, m - 1)
                        for g in range(8):
                            mm = pe.matmul(o2_ps[:, 0:C], mxT[:, g, :], eow[:, g, :], start=g == 0, stop=g == 7)
                        mm.then_inc(o_ok, 1)
                    experts(6)
                    experts(7)

            tiles2(0, True, False)
            with pe.Fori(1, B - 1) as it:
                tiles2(it, False, False)
            tiles2(B - 1, False, True)

        @block.scalar
        def _(act):
            act.preload_act_table_set("natural_log_exp_and_others")
            act.wait_ge(lam_chain, 3)
            act.activation(lam[:, 2:4], lam[:, 0:2], ACT.Exp).then_inc(lam_exp, 1)
            for b in range(B):
                act.wait_ge(ln_v, LNV * b + 3)
                act.activation(xsq, xc, ACT.Square).then_inc(ln_sq, 1)
                act.wait_ge(ln_v, LNV * b + 5)
                act.activation(stat[:, 3, :], stat[:, 2, :], ACT.Ln).then_inc(ln_y, 1)
                act.wait_ge(ln_y, 2 * b + 1)
                act.activation(stat[:, 4, :], stat[:, 3, :], ACT.Exp, scale=-0.5).then_inc(ln_y, 1)
                act.wait_ge(ln_T, 2 * b + 1)
                act.activation(xnT[:, b * T:b * T + HALF], score_ps[:, 0, 0:HALF], ACT.Copy).then_inc(ln_evA, 1)

            def proj_copy(part, j, par, wait_old):
                act.wait_ge(filled[part], j + 1)
                kind, half = part[0], int(part[1])
                if kind != "v":
                    if half == 0 and wait_old:
                        act.wait_ge(stacked[kind], 256 * j)
                    act.activation(split[:, 2 * "qk".index(kind), half * HALF:(half + 1) * HALF], misc_ps[:, :],
                                   ACT.Copy, scale=QSCALE if kind == "q" else 1.0).then_inc(high_ok[kind], 1)
                else:
                    act.activation(v_sb[:, par, half * 4:(half + 1) * 4, :],
                                   misc_ps[:, :].rearrange("p (t d) -> p t d", t=4), ACT.Copy).then_inc(v_ok, 1)

            for part, j in AHEAD:
                proj_copy(part, j, j, j > 0)

            def slots(it, first, last):
                end = SLOTS - 8 + TAIL_SLOTS if last else SLOTS
                for s in range(end):
                    n = SLOTS * it + s

                    def softmax(sub):
                        act.wait_ge(max_ok, 2 * n + sub + 1)
                        if sub == 0 and not (first and s < 2):
                            act.wait_ge(mix_ok, n - 1)
                        act.activation(prob[:, s % 2, sub, :], score_ps[:, sub, :], ACT.Exp,
                                       bias=negmax[:, s % 2, sub:sub + 1],
                                       accum_out=sums[:, s // 8, sub, s % 8:s % 8 + 1]).then_inc(exp_ok, 1)

                    if s < SLOTS:
                        softmax(0)
                        softmax(1)
                    half = half_at(s, COPY_LAG, first, last)
                    if half is not None:
                        act.wait_ge(pv_ok, 8 * (4 * it + half + 1))
                        if not (first and half == 0):
                            act.wait_ge(rows_ok, 4 * it + half)
                        act.activation(attnT[:, :], attn_ps[:, :], ACT.Copy).then_inc(attnT_ok, 1)
                    fill = None if first and s == 0 else misc_fill(s - 1, first, last)
                    if fill and fill[0] in PARTS:
                        part, step = fill
                        proj_copy(part, 2 * it + step, step % 2, True)
                    elif fill and fill[0] == "rows":
                        act.wait_ge(rows_ok, 4 * it + fill[1] + 1)
                        act.activation(attn[:, :, :, :].rearrange("p t h d -> p (t h d)"), misc_ps[:, :],
                                       ACT.Copy).then_inc(attn_copied, 1)
                        act.activation(attn_sq[:, :, :, :].rearrange("p t h d -> p (t h d)"), misc_ps[:, :],
                                       ACT.Square).then_inc(attn_copied, 1)
                    elif fill and fill[0] == "cols":
                        act.wait_ge(cols_ok, 4 * it + fill[1] + 1)
                        act.activation(attn_nT[:, :, :].rearrange("p t q -> p (t q)"), misc_ps[:, :],
                                       ACT.Copy).then_inc(attn_nT_ok, 1)
                    v = s - TRANS_LAG
                    if not (first and v < 0) and not (last and v >= SLOTS):
                        half, u = v // 8, v % 8
                        if u == 0 and not (first and half < 2):
                            act.wait_ge(pv_ok, 8 * (4 * it + half - 1))
                        act.wait_ge(trans_ok, 2 * (n - TRANS_LAG) + 1)
                        act.activation(probT[:, half % 2, 0:4, u // 4, (u % 4) * P:(u % 4 + 1) * P],
                                       trans_ps[:, 0, :].rearrange("p (k q) -> p k q", k=4),
                                       ACT.Copy).then_inc(probT_A, 1)
                    half = half_at(s, STAT_LAG, first, last)
                    if half is not None:
                        act.wait_ge(tail_v, TLV * (4 * it + half) + 5)
                        act.activation(tl[:, 3, :], tl[:, 2, :], ACT.Ln).then_inc(ln_ok, 1)
                        act.wait_ge(ln_ok, 4 * it + half + 1)
                        act.activation(tl[:, 4, :], tl[:, 3, :], ACT.Exp, scale=-0.5).then_inc(y_ok, 1)

            slots(0, True, False)
            with act.Fori(1, ITERS - 1) as it:
                slots(it, False, False)
            slots(ITERS - 1, False, True)

            def rsqrt_seed(y, l, v, ready, n, done_sem, k):
                act.wait_ge(ready, n)
                act.activation(l, v, ACT.Ln).then_inc(done_sem, 1)
                act.wait_ge(done_sem, k + 1)
                act.activation(y, l, ACT.Exp, scale=-0.5).then_inc(done_sem, 1)

            act.wait_ge(resid_ok, 2 * STEPS)
            act.activation(small[:, 6, :], sgate[:, :], ACT.Exp, scale=-1.0).then_inc(c2_a, 1)
            rsqrt_seed(small[:, 3, :], small[:, 2, :], small[:, 1, :], c2_v, 2, c2_a, 1)
            for b in range(B):
                act.wait_ge(g_v, GV * b + 3)
                act.activation(x2sq[:, :], x2c[:, :], ACT.Square).then_inc(g_sq, 1)
                rsqrt_seed(gs[:, 4, :], gs[:, 3, :], gs[:, 2, :], g_v, GV * b + 5, g_y, 4 * b)
                act.wait_ge(g_v, GV * b + 10)
                act.activation(x2sq[:, :], x2n[:, :], ACT.Square).then_inc(g_sq, 1)
                act.wait_ge(g_T, 2 * b + 1)
                if b > 0:
                    act.wait_ge(g_lg, b)
                    act.wait_ge(g_copied, 16 * b)
                act.activation(x2T[:, 0:HALF], t2_ps[:, 0, :], ACT.Copy).then_inc(g_evA, 1)
                rsqrt_seed(gs[:, 4, :], gs[:, 3, :], gs[:, 2, :], g_v, GV * b + 12, g_y, 4 * b + 2)
                act.wait_ge(g_v, GV * b + GEXP)
                act.activation(gl[:, 8, :, :], gl[:, 7, :, :], ACT.Exp).then_inc(g_exp, 1)

            def tiles2(it, first, last):
                for t in range(NT + PART2_LAG if last else NT):
                    m = NT * it + t

                    def live(lag):
                        return not (first and t < lag) and not (last and t - lag >= NT)

                    if live(1):
                        v = (t - 1) % NT
                        act.wait_ge(qkt_ps, m)
                        if not (first and t == 1):
                            act.wait_ge(s2_ok, m - 1)
                        act.activation(qkT[:, :, v * P:(v + 1) * P], qk_ps[:, 0:3 * P].rearrange("p (n q) -> p n q", n=3),
                                       ACT.Copy).then_inc(qkt_ok, 1)
                    if live(2):
                        v = (t - 2) % NT
                        act.wait_ge(t2_ok, m - 1)
                        if not (first and t == 2):
                            act.wait_ge(pv2, m - 2)
                        blocks = min(v + 1, 4)
                        act.activation(p2T[:, 0:blocks, :], t2_ps[:, 0, 0:blocks * P].rearrange("p (k q) -> p k q", k=blocks),
                                       ACT.Copy).then_inc(t2_A, 1)
                    if live(3):
                        act.wait_ge(mt_ok, 2 * (m - 2) - 1)
                        if not (first and t == 3):
                            act.wait_ge(o_ok, m - 3)
                        act.activation(mxT[:, 0:4, :], t2_ps[:, 0, :].rearrange("p (g q) -> p g q", g=4), ACT.Copy).then_inc(mt_A, 1)
                    if live(1):
                        v = (t - 1) % NT
                        keys = (v + 1) * P
                        act.wait_ge(max2, m)
                        if not (first and t < 3):
                            act.wait_ge(t2_ok, m - 2)
                        act.activation(p2[:, v % 2, 0:keys], s2_ps[:, 0:keys], ACT.Exp, bias=nm2[:, v % 2:v % 2 + 1],
                                       accum_out=sum2[:, v % 2:v % 2 + 1]).then_inc(exp2, 1)
                        if not (first and t < 2):
                            act.wait_ge(pv2, m - 1)
                        act.activation(kv2[:, v, :], acc[:, v % 2, DE:3 * DE], ACT.Copy).then_inc(kv_ok, 1)
                    if live(0):
                        act.wait_ge(e_v, 8 * m + 8)
                        if not (first and t < 2):
                            act.wait_ge(qkt_ps, m - 1)
                        act.activation(qs[:, t % 2, 0, 0:DE], acc[:, t % 2, 0:DE], ACT.Copy, scale=DE ** -0.5).then_inc(hi2, 1)
                        act.activation(qs[:, t % 2, 1, :].rearrange("p (n d) -> p n d", n=2),
                                       acc[:, t % 2, DE:2 * DE].unsqueeze(1).to_broadcast([P, 2, DE]), ACT.Copy).then_inc(hi2, 1)

            tiles2(0, True, False)
            with act.Fori(1, B - 1) as it:
                tiles2(it, False, False)
            tiles2(B - 1, False, True)

        @block.vector
        def _(dve):
            dve.wait_ge(const_in, 7 * 16)
            for n in range(2):
                dve.tensor_tensor(lam_pr[:, n, :], lam_in[:, 2 * n, :], lam_in[:, 2 * n + 1, :], ALU.mult).then_inc(lam_chain, 1)
            dve.wait_ge(lam_chain, 2)
            dve.tensor_reduce(lam[:, 0:2], lam_pr[:, :, :], AX.X, ALU.add).then_inc(lam_chain, 1)
            dve.tensor_scalar(wo_sb[:, :, :], wo_sb[:, :, :], gcol[:, :], 1.0 - LAMBDA_INIT, ALU.mult, ALU.mult).then_inc(wo_ok, 1)
            dve.wait_ge(lam_exp, 1)
            dve.tensor_tensor(lam[:, 4:5], lam[:, 3:4], lam[:, 2:3], ALU.subtract).then_inc(lam_chain, 1)
            dve.wait_ge(lam_chain, 4)
            dve.tensor_scalar(lam[:, 5:6], lam[:, 4:5], LAMBDA_INIT, None, ALU.subtract).then_inc(lam_ok, 1)
            dve.wait_ge(lam_ok, 1)

            def newton(y, v, t, u, sm, base):
                dve.tensor_tensor(t, v, y, ALU.mult).then_inc(sm, 1)
                dve.wait_ge(sm, base + 1)
                dve.tensor_tensor(u, t, y, ALU.mult).then_inc(sm, 1)
                dve.wait_ge(sm, base + 2)
                dve.tensor_scalar(u, u, -0.5, 1.5, ALU.mult, ALU.add).then_inc(sm, 1)
                dve.wait_ge(sm, base + 3)

            def tiles(ap):
                return ap.rearrange("p (t c) -> p t c", t=NT)

            for b in range(B):
                k = LNV * b
                dve.wait_ge(x_in, 16 * B)
                xb = resid[:, b * NT:(b + 1) * NT, :]
                dve.tensor_reduce(stat[:, 0, :], xb, AX.X, ALU.add).then_inc(ln_v, 1)
                dve.wait_ge(ln_v, k + 1)
                dve.tensor_scalar(stat[:, 1, :], stat[:, 0, :], -1.0 / C, None, ALU.mult).then_inc(ln_v, 1)
                dve.wait_ge(ln_v, k + 2)
                dve.tensor_tensor(tiles(xc), xb, stat[:, 1, :].unsqueeze(2).to_broadcast([P, NT, C]), ALU.add).then_inc(ln_v, 1)
                dve.wait_ge(ln_sq, b + 1)
                dve.tensor_reduce(stat[:, 0, :], tiles(xsq), AX.X, ALU.add).then_inc(ln_v, 1)
                dve.wait_ge(ln_v, k + 4)
                dve.tensor_scalar(stat[:, 2, :], stat[:, 0, :], 1.0 / C, LN_EPS, ALU.mult, ALU.add).then_inc(ln_v, 1)
                dve.wait_ge(ln_y, 2 * b + 2)
                newton(stat[:, 4, :], stat[:, 2, :], stat[:, 5, :], stat[:, 6, :], ln_v, k + 5)
                dve.tensor_tensor(stat[:, 7, :], stat[:, 4, :], stat[:, 6, :], ALU.mult).then_inc(ln_v, 1)
                dve.wait_ge(ln_v, k + 9)
                if b > 0:
                    dve.wait_ge(ln_T, 2 * b)
                dve.tensor_tensor(tiles(xn), tiles(xc), stat[:, 7, :].unsqueeze(2).to_broadcast([P, NT, C]), ALU.mult).then_inc(ln_v, 1)
                dve.wait_ge(ln_T, 2 * b + 2)
                dve.tensor_copy(xnT[:, b * T + HALF:(b + 1) * T], score_ps[:, 0, HALF:T]).then_inc(ln_evV, 1)

            def proj_low(part, j):
                kind, half = part[0], int(part[1])
                dve.wait_ge(high_ok[kind], 2 * j + half + 1)
                cols = slice(half * HALF, (half + 1) * HALF)
                row = 2 * "qk".index(kind)
                dve.scalar_tensor_tensor(out=split[:, row + 1, cols], in0=misc_ps[:, :],
                                         scalar=QSCALE if kind == "q" else 1.0, in1=split[:, row, cols],
                                         op0=ALU.mult, op1=ALU.subtract).then_inc(low_ok[kind], 1)

            for part, j in AHEAD:
                if part[0] != "v":
                    proj_low(part, j)

            def slots(it, first, last):
                end = SLOTS - 8 + TAIL_SLOTS if last else SLOTS
                for s in range(end):
                    n = SLOTS * it + s

                    def row_max(sub):
                        dve.wait_ge(score_ok, 2 * n + sub + 1)
                        dve.tensor_reduce(negmax[:, s % 2, sub:sub + 1], score_ps[:, sub, :], AX.X, ALU.max,
                                          negate=True).then_inc(max_ok, 1)

                    if s < SLOTS:
                        row_max(0)
                    if not (first and s < 1) and not (last and s > SLOTS):
                        r = (s - 1) % 2
                        half, u = ((s - 1) // 8) % 4, (s - 1) % 8
                        dve.wait_ge(exp_ok, 2 * n)
                        dve.reciprocal(recip2[:, r:r + 1], sums[:, half, 1, u:u + 1]).then_inc(rec_ok, 1)
                        dve.wait_ge(rec_ok, n)
                        dve.scalar_tensor_tensor(out=ccol[:, r:r + 1], in0=recip2[:, r:r + 1], scalar=lam[:, 5:6],
                                                 in1=sums[:, half, 0, u:u + 1], op0=ALU.mult,
                                                 op1=ALU.mult).then_inc(c_ok, 1)
                    v = s - TRANS_LAG - 1
                    if not (first and v < 0) and not (last and v >= SLOTS):
                        half, u = v // 8, v % 8
                        if u == 0 and not (first and half < 2):
                            dve.wait_ge(pv_ok, 8 * (4 * it + half - 1))
                        dve.wait_ge(trans_ok, 2 * (n - TRANS_LAG))
                        dve.tensor_copy(probT[:, half % 2, 4:8, u // 4, (u % 4) * P:(u % 4 + 1) * P],
                                        trans_ps[:, 1, :].rearrange("p (k q) -> p k q", k=4)).then_inc(probT_V, 1)
                    if s < SLOTS:
                        row_max(1)
                    fill = None if first and s < 2 else misc_fill(s - 2, first, last)
                    if fill and fill[0] in PARTS and fill[0][0] != "v":
                        proj_low(fill[0], 2 * it + fill[1])
                    half = half_at(s, PROJECT_LAG + 1, first, last)
                    if half is not None:
                        step = 2 * it + half // 2
                        tile0 = (step // G) * NT + (half % 2) * 4
                        dve.wait_ge(out_ok, 4 * it + half + 1)
                        rows = resid[:, bass.ds(tile0, 4), :]
                        dve.tensor_tensor(rows, rows, misc_ps[:, :].rearrange("p (t c) -> p t c", t=4),
                                          ALU.add).then_inc(resid_ok, 1)
                    half = half_at(s, STAT_LAG, first, last)
                    if half is not None:
                        k = TLV * (4 * it + half)
                        dve.wait_ge(attn_copied, 2 * (4 * it + half + 1))
                        dve.tensor_reduce(tl[:, 0, :].rearrange("p (h t) -> p h t", h=2),
                                          attn_sq[:, :, :, :].rearrange("p t h d -> p h t d"), AX.X, ALU.add).then_inc(tail_v, 1)
                        dve.reciprocal(tl[:, 1, :], sums[:, half % 4, 0, :]).then_inc(tail_v, 1)
                        dve.wait_ge(tail_v, k + 2)
                        dve.tensor_tensor(tl[:, 2, :], tl[:, 0, :], tl[:, 1, :], ALU.mult).then_inc(tail_v, 1)
                        dve.wait_ge(tail_v, k + 3)
                        dve.tensor_tensor(tl[:, 2, :], tl[:, 2, :], tl[:, 1, :], ALU.mult).then_inc(tail_v, 1)
                        dve.wait_ge(tail_v, k + 4)
                        dve.tensor_scalar(tl[:, 2, :], tl[:, 2, :], RSQ_SHIFT / DV, RSQ_LEAST, ALU.mult, ALU.max).then_inc(tail_v, 1)
                    half = half_at(s, NORM_LAG, first, last)
                    if half is not None:
                        k = TLV * (4 * it + half)
                        dve.wait_ge(y_ok, 4 * it + half + 1)
                        newton(tl[:, 4, :], tl[:, 2, :], tl[:, 5, :], tl[:, 6, :], tail_v, k + 5)
                        dve.tensor_tensor(tl[:, 7, :], tl[:, 5, :], tl[:, 6, :], ALU.mult).then_inc(tail_v, 1)
                        dve.wait_ge(tail_v, k + 9)
                        dve.tensor_scalar(tl[:, 8, :], tl[:, 7, :], RSQ_SHIFT ** -0.5, RMS_EPS, ALU.mult, ALU.add).then_inc(tail_v, 1)
                        dve.wait_ge(tail_v, k + 10)
                        dve.reciprocal(tl[:, 9, :], tl[:, 8, :]).then_inc(tail_v, 1)
                        dve.wait_ge(tail_v, k + 11)
                        dve.tensor_tensor(tl[:, 10, :], tl[:, 9, :], tl[:, 1, :], ALU.mult).then_inc(tail_v, 1)
                        dve.wait_ge(tail_v, k + 12)
                        dve.tensor_tensor(attn_n[:, :, :, :], attn[:, :, :, :],
                                          tl[:, 10, :].rearrange("p (h t) -> p t h", h=2).unsqueeze(3).to_broadcast([P, 4, 2, DV]),
                                          ALU.mult).then_inc(tail_v, 1)

            slots(0, True, False)
            with dve.Fori(1, ITERS - 1) as it:
                slots(it, False, False)
            slots(ITERS - 1, False, True)

            links = {}

            def link(ins, sm):
                links[sm.name] = links.get(sm.name, 0) + 1
                ins.then_inc(sm, 1)
                dve.wait_ge(sm, links[sm.name])

            dve.wait_ge(const2_in, 16 * 2)
            dve.wait_ge(iota_ok, 1 + E)
            dve.wait_ge(resid_ok, 2 * STEPS)
            link(dve.tensor_tensor(small[:, 0, :], simn[:, :], simn[:, :], ALU.mult), c2_v)
            dve.wait_ge(c2_p, 1)
            link(dve.tensor_scalar(small[:, 1, :], exp_ps[:, 0, 0:E], RSQ_SHIFT, RSQ_LEAST, ALU.mult, ALU.max), c2_v)
            dve.wait_ge(c2_a, 3)
            link(dve.tensor_scalar(small[:, 6, :], small[:, 6, :], 1.0, None, ALU.add), c2_v)
            link(dve.reciprocal(sgate[:, :], small[:, 6, :]), c2_v)

            def polished(y, v, t, u, sm):
                link(dve.tensor_tensor(t, v, y, ALU.mult), sm)
                link(dve.tensor_tensor(t, t, y, ALU.mult), sm)
                link(dve.tensor_scalar(t, t, -0.5, 1.5, ALU.mult, ALU.add), sm)
                link(dve.tensor_tensor(u, t, y, ALU.mult), sm)

            polished(small[:, 3, :], small[:, 1, :], small[:, 4, :], small[:, 5, :], c2_v)
            link(dve.tensor_scalar(small[:, 5, :], small[:, 5, :], RSQ_SHIFT ** 0.5, 1.0 / GATE_LEAST, ALU.mult, ALU.min), c2_v)
            link(dve.tensor_tensor(simn[:, :], simn[:, :], small[:, 5, :], ALU.mult), c2_v)
            assert links[c2_v.name] == C2V

            def per_token(ap):
                return ap.unsqueeze(2).to_broadcast([P, NT, E])

            def per_expert(ap):
                return ap.unsqueeze(1).to_broadcast([P, NT, E])

            for b in range(B):
                xb = resid[:, b * NT:(b + 1) * NT, :]
                link(dve.tensor_reduce(gs[:, 0, :], xb, AX.X, ALU.add), g_v)
                link(dve.tensor_scalar(gs[:, 1, :], gs[:, 0, :], -1.0 / C, None, ALU.mult), g_v)
                link(dve.tensor_tensor(tiles(x2c[:, :]), xb, gs[:, 1, :].unsqueeze(2).to_broadcast([P, NT, C]), ALU.add), g_v)
                dve.wait_ge(g_sq, 2 * b + 1)
                link(dve.tensor_reduce(gs[:, 0, :], tiles(x2sq[:, :]), AX.X, ALU.add), g_v)
                link(dve.tensor_scalar(gs[:, 2, :], gs[:, 0, :], 1.0 / C, LN_EPS, ALU.mult, ALU.add), g_v)
                dve.wait_ge(g_y, 4 * b + 2)
                polished(gs[:, 4, :], gs[:, 2, :], gs[:, 5, :], gs[:, 6, :], g_v)
                link(dve.tensor_tensor(tiles(x2n[:, :]), tiles(x2c[:, :]), gs[:, 6, :].unsqueeze(2).to_broadcast([P, NT, C]), ALU.mult), g_v)
                dve.wait_ge(g_sq, 2 * b + 2)
                link(dve.tensor_reduce(gs[:, 0, :], tiles(x2sq[:, :]), AX.X, ALU.add), g_v)
                link(dve.tensor_scalar(gs[:, 2, :], gs[:, 0, :], RSQ_SHIFT, RSQ_LEAST, ALU.mult, ALU.max), g_v)
                dve.wait_ge(g_T, 2 * b + 2)
                if b > 0:
                    dve.wait_ge(g_copied, 16 * b)
                dve.tensor_copy(x2T[:, HALF:T], t2_ps[:, 1, :]).then_inc(g_evV, 1)
                dve.wait_ge(g_y, 4 * b + 4)
                polished(gs[:, 4, :], gs[:, 2, :], gs[:, 5, :], gs[:, 6, :], g_v)
                link(dve.tensor_scalar(gs[:, 6, :], gs[:, 6, :], RSQ_SHIFT ** 0.5, 1.0 / GATE_LEAST, ALU.mult, ALU.min), g_v)
                dve.wait_ge(g_lg, b + 1)
                lg = gl[:, 0, :, :]
                link(dve.tensor_tensor(gl[:, 1, :, :], exp_ps[:, 0, 0:NT * E].rearrange("p (t e) -> p t e", t=NT),
                                       per_token(gs[:, 6, :]), ALU.mult), g_v)
                link(dve.tensor_tensor(lg, gl[:, 1, :, :], per_expert(sgate[:, :]), ALU.subtract), g_v)
                for t in range(NT):
                    link(dve.max(out=top8[:, t, :], in_=lg[:, t, :]), g_v)
                for t in range(NT):
                    link(dve.max_index(out=top8i[:, t, :], in_max=top8[:, t, :], in_values=lg[:, t, :]), g_v)
                link(dve.tensor_copy(top2f[:, :, :], top8i[:, :, 0:2]), g_v)
                for n in range(2):
                    link(dve.tensor_tensor(gl[:, 2 + n, :, :], per_expert(iota[:, :]),
                                           top2f[:, :, n:n + 1].to_broadcast([P, NT, E]), ALU.is_equal), g_v)
                link(dve.tensor_tensor(gl[:, 2, :, :], gl[:, 2, :, :], gl[:, 3, :, :], ALU.add), g_v)
                best = top8[:, :, 0:1].rearrange("p t a -> p (t a)")
                link(dve.tensor_scalar(gs[:, 0, :], best, 0.0, None, ALU.is_le), g_v)
                link(dve.tensor_tensor(gl[:, 2, :, :], gl[:, 2, :, :], per_token(gs[:, 0, :]), ALU.mult), g_v)
                link(dve.tensor_scalar(gl[:, 4, :, :], lg, 0.0, None, ALU.is_gt), g_v)
                link(dve.tensor_tensor(gl[:, 5, :, :], gl[:, 4, :, :], gl[:, 2, :, :], ALU.add), g_v)
                link(dve.tensor_scalar(gl[:, 6, :, :], lg, 0.0, None, ALU.max), g_v)
                link(dve.tensor_scalar(gs[:, 1, :], best, 0.0, None, ALU.max), g_v)
                link(dve.tensor_tensor(gl[:, 7, :, :], gl[:, 6, :, :], per_token(gs[:, 1, :]), ALU.subtract), g_v)
                assert links[g_v.name] == GV * b + GEXP
                dve.wait_ge(g_exp, b + 1)
                link(dve.tensor_tensor(gl[:, 9, :, :], gl[:, 8, :, :], gl[:, 5, :, :], ALU.mult), g_v)
                link(dve.tensor_reduce(gs[:, 0, :], gl[:, 9, :, :], AX.X, ALU.add), g_v)
                link(dve.reciprocal(gs[:, 1, :], gs[:, 0, :]), g_v)
                link(dve.tensor_tensor(rw_all[:, b * NT:(b + 1) * NT, :], gl[:, 9, :, :], per_token(gs[:, 1, :]), ALU.mult), g_v)
                assert links[g_v.name] == GV * (b + 1)

            def tiles2(it, first, last):
                for t in range(NT + PART2_LAG if last else NT):
                    m = NT * it + t

                    def live(lag):
                        return not (first and t < lag) and not (last and t - lag >= NT)

                    def add_up(c):
                        if not live(0):
                            return
                        if c == 0:
                            dve.tensor_copy(rw[:, t, :], rw_all[:, bass.ds(m, 1), :].rearrange("p a e -> p (a e)")).then_inc(rw_ok, 1)
                            dve.wait_ge(rw_ok, m + 1)
                            if not (first and t < 2):
                                dve.wait_ge(kv_ok, m - 1)
                                dve.wait_ge(hi2, 2 * (m - 1))
                        dve.wait_ge(e_ps, 8 * m + c + 1)
                        for e in range(2):
                            ex = 2 * c + e
                            src = exp_ps[:, c % 2, e * 3 * DE:(e + 1) * 3 * DE]
                            w = rw[:, t, ex:ex + 1]
                            if ex == 0:
                                ins = dve.tensor_scalar(acc[:, t % 2, :], src, w, None, ALU.mult)
                            else:
                                ins = dve.scalar_tensor_tensor(out=acc[:, t % 2, :], in0=src, scalar=w, in1=acc[:, t % 2, :],
                                                               op0=ALU.mult, op1=ALU.add)
                            if e == 0:
                                ins.then_inc(q_out, 1)
                                dve.wait_ge(q_out, 8 * m + c + 1)
                            else:
                                ins.then_inc(e_v, 1)
                                dve.wait_ge(e_v, 8 * m + c + 1)

                    add_up(0)
                    add_up(1)
                    if live(2):
                        v = (t - 2) % NT
                        dve.wait_ge(t2_ok, m - 1)
                        if not (first and t == 2):
                            dve.wait_ge(pv2, m - 2)
                        if v >= 4:
                            dve.tensor_copy(p2T[:, 4:v + 1, :], t2_ps[:, 1, 0:(v - 3) * P].rearrange("p (k q) -> p k q", k=v - 3)).then_inc(t2_V, 1)
                        else:
                            dve.sem_inc(t2_V, 1)
                    add_up(2)
                    if live(3):
                        dve.wait_ge(mt_ok, 2 * (m - 2))
                        if not (first and t == 3):
                            dve.wait_ge(o_ok, m - 3)
                        dve.tensor_copy(mxT[:, 4:8, :], t2_ps[:, 1, :].rearrange("p (g q) -> p g q", g=4)).then_inc(mt_V, 1)
                    add_up(3)
                    add_up(4)
                    if live(1):
                        v = (t - 1) % NT
                        dve.wait_ge(s2_ok, m)
                        dve.tensor_reduce(nm2[:, v % 2:v % 2 + 1], s2_ps[:, 0:(v + 1) * P], AX.X, ALU.max, negate=True).then_inc(max2, 1)
                    add_up(5)
                    if live(2):
                        v = (t - 2) % NT
                        dve.wait_ge(pv2, m - 1)
                        dve.reciprocal(rec2[:, v % 2:v % 2 + 1], sum2[:, v % 2:v % 2 + 1]).then_inc(rec2_ok, 1)
                        dve.wait_ge(rec2_ok, m - 1)
                        if not (first and t < 4):
                            dve.wait_ge(mt_ok, 2 * (m - 3))
                        dve.scalar_tensor_tensor(out=mx[:, v % 2, :, :], in0=o2_ps[:, DE:2 * DE].unsqueeze(1).to_broadcast([P, E, DE]),
                                                 scalar=rec2[:, v % 2:v % 2 + 1],
                                                 in1=rw[:, v, :].unsqueeze(2).to_broadcast([P, E, DE]),
                                                 op0=ALU.mult, op1=ALU.mult).then_inc(mx_ok, 1)
                    add_up(6)
                    if live(3):
                        v = (t - 3) % NT
                        dve.wait_ge(o_ok, m - 2)
                        if not (first and t < 5):
                            dve.wait_ge(stored[v % 2], 16 * (4 * it + (t - 5) // 2 + 1))
                        dve.tensor_tensor(yo[:, v % 2:v % 2 + 1, :], o2_ps[:, 0:C].unsqueeze(1), resid[:, bass.ds(m - 3, 1), :],
                                          ALU.add).then_inc(y_done, 1)
                    add_up(7)
                    if live(0):
                        dve.wait_ge(hi2, 2 * (m + 1))
                        dve.scalar_tensor_tensor(out=qs[:, t % 2, 0, DE:2 * DE], in0=acc[:, t % 2, 0:DE], scalar=DE ** -0.5,
                                                 in1=qs[:, t % 2, 0, 0:DE], op0=ALU.mult, op1=ALU.subtract).then_inc(lo2, 1)
                        dve.tensor_tensor(qs[:, t % 2, 2, :].rearrange("p (n d) -> p n d", n=2),
                                          acc[:, t % 2, DE:2 * DE].unsqueeze(1).to_broadcast([P, 2, DE]),
                                          qs[:, t % 2, 1, :].rearrange("p (n d) -> p n d", n=2), ALU.subtract).then_inc(lo2, 1)

            tiles2(0, True, False)
            with dve.Fori(1, B - 1) as it:
                tiles2(it, False, False)
            tiles2(B - 1, False, True)


_INS = ["L0_attn_x", "L0_attn_Wq", "L0_attn_Wkv", "L0_attn_Wout", "L0_attn_lambda_q1", "L0_attn_lambda_k1",
        "L0_attn_lambda_q2", "L0_attn_lambda_k2", "L0_attn_gamma", "L0_ffn_sim_matrix", "L0_ffn_gates",
        "L0_ffn_q_proj", "L0_ffn_k_proj", "L0_ffn_v_proj", "L0_ffn_o_proj"]


def kernel(**inputs):
    import concourse.bacc as bacc
    from concourse.bass_utils import run_bass_kernel_spmd

    nc = bacc.Bacc("TRN2", target_bir_lowering=False, num_devices=1)
    arrays, args = {}, []
    for name in _INS:
        a = np.ascontiguousarray(inputs[name])
        arrays[f"in_{name}"] = a
        args.append(nc.dram_tensor(f"in_{name}", a.shape, mybir.dt.from_np(a.dtype), kind="ExternalInput").ap())
    out = nc.dram_tensor("out_0", (B, T, C), F32, kind="ExternalOutput").ap()
    block_kernel(nc, *args, out)
    r = run_bass_kernel_spmd(nc, [arrays], core_ids=[0])
    return r.results[0]["out_0"]
```

```python
import math
from contextlib import ExitStack

import numpy as np
import concourse.bass as bass
from concourse import mybir

F32 = mybir.dt.float32
F16 = mybir.dt.float16
BF16 = mybir.dt.bfloat16
U32 = mybir.dt.uint32
ALU = mybir.AluOpType
ACT = mybir.ActivationFunctionType
AX = mybir.AxisListType

P = 128
B, T, C = 4, 1024, 128
NT = T // P
H, D = 8, 32
DV = 2 * D
G = H // 2
STEPS = B * G
UNITS = 16
ITERS = STEPS // 2
SLOTS = 2 * UNITS
HALF = T // 2
LAMBDA_INIT = 0.8 - 0.6 * math.exp(-0.3)
QSCALE = D ** -0.5
RMS_EPS = 1e-8
LN_EPS = 1e-5

TRANS_LAG = 3
SCALE_V = 768
DVE_COPIES = ()
RMS_AFTER = 4
PV_LAG = 11
PV_END = PV_LAG + NT - 1
COPY_LAG = PV_END
ROWS_LAG = COPY_LAG + 1
STAT_LAG = ROWS_LAG + 1
NORM_LAG = STAT_LAG + 3
COLS_LAG = NORM_LAG + 1
PROJECT_LAG = COLS_LAG + 1
TAIL_SLOTS = PROJECT_LAG + 3
PROJ_SLOTS = {2: ("k0", 1), 4: ("v1", 0), 6: ("k1", 1), 10: ("q0", 2), 12: ("v0", 1), 14: ("q1", 2)}
PARTS = ("q0", "q1", "k0", "k1", "v0", "v1")
AHEAD = [("q0", 0), ("q1", 0), ("k0", 0), ("k1", 0), ("v0", 0), ("q0", 1), ("q1", 1)]

E, DE = 16, 64
MASKED = -1e30
GATE_LEAST = 1e-12
PART2_LAG = 3
RSQ_SHIFT = 2.0 ** 30
RSQ_LEAST = 2.0 ** -64


def unit_of(s):
    j, u = divmod(s, UNITS)
    return j, j % 2, u // 8, (u // 4) % 2, u % 4, u % 8


def present(half, first, last):
    return not (first and half < 0) and not (last and half > 3)


def half_at(s, lag, first, last):
    half, rest = divmod(s - lag, 8)
    return half if rest == 0 and present(half, first, last) else None


def misc_fill(s, first, last):
    for stage, lag in (("rows", ROWS_LAG), ("cols", COLS_LAG), ("project", PROJECT_LAG)):
        if (s - lag) % 8 == 0:
            half = half_at(s, lag, first, last)
            return None if half is None else (stage, half)
    if s % UNITS not in PROJ_SLOTS or (first and s < 0):
        return None
    part, ahead = PROJ_SLOTS[s % UNITS]
    step = s // UNITS + ahead
    return None if last and step > 1 else (part, step)


def misc_fill_before(s, first, last):
    for r in range(s - 1, s - UNITS - 1, -1):
        if first and r < 0:
            return ("q1", 1)
        if found := misc_fill(r, first, last):
            return found


def block_kernel(nc, x, wq, wkv, wout, lq1, lk1, lq2, lk2, gamma, sim, gates, eq, ek, ev, eo, out):
    ctx = ExitStack()
    with ctx:
        stack_of = {"memory": ctx}

        def sb(name, shape, dt=F32):
            return stack_of["memory"].enter_context(nc.sbuf_tensor(name, shape, dt))

        def ps(name, shape, dt=F32):
            return stack_of["memory"].enter_context(nc.psum_tensor(name, shape, dt))

        def sem(name):
            return ctx.enter_context(nc.semaphore(name))

        resid = sb("resid", [P, B * NT, C])
        xnT = sb("xnT", [P, B * T])
        wo_sb = sb("wo_sb", [P, G, C])
        gcol = sb("gcol", [P, 1])
        ident = sb("ident", [P, P])
        lam_in = sb("lam_in", [P, 4, D])
        lam_pr = sb("lam_pr", [P, 2, D])
        lam = sb("lam", [P, 6])
        stat = sb("stat", [P, 8, NT])
        simn = sb("simn", [P, E])
        sgate = sb("sgate", [P, E])
        small = sb("small", [P, 8, E])
        iota = sb("iota", [P, E])
        ones = sb("ones", [P, P])
        identb = sb("identb", [P, P], BF16)
        identh = sb("identh", [P, P], F16)
        causal = sb("causal", [P, P], BF16)

        part1 = ExitStack()
        stack_of["memory"] = part1
        xg = sb("xg", [P, 2, T])
        wg = sb("wg", [P, 2, 3, P])
        split = sb("split", [P, 4, T], F16)
        qa = sb("qa", [P, 2, 4, T], F16)
        ka = sb("ka", [P, 2, 4, T], F16)
        v_sb = sb("v_sb", [P, 2, NT, P])
        prob1 = sb("prob1", [P, 4, T])
        prob2 = sb("prob2", [P, 2, T])
        probT = sb("probT", [P, 2, NT, 2, HALF])
        negmax = sb("negmax", [P, 2, 2])
        sums = sb("sums", [P, 4, 2, 8])
        recip2 = sb("recip2", [P, 2])
        ccol = sb("ccol", [P, 2])
        attnT = sb("attnT", [P, HALF])
        attn = sb("attn", [P, 4, 2, DV])
        rms_const = sb("rms_const", [P, 2])
        attn_sq = sb("attn_sq", [P, 4, 2, DV])
        attn_n = sb("attn_n", [P, 4, 2, DV])
        attn_nT = sb("attn_nT", [P, 4, P])
        tl = sb("tl", [P, 12, 8])
        xc = probT[:, 0, 0:2, :, :].rearrange("p a b c -> p (a b c)")[:, 0:T]
        xsq = probT[:, 0, 2:4, :, :].rearrange("p a b c -> p (a b c)")[:, 0:T]
        xn = probT[:, 0, 4:6, :, :].rearrange("p a b c -> p (a b c)")[:, 0:T]

        score_ps = ps("score_ps", [P, 2, T])
        trans_ps = ps("trans_ps", [P, 2, 512])
        attn_ps = ps("attn_ps", [P, HALF])
        misc_ps = ps("misc_ps", [P, 512])

        part1.close()
        stack_of["memory"] = ctx
        ew = sb("ew", [P, E, 3 * DE])
        eow = sb("eow", [P, E // 2, C])
        x2T_all = sb("x2T_all", [P, B * T])
        x2c = sb("x2c", [P, T])
        x2sq = sb("x2sq", [P, T])
        x2n = sb("x2n", [P, T])
        x2T = sb("x2T", [P, T])
        gs = sb("gs", [P, 8, NT])
        gl = sb("gl", [P, 10, NT, E])
        top8 = sb("top8", [P, NT, 8])
        top8i = sb("top8i", [P, NT, 8], U32)
        top2f = sb("top2f", [P, NT, 2])
        rw_all = sb("rw_all", [P, B * NT, E])
        rw = sb("rw", [P, NT, E])
        xr = sb("xr", [P, 4, P])
        acc = sb("acc", [P, 2, 3 * DE])
        kv2 = sb("kv2", [P, NT, 2 * DE])
        qs = sb("qs", [P, 2, 3, P], F16)
        qkT = sb("qkT", [P, 3, T], F16)
        p2 = sb("p2", [P, 2, T])
        p2T = sb("p2T", [P, NT, P])
        nm2 = sb("nm2", [P, 2])
        sum2 = sb("sum2", [P, 2])
        rec2 = sb("rec2", [P, 2])
        mx = sb("mx", [P, 2, E, DE])
        mxT = sb("mxT", [P, E // 2, P])
        yo = sb("yo", [P, 2, C])

        exp_ps = ps("exp_ps", [P, 2, 512])
        s2_ps = ps("s2_ps", [P, T])
        t2_ps = ps("t2_ps", [P, 2, 512])
        qk_ps = ps("qk_ps", [P, 1024], F16)
        o2_ps = ps("o2_ps", [P, 512])

        x_in, w_in, const_in = sem("x_in"), sem("w_in"), sem("const_in")
        ident_ok, lam_ok, wo_ok, lam_chain, lam_exp = (sem(n) for n in ("ident_ok", "lam_ok", "wo_ok", "lam_chain", "lam_exp"))
        ln_v, ln_sq, ln_y, ln_T, ln_evA, ln_evV = (sem(n) for n in ("ln_v", "ln_sq", "ln_y", "ln_T", "ln_evA", "ln_evV"))
        step_in = (sem("step_in_even"), sem("step_in_odd"))
        stacked = {"q": sem("q_stacked"), "k": sem("k_stacked")}
        filled = {part: sem("filled_" + part) for part in PARTS}
        high_ok = {"q": sem("q_high_ok"), "k": sem("k_high_ok")}
        low_ok = {"q": sem("q_low_ok"), "k": sem("k_low_ok")}
        v_ok, scaled_P, scaled_V = sem("v_ok"), sem("scaled_P"), sem("scaled_V")
        score_ok, max_ok, exp_ok, rec_ok, c_ok, mix_ok = (sem(n) for n in ("score_ok", "max_ok", "exp_ok", "rec_ok", "c_ok", "mix_ok"))
        trans_ok, pv_ok, attnT_ok = (sem(n) for n in ("trans_ok", "pv_ok", "attnT_ok"))
        probT_ok = (sem("probT_ok_0"), sem("probT_ok_1"))
        rows_ok, attn_copied, stat_ok, rms_v, norm_v = (sem(n) for n in ("rows_ok", "attn_copied", "stat_ok", "rms_v", "norm_v"))
        cols_ok, attn_nT_ok, out_ok, resid_ok = (sem(n) for n in ("cols_ok", "attn_nT_ok", "out_ok", "resid_ok"))
        rms_const_ok = sem("rms_const_ok")
        experts_in = sem("experts_in")
        const2_in, iota_ok, mask_ok = sem("const2_in"), sem("iota_ok"), sem("mask_ok")
        c2_v, c2_a, c2_p = sem("c2_v"), sem("c2_a"), sem("c2_p")
        g_v, g_sq, g_y, g_T, g_evA, g_evV, g_lg, g_exp, g_copied = (
            sem("g_" + n) for n in ("v", "sq", "y", "T", "evA", "evV", "lg", "exp", "copied"))
        xr_in = [sem(f"xr_in{r}") for r in range(4)]
        (e_ps, e_v, rw_ok, hi2, lo2, qkt_ps, qkt_ok, s2_ok, max2, exp2, t2_ok, t2_A, t2_V, pv2, rec2_ok, mx_ok,
         mt_ok, mt_A, mt_V, o_ok, y_done, kv_ok, q_out) = (sem("p2_" + n) for n in (
            "e_ps", "e_v", "rw_ok", "hi", "lo", "qkt_ps", "qkt_ok", "s_ok", "max", "exp", "t_ok", "t_A", "t_V", "pv",
            "rec", "mx_ok", "mt_ok", "mt_A", "mt_V", "o_ok", "y_done", "kv_ok", "q_out"))
        stored = [sem("stored0"), sem("stored1")]

        LNV = 10
        GV, GEXP = 50, 46
        C2V = 10

        def misc_free(eng, s, it, first, last):
            kind, which = misc_fill_before(s, first, last)
            if kind in PARTS:
                read(eng, kind, 2 * it + which)
            elif kind == "rows":
                eng.wait_ge(attn_copied, 2 * (4 * it + which + 1))
            elif kind == "cols":
                eng.wait_ge(attn_nT_ok, 4 * it + which + 1)
            else:
                eng.wait_ge(resid_ok, 4 * it + which + 1)

        def read(eng, part, j):
            eng.wait_ge(v_ok if part[0] == "v" else low_ok[part[0]], 2 * j + int(part[1]) + 1)

        def copied_by_dve(s):
            return s % 8 in DVE_COPIES

        def copy_probT(eng, copy, it, s, n, bank, first, last):
            v = s - TRANS_LAG
            if (first and v < 0) or (last and v >= SLOTS):
                return
            half, u = v // 8, v % 8
            if u == 0 and not (first and half < 2):
                eng.wait_ge(pv_ok, 8 * (4 * it + half - 1))
            eng.wait_ge(trans_ok, 2 * (n - TRANS_LAG) + bank + 1)
            copy(probT[:, half % 2, 4 * bank:4 * bank + 4, u // 4, (u % 4) * P:(u % 4 + 1) * P],
                 trans_ps[:, bank, :].rearrange("p (k q) -> p k q", k=4)).then_inc(probT_ok[bank], 1)

        block = ctx.enter_context(nc.Block())

        @block.sync
        def _(sp):
            for b in range(B):
                sp.dma_start(resid[:, b * NT:(b + 1) * NT, :],
                             x[b].rearrange("(t p) c -> p t c", p=P)).then_inc(x_in, 16)
            for n, v in enumerate((lq1, lk1, lq2, lk2)):
                sp.dma_start(lam_in[:, n, :], v.rearrange("(a d) -> a d", a=1).to_broadcast([P, D])).then_inc(const_in, 16)
            sp.dma_start(gcol[0:DV, :], gamma.rearrange("(d a) -> d a", a=1)).then_inc(const_in, 16)
            sp.dma_start(gcol[DV:P, :], gamma.rearrange("(d a) -> d a", a=1)).then_inc(const_in, 16)
            sp.dma_start(wo_sb[:, :, :], wout.rearrange("(g p) c -> p g c", p=P)).then_inc(const_in, 16)

            sp.dma_start(simn[:, :], sim).then_inc(const2_in, 16)
            sp.dma_start(sgate[:, :], gates.rearrange("(a e) -> a e", a=1).to_broadcast([P, E])).then_inc(const2_in, 16)
            out_rows = out.rearrange("b (t p) c -> p (b t) c", p=P)

            def load_step(par, token0, column0):
                for n, w in enumerate((wq[:, bass.ds(column0, P)], wkv[:, bass.ds(column0, P)],
                                       wkv[:, bass.ds(column0 + H * DV, P)])):
                    sp.dma_start(wg[:, par, n, :], w).then_inc(step_in[par], 16)
                sp.dma_start(xg[:, par, :], xnT[:, bass.ds(token0, T)]).then_inc(step_in[par], 16)

            def stack(kind, par, j, scored=None):
                dst, base, order = {"q": (qa, 0, (0, 0, 1, 1)), "k": (ka, 2, (0, 1, 0, 1))}[kind]
                halves, tiles = 2 * (j + 1), None if scored is None else 2 * scored
                sp.wait_ge(low_ok[kind], halves)
                if scored is not None:
                    sp.wait_ge(score_ok, tiles)
                for row, part in enumerate(order):
                    for sub in range(4):
                        sp.dma_start(dst[D * row:D * row + D, par, sub, :],
                                     split[D * sub:D * sub + D, base + part, :]).then_inc(stacked[kind], 16)

            sp.wait_ge(ln_evA, B)
            sp.wait_ge(ln_evV, B)
            load_step(0, 0, 0)
            load_step(1, 0, P)
            stack("q", 0, 0)
            stack("k", 0, 0)
            stack("q", 1, 1)

            def two_steps(it, first, last):
                for k in range(2):
                    j = 2 * it + k
                    if not last:
                        token0, column0 = (j + 2) // G * T, (j + 2) % G * P
                        sp.wait_ge(filled["v1"], j + 1)
                        load_step(k, token0, column0)
                    if not (last and k == 1):
                        stack("k", (k + 1) % 2, j + 1, None if first and k == 0 else UNITS * j)
                    if not last:
                        stack("q", k, j + 2, UNITS * (j + 1))

            two_steps(0, True, False)
            with sp.Fori(1, ITERS - 1) as it:
                two_steps(it, False, False)
            two_steps(ITERS - 1, False, True)
            sp.wait_ge(resid_ok, 2 * STEPS)
            for n, w in enumerate((eq, ek, ev)):
                sp.dma_start(ew[:, :, n * DE:(n + 1) * DE], w.rearrange("e c d -> c e d")).then_inc(experts_in, 16)
            for half in range(2):
                sp.dma_start(eow[half * DE:(half + 1) * DE, :, :],
                             eo.rearrange("(g two) d c -> two d g c", two=2)[half]).then_inc(experts_in, 16)
            for b in range(B):
                sp.wait_ge(g_evA, b + 1)
                sp.wait_ge(g_evV, b + 1)
                sp.dma_start(x2T_all[:, b * T:(b + 1) * T], x2T[:, :]).then_inc(g_copied, 16)
            sp.wait_ge(g_copied, 16 * B)

            def tiles2(it, first, last):
                for t in range(NT + PART2_LAG if last else NT):
                    m = NT * it + t
                    if t < NT:
                        if not (first and t < 4):
                            sp.wait_ge(e_ps, 8 * (m - 3))
                        sp.dma_start(xr[:, t % 4, :], x2T_all[:, bass.ds(m * P, P)]).then_inc(xr_in[t % 4], 16)
                    v = t - PART2_LAG
                    if not (first and v < 0):
                        sp.wait_ge(y_done, m - PART2_LAG + 1)
                        tile = m - PART2_LAG
                        sp.dma_start(out_rows[:, bass.ds(tile, 1), :], yo[:, v % 2:v % 2 + 1, :]).then_inc(stored[v % 2], 16)

            tiles2(0, True, False)
            with sp.Fori(1, B - 1) as it:
                tiles2(it, False, False)
            tiles2(B - 1, False, True)
            for r in range(2):
                sp.wait_ge(stored[r], 16 * B * NT // 2)

        @block.gpsimd
        def _(pool):
            pool.memset(ident[:, :], 0.0).then_inc(ident_ok, 1)
            pool.wait_ge(ident_ok, 1)
            pool.affine_select(out=ident[:, :], in_=ident[:, :], compare_op=ALU.not_equal, fill=1.0, base=0,
                               pattern=[[-1, P]], channel_multiplier=1).then_inc(ident_ok, 1)

            pool.memset(rms_const[:, 0:1], 0.5).then_inc(rms_const_ok, 1)
            pool.memset(rms_const[:, 1:2], RMS_EPS).then_inc(rms_const_ok, 1)
            pool.wait_ge(rms_const_ok, 2)
            pool.memset(ones[:, :], 1.0).then_inc(iota_ok, 1)
            for e in range(E):
                pool.memset(iota[:, e:e + 1], float(e)).then_inc(iota_ok, 1)
            pool.memset(causal[:, :], 0.0).then_inc(mask_ok, 1)
            pool.wait_ge(mask_ok, 1)
            pool.affine_select(out=causal[:, :], in_=causal[:, :], compare_op=ALU.is_ge, fill=MASKED, base=0,
                               pattern=[[-1, P]], channel_multiplier=1).then_inc(mask_ok, 1)
            for i in (identb, identh):
                pool.memset(i[:, :], 0.0).then_inc(mask_ok, 1)
            pool.wait_ge(mask_ok, 4)
            for i in (identb, identh):
                pool.affine_select(out=i[:, :], in_=i[:, :], compare_op=ALU.not_equal, fill=1.0, base=0,
                                   pattern=[[-1, P]], channel_multiplier=1).then_inc(mask_ok, 1)

            def mix(n, u):
                pool.wait_ge(c_ok, n + 1)
                pool.tensor_tensor(prob2[:, u % 2, SCALE_V:T], prob2[:, u % 2, SCALE_V:T],
                                   ccol[:, u % 2:u % 2 + 1].to_broadcast([P, T - SCALE_V]), ALU.mult).then_inc(scaled_P, 1)
                pool.wait_ge(scaled_P, n + 1)
                pool.wait_ge(scaled_V, n + 1)
                pool.tensor_tensor(prob1[:, u, :], prob1[:, u, :], prob2[:, u % 2, :], ALU.add).then_inc(mix_ok, 1)

            def rms(h):
                pool.wait_ge(stat_ok, 2 * (h + 1))
                pool.tensor_tensor(tl[:, 2, :], tl[:, 1, :], tl[:, 1, :], ALU.mult).then_inc(rms_v, 1)
                pool.wait_ge(rms_v, 4 * h + 1)
                pool.tensor_tensor(tl[:, 3, :], tl[:, 2, :], tl[:, 0, :], ALU.mult).then_inc(rms_v, 1)
                pool.wait_ge(rms_v, 4 * h + 2)
                pool.tensor_tensor(tl[:, 4, :], tl[:, 3, :], rms_const[:, 0:1].to_broadcast([P, 8]), ALU.pow).then_inc(rms_v, 1)
                pool.wait_ge(rms_v, 4 * h + 3)
                pool.tensor_tensor(tl[:, 5, :], tl[:, 4, :], rms_const[:, 1:2].to_broadcast([P, 8]), ALU.add).then_inc(rms_v, 1)

            def units(h, tail):
                for u in range(8):
                    mix(8 * h + u, u % 4)
                    if tail and u == RMS_AFTER:
                        rms(h - 2)

            with pool.Fori(0, 2) as h:
                units(h, False)
            with pool.Fori(2, 2 * STEPS) as h:
                units(h, True)
            rms(2 * STEPS - 2)
            rms(2 * STEPS - 1)

        @block.tensor
        def _(pe):
            pe.wait_ge(ident_ok, 2)

            def ln_transposes(b):
                pe.wait_ge(ln_v, LNV * (b + 1))
                if b > 0:
                    pe.wait_ge(ln_evA, b)
                    pe.wait_ge(ln_evV, b)
                for t in range(NT):
                    mm = pe.transpose(score_ps[:, 0, t * P:(t + 1) * P], xn[:, t * P:(t + 1) * P], ident[:, :])
                    if t % 4 == 3:
                        mm.then_inc(ln_T, 1)
            for b in range(B):
                ln_transposes(b)

            def proj_fill(part, j, par, pair):
                if part == "q0":
                    pe.wait_ge(step_in[par], 64 * (pair + 1))
                half = int(part[1])
                if part[0] != "v":
                    mm = pe.matmul(misc_ps[:, :], wg[:, par, "qk".index(part[0]), :],
                                   xg[:, par, half * HALF:(half + 1) * HALF], start=True, stop=True)
                else:
                    for t in range(4):
                        tile = half * 4 + t
                        mm = pe.matmul(misc_ps[:, t * P:(t + 1) * P], xg[:, par, tile * P:(tile + 1) * P],
                                       wg[:, par, 2, :], start=True, stop=True)
                mm.then_inc(filled[part], 1)

            before = None
            for part, j in AHEAD:
                if before:
                    read(pe, *before)
                proj_fill(part, j, j, 0)
                before = (part, j)

            def scores(n, s, sub, peeled):
                j, par, half, head, qt, _ = unit_of(s)
                if not (peeled and n < 1):
                    pe.wait_ge(exp_ok, 2 * n - 1 + sub)
                q0 = (half * 4 + qt) * P
                for kh in range(2):
                    mm = pe.matmul(score_ps[:, sub, kh * HALF:(kh + 1) * HALF],
                                   qa[:, par, head * 2 + sub, q0:q0 + P],
                                   ka[:, par, head * 2 + sub, kh * HALF:(kh + 1) * HALF], start=True, stop=True)
                mm.then_inc(score_ok, 1)

            def slots(it, first, last):
                end = SLOTS - 8 + TAIL_SLOTS if last else SLOTS
                if first:
                    pe.wait_ge(stacked["q"], 256)
                    pe.wait_ge(stacked["k"], 256)
                    scores(0, 0, 0, True)
                for s in range(end):
                    n = SLOTS * it + s
                    if s < SLOTS:
                        scores(n, s, 1, first and s == 0)
                    u = s - TRANS_LAG
                    if not (first and u < 0) and not (last and u >= SLOTS):
                        pe.wait_ge(mix_ok, n - TRANS_LAG + 1)
                        for kb in range(2):
                            if not (first and u == 0):
                                pe.wait_ge(probT_ok[kb], n - TRANS_LAG)
                            for t in range(4):
                                k0 = (kb * 4 + t) * P
                                mm = pe.transpose(trans_ps[:, kb, t * P:(t + 1) * P], prob1[:, u % 4, k0:k0 + P], ident[:, :])
                            mm.then_inc(trans_ok, 1)
                    half, kt = divmod(s - PV_LAG, 8)

                    def values(head):
                        return pe.matmul(attn_ps[head * DV:(head + 1) * DV, :],
                                         v_sb[:, (half // 2) % 2, kt, head * DV:(head + 1) * DV],
                                         probT[:, half % 2, kt, head, :], start=kt == 0, stop=kt == 7)

                    if present(half, first, last):
                        if kt == 0:
                            pe.wait_ge(probT_ok[0], 8 * (4 * it + half + 1))
                            pe.wait_ge(probT_ok[1], 8 * (4 * it + half + 1))
                            if not (first and half == 0):
                                pe.wait_ge(attnT_ok, 4 * it + half)
                        if half % 2 == 0 and kt in (0, 4):
                            pe.wait_ge(v_ok, 2 * (2 * it + half // 2) + kt // 4 + 1)
                        values(0)
                    if s + 1 < SLOTS or not last:
                        if (s + 1) % UNITS == 0:
                            j = 2 * it + (s + 1) // UNITS
                            pe.wait_ge(stacked["q"], 256 * (j + 1))
                            pe.wait_ge(stacked["k"], 256 * (j + 1))
                        scores(n + 1, s + 1, 0, False)
                    if present(half, first, last):
                        values(1).then_inc(pv_ok, 1)
                    fill = misc_fill(s, first, last)
                    if fill:
                        misc_free(pe, s, it, first, last)
                        kind, which = fill
                        if kind in PARTS:
                            proj_fill(kind, 2 * it + which, which % 2, it + which // 2)
                        elif kind == "rows":
                            pe.wait_ge(attnT_ok, 4 * it + which + 1)
                            for t in range(4):
                                mm = pe.transpose(misc_ps[:, t * P:(t + 1) * P], attnT[:, t * P:(t + 1) * P], ident[:, :])
                            mm.then_inc(rows_ok, 1)
                        elif kind == "cols":
                            pe.wait_ge(norm_v, 3 * (4 * it + which + 1))
                            for t in range(4):
                                mm = pe.transpose(misc_ps[:, t * P:(t + 1) * P],
                                                  attn_n[:, t, :, :].rearrange("p h d -> p (h d)"), ident[:, :])
                            mm.then_inc(cols_ok, 1)
                        else:
                            pe.wait_ge(attn_nT_ok, 4 * it + which + 1)
                            if which == 0 and first:
                                pe.wait_ge(wo_ok, 1)
                            step = 2 * it + which // 2
                            wo_g = wo_sb[:, bass.ds(step % G, 1), :].rearrange("p a c -> p (a c)")
                            for t in range(4):
                                mm = pe.matmul(misc_ps[:, t * P:(t + 1) * P], attn_nT[:, t, :], wo_g,
                                               start=True, stop=True)
                            mm.then_inc(out_ok, 1)

            slots(0, True, False)
            with pe.Fori(1, ITERS - 1) as it:
                slots(it, False, False)
            slots(ITERS - 1, False, True)

            pe.wait_ge(resid_ok, 2 * STEPS)
            pe.wait_ge(c2_v, 1)
            pe.wait_ge(iota_ok, 1)
            pe.wait_ge(mask_ok, 6)
            pe.matmul(exp_ps[:, 0, 0:E], ones[:, :], small[:, 0, :], start=True, stop=True).then_inc(c2_p, 1)
            for b in range(B):
                pe.wait_ge(g_v, GV * b + 10)
                for t in range(NT):
                    mm = pe.transpose(t2_ps[:, t // 4, t % 4 * P:(t % 4 + 1) * P], x2n[:, t * P:(t + 1) * P], ident[:, :])
                    if t % 4 == 3:
                        mm.then_inc(g_T, 1)
                pe.wait_ge(g_evA, b + 1)
                pe.wait_ge(g_evV, b + 1)
                pe.wait_ge(c2_v, C2V)
                for t in range(NT):
                    mm = pe.matmul(exp_ps[:, 0, t * E:(t + 1) * E], x2T[:, t * P:(t + 1) * P], simn[:, :],
                                   start=True, stop=True)
                mm.then_inc(g_lg, 1)
            pe.wait_ge(experts_in, 16 * 5)
            pe.wait_ge(g_v, GV * B)

            def tiles2(it, first, last):
                for t in range(NT + PART2_LAG if last else NT):
                    m = NT * it + t

                    def live(lag):
                        return not (first and t < lag) and not (last and t - lag >= NT)

                    def experts(c):
                        if not live(0):
                            return
                        if c == 0:
                            pe.wait_ge(xr_in[t % 4], 16 * (2 * it + t // 4 + 1))
                        if not (first and t == 0 and c < 2):
                            pe.wait_ge(e_v, 8 * m + c - 1)
                        pe.matmul(exp_ps[:, c % 2, 0:6 * DE], xr[:, t % 4, :],
                                  ew[:, 2 * c:2 * c + 2, :].rearrange("p e d -> p (e d)"),
                                  start=True, stop=True).then_inc(e_ps, 1)

                    experts(0)
                    if live(1):
                        v = (t - 1) % NT
                        pe.wait_ge(hi2, 2 * m)
                        pe.wait_ge(lo2, 2 * m)
                        if not (first and t == 1):
                            pe.wait_ge(qkt_ok, m - 1)
                        for n in range(3):
                            mm = pe.transpose(qk_ps[:, n * P:(n + 1) * P], qs[:, v % 2, n, :], identh[:, :])
                        mm.then_inc(qkt_ps, 1)
                    experts(1)
                    if live(2):
                        v = (t - 2) % NT
                        pe.wait_ge(exp2, m - 1)
                        if not (first and t < 4):
                            pe.wait_ge(mt_A, m - 3)
                            pe.wait_ge(mt_V, m - 3)
                        elif t == 3:
                            pe.wait_ge(t2_A, m - 2)
                            pe.wait_ge(t2_V, m - 2)
                        for kb in range(v + 1):
                            mm = pe.transpose(t2_ps[:, kb // 4, kb % 4 * P:(kb % 4 + 1) * P],
                                              p2[:, v % 2, kb * P:(kb + 1) * P], ident[:, :])
                        mm.then_inc(t2_ok, 1)
                    experts(2)
                    if live(3):
                        v = (t - 3) % NT
                        pe.wait_ge(mx_ok, m - 2)
                        if live(2):
                            pe.wait_ge(t2_A, m - 1)
                            pe.wait_ge(t2_V, m - 1)
                        elif last:
                            pe.wait_ge(mt_A, m - 3)
                            pe.wait_ge(mt_V, m - 3)
                        for g in range(8):
                            mm = pe.transpose(t2_ps[:, g // 4, g % 4 * P:(g % 4 + 1) * P],
                                              mx[:, v % 2, 2 * g:2 * g + 2, :].rearrange("p e d -> p (e d)"), ident[:, :])
                            if g % 4 == 3:
                                mm.then_inc(mt_ok, 1)
                    experts(3)
                    if live(1):
                        v = (t - 1) % NT
                        pe.wait_ge(qkt_ok, m)
                        if not (first and t == 1):
                            pe.wait_ge(exp2, m - 1)
                        keys = (v + 1) * P
                        for k0 in range(0, keys, 512):
                            k1 = min(k0 + 512, keys)
                            diag = k1 == keys
                            pe.matmul(s2_ps[:, k0:k1], qkT[:, 0, v * P:(v + 1) * P], qkT[:, 1, k0:k1], start=True, stop=False)
                            mm = pe.matmul(s2_ps[:, k0:k1], qkT[:, 0, v * P:(v + 1) * P], qkT[:, 2, k0:k1], start=False, stop=not diag)
                            if diag:
                                mm = pe.matmul(s2_ps[:, k1 - P:k1], identb[:, :], causal[:, :], start=False, stop=True)
                        mm.then_inc(s2_ok, 1)
                    experts(4)
                    if live(2):
                        v = (t - 2) % NT
                        pe.wait_ge(t2_A, m - 1)
                        pe.wait_ge(t2_V, m - 1)
                        pe.wait_ge(kv_ok, m - 1)
                        if not (first and t < 4):
                            pe.wait_ge(y_done, m - 3)
                        elif not (first and t == 2):
                            pe.wait_ge(mx_ok, m - 2)
                        for kb in range(v + 1):
                            mm = pe.matmul(o2_ps[:, 0:2 * DE], p2T[:, kb, :], kv2[:, kb, :], start=kb == 0, stop=kb == v)
                        mm.then_inc(pv2, 1)
                    experts(5)
                    if live(3):
                        pe.wait_ge(mt_A, m - 2)
                        pe.wait_ge(mt_V, m - 2)
                        if live(2):
                            pe.wait_ge(mx_ok, m - 1)
                        for g in range(8):
                            mm = pe.matmul(o2_ps[:, 0:C], mxT[:, g, :], eow[:, g, :], start=g == 0, stop=g == 7)
                        mm.then_inc(o_ok, 1)
                    experts(6)
                    experts(7)

            tiles2(0, True, False)
            with pe.Fori(1, B - 1) as it:
                tiles2(it, False, False)
            tiles2(B - 1, False, True)

        @block.scalar
        def _(act):
            act.preload_act_table_set("natural_log_exp_and_others")

            def act_copy(dst, src):
                return act.activation(dst, src, ACT.Copy)

            act.wait_ge(lam_chain, 3)
            act.activation(lam[:, 2:4], lam[:, 0:2], ACT.Exp).then_inc(lam_exp, 1)
            for b in range(B):
                act.wait_ge(ln_v, LNV * b + 3)
                act.activation(xsq, xc, ACT.Square).then_inc(ln_sq, 1)
                act.wait_ge(ln_v, LNV * b + 5)
                act.activation(stat[:, 3, :], stat[:, 2, :], ACT.Ln).then_inc(ln_y, 1)
                act.wait_ge(ln_y, 2 * b + 1)
                act.activation(stat[:, 4, :], stat[:, 3, :], ACT.Exp, scale=-0.5).then_inc(ln_y, 1)
                act.wait_ge(ln_T, 2 * b + 1)
                act.activation(xnT[:, b * T:b * T + HALF], score_ps[:, 0, 0:HALF], ACT.Copy).then_inc(ln_evA, 1)

            def proj_copy(part, j, par, wait_old):
                act.wait_ge(filled[part], j + 1)
                kind, half = part[0], int(part[1])
                if kind != "v":
                    if half == 0 and wait_old:
                        act.wait_ge(stacked[kind], 256 * j)
                    act.activation(split[:, 2 * "qk".index(kind), half * HALF:(half + 1) * HALF], misc_ps[:, :],
                                   ACT.Copy, scale=QSCALE if kind == "q" else 1.0).then_inc(high_ok[kind], 1)
                else:
                    act.activation(v_sb[:, par, half * 4:(half + 1) * 4, :],
                                   misc_ps[:, :].rearrange("p (t d) -> p t d", t=4), ACT.Copy).then_inc(v_ok, 1)

            for part, j in AHEAD:
                proj_copy(part, j, j, j > 0)

            def slots(it, first, last):
                end = SLOTS - 8 + TAIL_SLOTS if last else SLOTS
                for s in range(end):
                    n = SLOTS * it + s

                    def softmax(sub):
                        act.wait_ge(max_ok, 2 * n + sub + 1)
                        if sub == 0 and not (first and s < 4):
                            act.wait_ge(trans_ok, 2 * (n - 3))
                        if sub == 1 and not (first and s < 2):
                            act.wait_ge(mix_ok, n - 1)
                        act.activation(prob2[:, s % 2, :] if sub else prob1[:, s % 4, :], score_ps[:, sub, :], ACT.Exp,
                                       bias=negmax[:, s % 2, sub:sub + 1],
                                       accum_out=sums[:, s // 8, sub, s % 8:s % 8 + 1]).then_inc(exp_ok, 1)

                    if s < SLOTS:
                        softmax(0)
                    copy_probT(act, act_copy, it, s, n, 0, first, last)
                    if s < SLOTS:
                        softmax(1)
                    if not copied_by_dve(s):
                        copy_probT(act, act_copy, it, s, n, 1, first, last)
                    half = half_at(s, COPY_LAG, first, last)
                    if half is not None:
                        act.wait_ge(pv_ok, 8 * (4 * it + half + 1))
                        if not (first and half == 0):
                            act.wait_ge(rows_ok, 4 * it + half)
                        act.activation(attnT[:, :], attn_ps[:, :], ACT.Copy).then_inc(attnT_ok, 1)
                    fill = misc_fill(s, first, last)
                    if fill and fill[0] in PARTS:
                        part, step = fill
                        proj_copy(part, 2 * it + step, step % 2, True)
                    elif fill and fill[0] == "rows":
                        act.wait_ge(rows_ok, 4 * it + fill[1] + 1)
                        act.activation(attn[:, :, :, :].rearrange("p t h d -> p (t h d)"), misc_ps[:, :],
                                       ACT.Copy).then_inc(attn_copied, 1)
                        act.activation(attn_sq[:, :, :, :].rearrange("p t h d -> p (t h d)"), misc_ps[:, :],
                                       ACT.Square, scale=DV ** -0.5).then_inc(attn_copied, 1)
                    elif fill and fill[0] == "cols":
                        act.wait_ge(cols_ok, 4 * it + fill[1] + 1)
                        act.activation(attn_nT[:, :, :].rearrange("p t q -> p (t q)"), misc_ps[:, :],
                                       ACT.Copy).then_inc(attn_nT_ok, 1)

            slots(0, True, False)
            with act.Fori(1, ITERS - 1) as it:
                slots(it, False, False)
            slots(ITERS - 1, False, True)

            def rsqrt_seed(y, l, v, ready, n, done_sem, k):
                act.wait_ge(ready, n)
                act.activation(l, v, ACT.Ln).then_inc(done_sem, 1)
                act.wait_ge(done_sem, k + 1)
                act.activation(y, l, ACT.Exp, scale=-0.5).then_inc(done_sem, 1)

            act.wait_ge(resid_ok, 2 * STEPS)
            act.activation(small[:, 6, :], sgate[:, :], ACT.Exp, scale=-1.0).then_inc(c2_a, 1)
            rsqrt_seed(small[:, 3, :], small[:, 2, :], small[:, 1, :], c2_v, 2, c2_a, 1)
            for b in range(B):
                act.wait_ge(g_v, GV * b + 3)
                act.activation(x2sq[:, :], x2c[:, :], ACT.Square).then_inc(g_sq, 1)
                rsqrt_seed(gs[:, 4, :], gs[:, 3, :], gs[:, 2, :], g_v, GV * b + 5, g_y, 4 * b)
                act.wait_ge(g_v, GV * b + 10)
                act.activation(x2sq[:, :], x2n[:, :], ACT.Square).then_inc(g_sq, 1)
                act.wait_ge(g_T, 2 * b + 1)
                if b > 0:
                    act.wait_ge(g_lg, b)
                    act.wait_ge(g_copied, 16 * b)
                act.activation(x2T[:, 0:HALF], t2_ps[:, 0, :], ACT.Copy).then_inc(g_evA, 1)
                rsqrt_seed(gs[:, 4, :], gs[:, 3, :], gs[:, 2, :], g_v, GV * b + 12, g_y, 4 * b + 2)
                act.wait_ge(g_v, GV * b + GEXP)
                act.activation(gl[:, 8, :, :], gl[:, 7, :, :], ACT.Exp).then_inc(g_exp, 1)

            def tiles2(it, first, last):
                for t in range(NT + PART2_LAG if last else NT):
                    m = NT * it + t

                    def live(lag):
                        return not (first and t < lag) and not (last and t - lag >= NT)

                    if live(1):
                        v = (t - 1) % NT
                        act.wait_ge(qkt_ps, m)
                        if not (first and t == 1):
                            act.wait_ge(s2_ok, m - 1)
                        act.activation(qkT[:, :, v * P:(v + 1) * P], qk_ps[:, 0:3 * P].rearrange("p (n q) -> p n q", n=3),
                                       ACT.Copy).then_inc(qkt_ok, 1)
                    if live(2):
                        v = (t - 2) % NT
                        act.wait_ge(t2_ok, m - 1)
                        if not (first and t == 2):
                            act.wait_ge(pv2, m - 2)
                        blocks = min(v + 1, 4)
                        act.activation(p2T[:, 0:blocks, :], t2_ps[:, 0, 0:blocks * P].rearrange("p (k q) -> p k q", k=blocks),
                                       ACT.Copy).then_inc(t2_A, 1)
                    if live(3):
                        act.wait_ge(mt_ok, 2 * (m - 2) - 1)
                        if not (first and t == 3):
                            act.wait_ge(o_ok, m - 3)
                        act.activation(mxT[:, 0:4, :], t2_ps[:, 0, :].rearrange("p (g q) -> p g q", g=4), ACT.Copy).then_inc(mt_A, 1)
                    if live(1):
                        v = (t - 1) % NT
                        keys = (v + 1) * P
                        act.wait_ge(max2, m)
                        if not (first and t < 3):
                            act.wait_ge(t2_ok, m - 2)
                        act.activation(p2[:, v % 2, 0:keys], s2_ps[:, 0:keys], ACT.Exp, bias=nm2[:, v % 2:v % 2 + 1],
                                       accum_out=sum2[:, v % 2:v % 2 + 1]).then_inc(exp2, 1)
                        if not (first and t < 2):
                            act.wait_ge(pv2, m - 1)
                        act.activation(kv2[:, v, :], acc[:, v % 2, DE:3 * DE], ACT.Copy).then_inc(kv_ok, 1)
                    if live(0):
                        act.wait_ge(e_v, 8 * m + 8)
                        if not (first and t < 2):
                            act.wait_ge(qkt_ps, m - 1)
                        act.activation(qs[:, t % 2, 0, 0:DE], acc[:, t % 2, 0:DE], ACT.Copy, scale=DE ** -0.5).then_inc(hi2, 1)
                        act.activation(qs[:, t % 2, 1, :].rearrange("p (n d) -> p n d", n=2),
                                       acc[:, t % 2, DE:2 * DE].unsqueeze(1).to_broadcast([P, 2, DE]), ACT.Copy).then_inc(hi2, 1)

            tiles2(0, True, False)
            with act.Fori(1, B - 1) as it:
                tiles2(it, False, False)
            tiles2(B - 1, False, True)

        @block.vector
        def _(dve):
            dve.wait_ge(const_in, 7 * 16)
            for n in range(2):
                dve.tensor_tensor(lam_pr[:, n, :], lam_in[:, 2 * n, :], lam_in[:, 2 * n + 1, :], ALU.mult).then_inc(lam_chain, 1)
            dve.wait_ge(lam_chain, 2)
            dve.tensor_reduce(lam[:, 0:2], lam_pr[:, :, :], AX.X, ALU.add).then_inc(lam_chain, 1)
            dve.tensor_scalar(wo_sb[:, :, :], wo_sb[:, :, :], gcol[:, :], 1.0 - LAMBDA_INIT, ALU.mult, ALU.mult).then_inc(wo_ok, 1)
            dve.wait_ge(lam_exp, 1)
            dve.tensor_tensor(lam[:, 4:5], lam[:, 3:4], lam[:, 2:3], ALU.subtract).then_inc(lam_chain, 1)
            dve.wait_ge(lam_chain, 4)
            dve.tensor_scalar(lam[:, 5:6], lam[:, 4:5], LAMBDA_INIT, None, ALU.subtract).then_inc(lam_ok, 1)
            dve.wait_ge(lam_ok, 1)

            def newton(y, v, t, u, sm, base):
                dve.tensor_tensor(t, v, y, ALU.mult).then_inc(sm, 1)
                dve.wait_ge(sm, base + 1)
                dve.tensor_tensor(u, t, y, ALU.mult).then_inc(sm, 1)
                dve.wait_ge(sm, base + 2)
                dve.tensor_scalar(u, u, -0.5, 1.5, ALU.mult, ALU.add).then_inc(sm, 1)
                dve.wait_ge(sm, base + 3)

            def tiles(ap):
                return ap.rearrange("p (t c) -> p t c", t=NT)

            for b in range(B):
                k = LNV * b
                dve.wait_ge(x_in, 16 * B)
                xb = resid[:, b * NT:(b + 1) * NT, :]
                dve.tensor_reduce(stat[:, 0, :], xb, AX.X, ALU.add).then_inc(ln_v, 1)
                dve.wait_ge(ln_v, k + 1)
                dve.tensor_scalar(stat[:, 1, :], stat[:, 0, :], -1.0 / C, None, ALU.mult).then_inc(ln_v, 1)
                dve.wait_ge(ln_v, k + 2)
                dve.tensor_tensor(tiles(xc), xb, stat[:, 1, :].unsqueeze(2).to_broadcast([P, NT, C]), ALU.add).then_inc(ln_v, 1)
                dve.wait_ge(ln_sq, b + 1)
                dve.tensor_reduce(stat[:, 0, :], tiles(xsq), AX.X, ALU.add).then_inc(ln_v, 1)
                dve.wait_ge(ln_v, k + 4)
                dve.tensor_scalar(stat[:, 2, :], stat[:, 0, :], 1.0 / C, LN_EPS, ALU.mult, ALU.add).then_inc(ln_v, 1)
                dve.wait_ge(ln_y, 2 * b + 2)
                newton(stat[:, 4, :], stat[:, 2, :], stat[:, 5, :], stat[:, 6, :], ln_v, k + 5)
                dve.tensor_tensor(stat[:, 7, :], stat[:, 4, :], stat[:, 6, :], ALU.mult).then_inc(ln_v, 1)
                dve.wait_ge(ln_v, k + 9)
                if b > 0:
                    dve.wait_ge(ln_T, 2 * b)
                dve.tensor_tensor(tiles(xn), tiles(xc), stat[:, 7, :].unsqueeze(2).to_broadcast([P, NT, C]), ALU.mult).then_inc(ln_v, 1)
                dve.wait_ge(ln_T, 2 * b + 2)
                dve.tensor_copy(xnT[:, b * T + HALF:(b + 1) * T], score_ps[:, 0, HALF:T]).then_inc(ln_evV, 1)

            def proj_low(part, j):
                kind, half = part[0], int(part[1])
                dve.wait_ge(high_ok[kind], 2 * j + half + 1)
                cols = slice(half * HALF, (half + 1) * HALF)
                row = 2 * "qk".index(kind)
                dve.scalar_tensor_tensor(out=split[:, row + 1, cols], in0=misc_ps[:, :],
                                         scalar=QSCALE if kind == "q" else 1.0, in1=split[:, row, cols],
                                         op0=ALU.mult, op1=ALU.subtract).then_inc(low_ok[kind], 1)

            for part, j in AHEAD:
                if part[0] != "v":
                    proj_low(part, j)

            def slots(it, first, last):
                end = SLOTS - 8 + TAIL_SLOTS if last else SLOTS
                for s in range(end):
                    n = SLOTS * it + s

                    def row_max(n, s, sub):
                        dve.wait_ge(score_ok, 2 * n + sub + 1)
                        dve.tensor_reduce(negmax[:, s % 2, sub:sub + 1], score_ps[:, sub, :], AX.X, ALU.max,
                                          negate=True).then_inc(max_ok, 1)

                    if first and s == 0:
                        row_max(0, 0, 0)
                    r = (s - 1) % 2
                    last_unit = not (first and s < 1) and not (last and s > SLOTS)
                    if last_unit:
                        half, u = ((s - 1) // 8) % 4, (s - 1) % 8
                        dve.wait_ge(exp_ok, 2 * n)
                        dve.reciprocal(recip2[:, r:r + 1], sums[:, half, 1, u:u + 1]).then_inc(rec_ok, 1)
                        dve.wait_ge(rec_ok, n)
                        dve.scalar_tensor_tensor(out=ccol[:, r:r + 1], in0=recip2[:, r:r + 1], scalar=lam[:, 5:6],
                                                 in1=sums[:, half, 0, u:u + 1], op0=ALU.mult,
                                                 op1=ALU.mult).then_inc(c_ok, 1)
                    norm = half_at(s, NORM_LAG, first, last)
                    if norm is not None:
                        k = 3 * (4 * it + norm)
                        dve.wait_ge(rms_v, 4 * (4 * it + norm + 1))
                        dve.reciprocal(tl[:, 6, :], tl[:, 5, :]).then_inc(norm_v, 1)
                    if s < SLOTS:
                        row_max(n, s, 1)
                    if norm is not None:
                        dve.wait_ge(norm_v, k + 1)
                        dve.tensor_tensor(tl[:, 7, :], tl[:, 6, :], tl[:, 1, :], ALU.mult).then_inc(norm_v, 1)
                    fill = None if first and s < 1 else misc_fill(s - 1, first, last)
                    if fill and fill[0] in PARTS and fill[0][0] != "v":
                        proj_low(fill[0], 2 * it + fill[1])
                    half = half_at(s, PROJECT_LAG + 1, first, last)
                    if half is not None:
                        step = 2 * it + half // 2
                        tile0 = (step // G) * NT + (half % 2) * 4
                        dve.wait_ge(out_ok, 4 * it + half + 1)
                        rows = resid[:, bass.ds(tile0, 4), :]
                        dve.tensor_tensor(rows, rows, misc_ps[:, :].rearrange("p (t c) -> p t c", t=4),
                                          ALU.add).then_inc(resid_ok, 1)
                    if last_unit:
                        dve.wait_ge(c_ok, n)
                        dve.tensor_scalar(prob2[:, r, 0:SCALE_V], prob2[:, r, 0:SCALE_V], ccol[:, r:r + 1], None,
                                          ALU.mult).then_inc(scaled_V, 1)
                    if s + 1 < SLOTS or not last:
                        row_max(n + 1, s + 1, 0)
                    if copied_by_dve(s):
                        copy_probT(dve, dve.tensor_copy, it, s, n, 1, first, last)
                    half = half_at(s, STAT_LAG, first, last)
                    if half is not None:
                        if not (first and half == 0):
                            dve.wait_ge(norm_v, 3 * (4 * it + half))
                        dve.reciprocal(tl[:, 1, :], sums[:, half % 4, 0, :]).then_inc(stat_ok, 1)
                        dve.wait_ge(attn_copied, 2 * (4 * it + half + 1))
                        dve.tensor_reduce(tl[:, 0, :].rearrange("p (h t) -> p h t", h=2),
                                          attn_sq[:, :, :, :].rearrange("p t h d -> p h t d"), AX.X, ALU.add).then_inc(stat_ok, 1)
                    if norm is not None:
                        dve.wait_ge(norm_v, k + 2)
                        dve.tensor_tensor(attn_n[:, :, :, :], attn[:, :, :, :],
                                          tl[:, 7, :].rearrange("p (h t) -> p t h", h=2).unsqueeze(3).to_broadcast([P, 4, 2, DV]),
                                          ALU.mult).then_inc(norm_v, 1)

            slots(0, True, False)
            with dve.Fori(1, ITERS - 1) as it:
                slots(it, False, False)
            slots(ITERS - 1, False, True)

            links = {}

            def link(ins, sm):
                links[sm.name] = links.get(sm.name, 0) + 1
                ins.then_inc(sm, 1)
                dve.wait_ge(sm, links[sm.name])

            dve.wait_ge(const2_in, 16 * 2)
            dve.wait_ge(iota_ok, 1 + E)
            dve.wait_ge(resid_ok, 2 * STEPS)
            link(dve.tensor_tensor(small[:, 0, :], simn[:, :], simn[:, :], ALU.mult), c2_v)
            dve.wait_ge(c2_p, 1)
            link(dve.tensor_scalar(small[:, 1, :], exp_ps[:, 0, 0:E], RSQ_SHIFT, RSQ_LEAST, ALU.mult, ALU.max), c2_v)
            dve.wait_ge(c2_a, 3)
            link(dve.tensor_scalar(small[:, 6, :], small[:, 6, :], 1.0, None, ALU.add), c2_v)
            link(dve.reciprocal(sgate[:, :], small[:, 6, :]), c2_v)

            def polished(y, v, t, u, sm):
                link(dve.tensor_tensor(t, v, y, ALU.mult), sm)
                link(dve.tensor_tensor(t, t, y, ALU.mult), sm)
                link(dve.tensor_scalar(t, t, -0.5, 1.5, ALU.mult, ALU.add), sm)
                link(dve.tensor_tensor(u, t, y, ALU.mult), sm)

            polished(small[:, 3, :], small[:, 1, :], small[:, 4, :], small[:, 5, :], c2_v)
            link(dve.tensor_scalar(small[:, 5, :], small[:, 5, :], RSQ_SHIFT ** 0.5, 1.0 / GATE_LEAST, ALU.mult, ALU.min), c2_v)
            link(dve.tensor_tensor(simn[:, :], simn[:, :], small[:, 5, :], ALU.mult), c2_v)
            assert links[c2_v.name] == C2V

            def per_token(ap):
                return ap.unsqueeze(2).to_broadcast([P, NT, E])

            def per_expert(ap):
                return ap.unsqueeze(1).to_broadcast([P, NT, E])

            for b in range(B):
                xb = resid[:, b * NT:(b + 1) * NT, :]
                link(dve.tensor_reduce(gs[:, 0, :], xb, AX.X, ALU.add), g_v)
                link(dve.tensor_scalar(gs[:, 1, :], gs[:, 0, :], -1.0 / C, None, ALU.mult), g_v)
                link(dve.tensor_tensor(tiles(x2c[:, :]), xb, gs[:, 1, :].unsqueeze(2).to_broadcast([P, NT, C]), ALU.add), g_v)
                dve.wait_ge(g_sq, 2 * b + 1)
                link(dve.tensor_reduce(gs[:, 0, :], tiles(x2sq[:, :]), AX.X, ALU.add), g_v)
                link(dve.tensor_scalar(gs[:, 2, :], gs[:, 0, :], 1.0 / C, LN_EPS, ALU.mult, ALU.add), g_v)
                dve.wait_ge(g_y, 4 * b + 2)
                polished(gs[:, 4, :], gs[:, 2, :], gs[:, 5, :], gs[:, 6, :], g_v)
                link(dve.tensor_tensor(tiles(x2n[:, :]), tiles(x2c[:, :]), gs[:, 6, :].unsqueeze(2).to_broadcast([P, NT, C]), ALU.mult), g_v)
                dve.wait_ge(g_sq, 2 * b + 2)
                link(dve.tensor_reduce(gs[:, 0, :], tiles(x2sq[:, :]), AX.X, ALU.add), g_v)
                link(dve.tensor_scalar(gs[:, 2, :], gs[:, 0, :], RSQ_SHIFT, RSQ_LEAST, ALU.mult, ALU.max), g_v)
                dve.wait_ge(g_T, 2 * b + 2)
                if b > 0:
                    dve.wait_ge(g_copied, 16 * b)
                dve.tensor_copy(x2T[:, HALF:T], t2_ps[:, 1, :]).then_inc(g_evV, 1)
                dve.wait_ge(g_y, 4 * b + 4)
                polished(gs[:, 4, :], gs[:, 2, :], gs[:, 5, :], gs[:, 6, :], g_v)
                link(dve.tensor_scalar(gs[:, 6, :], gs[:, 6, :], RSQ_SHIFT ** 0.5, 1.0 / GATE_LEAST, ALU.mult, ALU.min), g_v)
                dve.wait_ge(g_lg, b + 1)
                lg = gl[:, 0, :, :]
                link(dve.tensor_tensor(gl[:, 1, :, :], exp_ps[:, 0, 0:NT * E].rearrange("p (t e) -> p t e", t=NT),
                                       per_token(gs[:, 6, :]), ALU.mult), g_v)
                link(dve.tensor_tensor(lg, gl[:, 1, :, :], per_expert(sgate[:, :]), ALU.subtract), g_v)
                for t in range(NT):
                    link(dve.max(out=top8[:, t, :], in_=lg[:, t, :]), g_v)
                for t in range(NT):
                    link(dve.max_index(out=top8i[:, t, :], in_max=top8[:, t, :], in_values=lg[:, t, :]), g_v)
                link(dve.tensor_copy(top2f[:, :, :], top8i[:, :, 0:2]), g_v)
                for n in range(2):
                    link(dve.tensor_tensor(gl[:, 2 + n, :, :], per_expert(iota[:, :]),
                                           top2f[:, :, n:n + 1].to_broadcast([P, NT, E]), ALU.is_equal), g_v)
                link(dve.tensor_tensor(gl[:, 2, :, :], gl[:, 2, :, :], gl[:, 3, :, :], ALU.add), g_v)
                best = top8[:, :, 0:1].rearrange("p t a -> p (t a)")
                link(dve.tensor_scalar(gs[:, 0, :], best, 0.0, None, ALU.is_le), g_v)
                link(dve.tensor_tensor(gl[:, 2, :, :], gl[:, 2, :, :], per_token(gs[:, 0, :]), ALU.mult), g_v)
                link(dve.tensor_scalar(gl[:, 4, :, :], lg, 0.0, None, ALU.is_gt), g_v)
                link(dve.tensor_tensor(gl[:, 5, :, :], gl[:, 4, :, :], gl[:, 2, :, :], ALU.add), g_v)
                link(dve.tensor_scalar(gl[:, 6, :, :], lg, 0.0, None, ALU.max), g_v)
                link(dve.tensor_scalar(gs[:, 1, :], best, 0.0, None, ALU.max), g_v)
                link(dve.tensor_tensor(gl[:, 7, :, :], gl[:, 6, :, :], per_token(gs[:, 1, :]), ALU.subtract), g_v)
                assert links[g_v.name] == GV * b + GEXP
                dve.wait_ge(g_exp, b + 1)
                link(dve.tensor_tensor(gl[:, 9, :, :], gl[:, 8, :, :], gl[:, 5, :, :], ALU.mult), g_v)
                link(dve.tensor_reduce(gs[:, 0, :], gl[:, 9, :, :], AX.X, ALU.add), g_v)
                link(dve.reciprocal(gs[:, 1, :], gs[:, 0, :]), g_v)
                link(dve.tensor_tensor(rw_all[:, b * NT:(b + 1) * NT, :], gl[:, 9, :, :], per_token(gs[:, 1, :]), ALU.mult), g_v)
                assert links[g_v.name] == GV * (b + 1)

            def tiles2(it, first, last):
                for t in range(NT + PART2_LAG if last else NT):
                    m = NT * it + t

                    def live(lag):
                        return not (first and t < lag) and not (last and t - lag >= NT)

                    def add_up(c):
                        if not live(0):
                            return
                        if c == 0:
                            dve.tensor_copy(rw[:, t, :], rw_all[:, bass.ds(m, 1), :].rearrange("p a e -> p (a e)")).then_inc(rw_ok, 1)
                            dve.wait_ge(rw_ok, m + 1)
                            if not (first and t < 2):
                                dve.wait_ge(kv_ok, m - 1)
                                dve.wait_ge(hi2, 2 * (m - 1))
                        dve.wait_ge(e_ps, 8 * m + c + 1)
                        for e in range(2):
                            ex = 2 * c + e
                            src = exp_ps[:, c % 2, e * 3 * DE:(e + 1) * 3 * DE]
                            w = rw[:, t, ex:ex + 1]
                            if ex == 0:
                                ins = dve.tensor_scalar(acc[:, t % 2, :], src, w, None, ALU.mult)
                            else:
                                ins = dve.scalar_tensor_tensor(out=acc[:, t % 2, :], in0=src, scalar=w, in1=acc[:, t % 2, :],
                                                               op0=ALU.mult, op1=ALU.add)
                            if e == 0:
                                ins.then_inc(q_out, 1)
                                dve.wait_ge(q_out, 8 * m + c + 1)
                            else:
                                ins.then_inc(e_v, 1)
                                dve.wait_ge(e_v, 8 * m + c + 1)

                    add_up(0)
                    add_up(1)
                    if live(2):
                        v = (t - 2) % NT
                        dve.wait_ge(t2_ok, m - 1)
                        if not (first and t == 2):
                            dve.wait_ge(pv2, m - 2)
                        if v >= 4:
                            dve.tensor_copy(p2T[:, 4:v + 1, :], t2_ps[:, 1, 0:(v - 3) * P].rearrange("p (k q) -> p k q", k=v - 3)).then_inc(t2_V, 1)
                        else:
                            dve.sem_inc(t2_V, 1)
                    add_up(2)
                    if live(3):
                        dve.wait_ge(mt_ok, 2 * (m - 2))
                        if not (first and t == 3):
                            dve.wait_ge(o_ok, m - 3)
                        dve.tensor_copy(mxT[:, 4:8, :], t2_ps[:, 1, :].rearrange("p (g q) -> p g q", g=4)).then_inc(mt_V, 1)
                    add_up(3)
                    add_up(4)
                    if live(1):
                        v = (t - 1) % NT
                        dve.wait_ge(s2_ok, m)
                        dve.tensor_reduce(nm2[:, v % 2:v % 2 + 1], s2_ps[:, 0:(v + 1) * P], AX.X, ALU.max, negate=True).then_inc(max2, 1)
                    add_up(5)
                    if live(2):
                        v = (t - 2) % NT
                        dve.wait_ge(pv2, m - 1)
                        dve.reciprocal(rec2[:, v % 2:v % 2 + 1], sum2[:, v % 2:v % 2 + 1]).then_inc(rec2_ok, 1)
                        dve.wait_ge(rec2_ok, m - 1)
                        if not (first and t < 4):
                            dve.wait_ge(mt_ok, 2 * (m - 3))
                        dve.scalar_tensor_tensor(out=mx[:, v % 2, :, :], in0=o2_ps[:, DE:2 * DE].unsqueeze(1).to_broadcast([P, E, DE]),
                                                 scalar=rec2[:, v % 2:v % 2 + 1],
                                                 in1=rw[:, v, :].unsqueeze(2).to_broadcast([P, E, DE]),
                                                 op0=ALU.mult, op1=ALU.mult).then_inc(mx_ok, 1)
                    add_up(6)
                    if live(3):
                        v = (t - 3) % NT
                        dve.wait_ge(o_ok, m - 2)
                        if not (first and t < 5):
                            dve.wait_ge(stored[v % 2], 16 * (4 * it + (t - 5) // 2 + 1))
                        dve.tensor_tensor(yo[:, v % 2:v % 2 + 1, :], o2_ps[:, 0:C].unsqueeze(1), resid[:, bass.ds(m - 3, 1), :],
                                          ALU.add).then_inc(y_done, 1)
                    add_up(7)
                    if live(0):
                        dve.wait_ge(hi2, 2 * (m + 1))
                        dve.scalar_tensor_tensor(out=qs[:, t % 2, 0, DE:2 * DE], in0=acc[:, t % 2, 0:DE], scalar=DE ** -0.5,
                                                 in1=qs[:, t % 2, 0, 0:DE], op0=ALU.mult, op1=ALU.subtract).then_inc(lo2, 1)
                        dve.tensor_tensor(qs[:, t % 2, 2, :].rearrange("p (n d) -> p n d", n=2),
                                          acc[:, t % 2, DE:2 * DE].unsqueeze(1).to_broadcast([P, 2, DE]),
                                          qs[:, t % 2, 1, :].rearrange("p (n d) -> p n d", n=2), ALU.subtract).then_inc(lo2, 1)

            tiles2(0, True, False)
            with dve.Fori(1, B - 1) as it:
                tiles2(it, False, False)
            tiles2(B - 1, False, True)


_INS = ["L0_attn_x", "L0_attn_Wq", "L0_attn_Wkv", "L0_attn_Wout", "L0_attn_lambda_q1", "L0_attn_lambda_k1",
        "L0_attn_lambda_q2", "L0_attn_lambda_k2", "L0_attn_gamma", "L0_ffn_sim_matrix", "L0_ffn_gates",
        "L0_ffn_q_proj", "L0_ffn_k_proj", "L0_ffn_v_proj", "L0_ffn_o_proj"]


def kernel(**inputs):
    import concourse.bacc as bacc
    from concourse.bass_utils import run_bass_kernel_spmd

    nc = bacc.Bacc("TRN2", target_bir_lowering=False, num_devices=1)
    arrays, args = {}, []
    for name in _INS:
        a = np.ascontiguousarray(inputs[name])
        arrays[f"in_{name}"] = a
        args.append(nc.dram_tensor(f"in_{name}", a.shape, mybir.dt.from_np(a.dtype), kind="ExternalInput").ap())
    out = nc.dram_tensor("out_0", (B, T, C), F32, kind="ExternalOutput").ap()
    block_kernel(nc, *args, out)
    r = run_bass_kernel_spmd(nc, [arrays], core_ids=[0])
    return r.results[0]["out_0"]
```

```python
import math
from contextlib import ExitStack

import numpy as np
import concourse.bass as bass
from concourse import mybir

F32 = mybir.dt.float32
F16 = mybir.dt.float16
BF16 = mybir.dt.bfloat16
U32 = mybir.dt.uint32
ALU = mybir.AluOpType
ACT = mybir.ActivationFunctionType
AX = mybir.AxisListType

P = 128
B, T, C = 4, 1024, 128
NT = T // P
H, D = 8, 32
DV = 2 * D
G = H // 2
STEPS = B * G
UNITS = 16
ITERS = STEPS // 2
SLOTS = 2 * UNITS
HALF = T // 2
LAMBDA_INIT = 0.8 - 0.6 * math.exp(-0.3)
QSCALE = D ** -0.5
RMS_EPS = 1e-8
LN_EPS = 1e-5

SCALE_V = 640
TRANS_LAG = 3
RMS_AFTER = 4
PV_LAG = 11
PV_END = PV_LAG + NT - 1
COPY_LAG = PV_END
ROWS_LAG = COPY_LAG + 1
STAT_LAG = ROWS_LAG + 1
NORM_LAG = STAT_LAG + 3
COLS_LAG = NORM_LAG + 1
PROJECT_LAG = COLS_LAG + 1
TAIL_SLOTS = PROJECT_LAG + 3
PROJ_SLOTS = {4: ("v1", 0), 5: ("k0", 1), 7: ("k1", 1), 12: ("v0", 1), 13: ("q0", 2), 15: ("q1", 2)}
PARTS = ("q0", "q1", "k0", "k1", "v0", "v1")
AHEAD = ("q0", "q1", "k0", "k1", "v0")
FIRST_SLOTS = {0: ("ln", 0), 1: ("ln", 1), 2: ("ln", 2), 3: ("q0", 1), 6: ("q1", 1), 8: ("ln", 3), 9: ("ln", 4), 10: ("ln", 5)}

E, DE = 16, 64
MASKED = -1e30
GATE_LEAST = 1e-12
WSCALE = 64.0
PART2_LAG = 4
EARLY = 3
POOL_BATCHES = (0, 1)
LN2_SLOT = SLOTS + 1
BT = EARLY * NT
RSQ_SHIFT = 2.0 ** 30
RSQ_LEAST = 2.0 ** -64


SPLIT_PRODUCTS = ((0, 0), (0, 1), (1, 0))


def unit_of(s):
    j, u = divmod(s, UNITS)
    return j, j % 2, u // 8, (u // 4) % 2, u % 4, u % 8


def present(half, first, last):
    return not (first and half < 0) and not (last and half > 3)


def half_at(s, lag, first, last):
    half, rest = divmod(s - lag, 8)
    return half if rest == 0 and present(half, first, last) else None


def misc_fill(s, first, last):
    if first and s in FIRST_SLOTS:
        return FIRST_SLOTS[s]
    for stage, lag in (("rows", ROWS_LAG), ("cols", COLS_LAG), ("project", PROJECT_LAG)):
        if (s - lag) % 8 == 0:
            half = half_at(s, lag, first, last)
            return None if half is None else (stage, half)
    if s % UNITS not in PROJ_SLOTS or (first and s < 0):
        return None
    part, ahead = PROJ_SLOTS[s % UNITS]
    step = s // UNITS + ahead
    return None if last and step > 1 else (part, step)


def misc_fill_before(s, first, last):
    for r in range(s - 1, s - UNITS - 1, -1):
        if first and r < 0:
            return (AHEAD[-1], 0)
        if found := misc_fill(r, first, last):
            return found


def block_kernel(nc, x, wq, wkv, wout, lq1, lk1, lq2, lk2, gamma, sim, gates, eq, ek, ev, eo, out):
    ctx = ExitStack()
    with ctx:
        stack_of = {"memory": ctx}

        def sb(name, shape, dt=F32):
            return stack_of["memory"].enter_context(nc.sbuf_tensor(name, shape, dt))

        def ps(name, shape, dt=F32):
            return stack_of["memory"].enter_context(nc.psum_tensor(name, shape, dt))

        def sem(name):
            return ctx.enter_context(nc.semaphore(name))

        resid = sb("resid", [P, B * NT, C])
        xnT = sb("xnT", [P, B * T])
        wo_sb = sb("wo_sb", [P, G, C])
        gcol = sb("gcol", [P, 1])
        ident = sb("ident", [P, P])
        lam_in = sb("lam_in", [P, 4, D])
        lam_pr = sb("lam_pr", [P, 2, D])
        lam = sb("lam", [P, 6])
        stat = sb("stat", [P, 8, B * NT])
        simn = sb("simn", [P, E])
        simn_split = sb("simn_split", [P, 2, E], F16)
        sgate = sb("sgate", [P, E])
        small = sb("small", [P, 8, E])
        iota = sb("iota", [P, E])
        ones = sb("ones", [P, P])
        identb = sb("identb", [P, P], BF16)
        identh = sb("identh", [P, P], F16)
        causal = sb("causal", [P, P], BF16)

        prob1 = sb("prob1", [P, 4, T])
        prob2 = sb("prob2", [P, 4, T])
        x2c = prob2.rearrange("p b (t c) -> p (b t) c", c=C)
        x2sq = prob1
        x2n = xnT.rearrange("p (t c) -> p t c", c=C)
        gs = sb("gs", [P, 8, B * NT])
        part1 = ExitStack()
        stack_of["memory"] = part1
        xg = sb("xg", [P, 2, T])
        wg = sb("wg", [P, 2, 3, P])
        split = sb("split", [P, 4, T], F16)
        qa = sb("qa", [P, 2, 4, T], F16)
        ka = sb("ka", [P, 2, 4, T], F16)
        v_sb = sb("v_sb", [P, 2, NT, P])
        probT = sb("probT", [P, 2, NT, 2, HALF])
        negmax = sb("negmax", [P, 2, 2])
        sums = sb("sums", [P, 4, 2, 8])
        recip2 = sb("recip2", [P, 2])
        ccol = sb("ccol", [P, 4])
        attnT = sb("attnT", [P, HALF])
        attn_both = sb("attn_both", [P, 2, 4, 2, DV])
        attn, attn_sq = attn_both[:, 0, :, :, :], attn_both[:, 1, :, :, :]
        rms_const = sb("rms_const", [P, 2])
        attn_n = sb("attn_n", [P, 4, 2, DV])
        attn_nT = sb("attn_nT", [P, 4, P])
        tl = sb("tl", [P, 12, 8])
        xn_last = attn_both[:, :, :, :, :].rearrange("p n t h d -> p (n t h d)")
        xc_all = probT[:, 0, :, :, :].rearrange("p a b c -> p (a b c)")[:, 0:B * T]
        xn_all = probT[:, 1, :, :, :].rearrange("p a b c -> p (a b c)")[:, 0:B * T]
        xc = [xc_all[:, b * T:(b + 1) * T] for b in range(B)]
        xn = [xn_all[:, b * T:(b + 1) * T] for b in range(B - 1)] + [xn_last]
        xsq = [prob1[:, b, :] for b in range(B)]
        score_ps = ps("score_ps", [P, 2, T])
        trans_ps = ps("trans_ps", [P, 2, 512])
        attn_ps = ps("attn_ps", [P, HALF])
        misc_ps = ps("misc_ps", [P, 512])
        ahead_ps = [score_ps[:, n // 2, n % 2 * HALF:(n % 2 + 1) * HALF] for n in range(4)] + [misc_ps[:, :]]

        part1.close()
        stack_of["memory"] = ctx
        ew = sb("ew", [P, E, 3 * DE])
        eow = sb("eow", [P, E // 2, C])
        x2T = sb("x2T", [P, 2, 2, T], F16)
        gl = sb("gl", [P, 10, B * NT, E])
        top8 = sb("top8", [P, B * NT, 8])
        top8i = sb("top8i", [P, B * NT, 8], U32)
        top2f = sb("top2f", [P, B * NT, 2])
        rw_all = sb("rw_all", [P, B * NT, E])
        xs = sb("xs", [P, 2, E, C])
        ew_split = sb("ew_split", [P, 2, E, 3 * DE], F16)
        eow_split = sb("eow_split", [P, 2, E // 2, C], F16)
        xsT = sb("xsT", [P, 2, 2, E, P], F16)
        kv2 = sb("kv2", [P, NT, 2 * DE])
        kv_first = sb("kv_first", [P, 2 * DE])
        qs = sb("qs", [P, 2, 3, P], F16)
        qkT = sb("qkT", [P, 3, T], F16)
        p2 = sb("p2", [P, 2, T])
        p2T = sb("p2T", [P, NT, P])
        nm2 = sb("nm2", [P, 2])
        sum2 = sb("sum2", [P, 2])
        rec2 = sb("rec2", [P, 2])
        mx = sb("mx", [P, 2, E, DE])
        mxT = sb("mxT", [P, 2, E // 2, P], F16)
        yo = sb("yo", [P, 2, C])

        t_ps = ps("t_ps", [P, 2, 512])
        s2_ps = ps("s2_ps", [P, T])
        qkv_ps = ps("qkv_ps", [P, 512])
        qk_ps = ps("qk_ps", [P, 1024], F16)
        o2_ps = ps("o2_ps", [P, 512])
        y_ps = ps("y_ps", [P, 512])

        x_in, const_in = [sem(f"x_in{b}") for b in range(B)], sem("const_in")
        ident_ok, lam_ok, wo_ok, lam_chain, lam_exp = (sem(n) for n in ("ident_ok", "lam_ok", "wo_ok", "lam_chain", "lam_exp"))
        ln_v, ln_sq, ln_y, ln_T, ln_A, ln_V, ln_late = (sem(n) for n in ("ln_v", "ln_sq", "ln_y", "ln_T", "ln_A", "ln_V", "ln_late"))
        ln_mean_v, ln_mean, ln_centred, ln_scale, ln_normed = (sem(n) for n in ("ln_mean_v", "ln_mean", "ln_centred", "ln_scale", "ln_normed"))
        first_weights, first_stacked = sem("first_weights"), sem("first_stacked")
        step_in = (sem("step_in_even"), sem("step_in_odd"))
        stacked = {"q": sem("q_stacked"), "k": sem("k_stacked")}
        filled = {part: sem("filled_" + part) for part in PARTS}
        high_ok = {"q": sem("q_high_ok"), "k": sem("k_high_ok")}
        low_ok = {"q": sem("q_low_ok"), "k": sem("k_low_ok")}
        v_ok, scaled_P, scaled_V = sem("v_ok"), sem("scaled_P"), sem("scaled_V")
        score_ok, max_ok, exp_ok, rec_ok, c_ok, mix_ok = (sem(n) for n in ("score_ok", "max_ok", "exp_ok", "rec_ok", "c_ok", "mix_ok"))
        trans_ok, pv_ok, attnT_ok = (sem(n) for n in ("trans_ok", "pv_ok", "attnT_ok"))
        probT_ok = (sem("probT_ok_0"), sem("probT_ok_1"))
        rows_ok, attn_copied, stat_ok, rms_v, norm_v = (sem(n) for n in ("rows_ok", "attn_copied", "stat_ok", "rms_v", "norm_v"))
        cols_ok, attn_nT_ok, out_ok, resid_ok = (sem(n) for n in ("cols_ok", "attn_nT_ok", "out_ok", "resid_ok"))
        rms_const_ok = sem("rms_const_ok")
        experts_in = sem("experts_in")
        const2_in, iota_ok, mask_ok = sem("const2_in"), sem("iota_ok"), sem("mask_ok")
        g_top, w_scaled, w_hi, w_lo = sem("g_top"), sem("w_scaled"), sem("w_hi"), sem("w_lo")
        c2_v, c2_a, c2_p = sem("c2_v"), sem("c2_a"), sem("c2_p")
        g_sum, g_mean, g_cP, g_cV, g_sq, g_ss, g_y, g_scale, g_nP, g_nV, g_T, g_A, g_V, g_lg, g_v, g_exp, rw_ok = (
            sem("g_" + n) for n in ("sum", "mean", "centred_P", "centred_V", "sq", "ss", "y", "scale", "normed_P",
                                    "normed_V", "T", "A", "V", "lg", "v", "exp", "rw"))
        (xs_ok, xT_ps, xT_hi, xT_lo, qkv_ok, hi2, lo2, kv_read, kv_first_ok, qkt_ps, qkt_ok, s2_ok, max2, exp2, pT_ps,
         pT_A, pT_V, pv2, rec2_ok, mx_ok, mT_ps, mT_hi, mT_lo, y_ok, y_done) = (sem("p2_" + n) for n in (
            "xs", "xT_ps", "xT_hi", "xT_lo", "qkv", "hi", "lo", "kv_read", "kv_first", "qkt_ps", "qkt", "s", "max", "exp",
            "pT_ps", "pT_A", "pT_V", "pv", "rec", "mx", "mT_ps", "mT_hi", "mT_lo", "y", "y_done"))
        stored = [sem("stored0"), sem("stored1")]

        C2V = 12
        GLATE, GNORM, GEXP = 6, 13, 22

        def gate_ps(n, half):
            return (t_ps[:, half, :], s2_ps[:, half * 512:(half + 1) * 512])[n % 2]

        def misc_free(eng, s, it, first, last):
            kind, which = misc_fill_before(s, first, last)
            if kind in PARTS:
                read(eng, kind, 2 * it + which)
            elif kind == "ln":
                eng.wait_ge(ln_late, which + 1)
            elif kind == "rows":
                eng.wait_ge(attn_copied, 2 * (4 * it + which + 1))
            elif kind == "cols":
                eng.wait_ge(attn_nT_ok, 4 * it + which + 1)
            else:
                eng.wait_ge(resid_ok, 4 * it + which + 1)

        def read(eng, part, j):
            eng.wait_ge(v_ok if part[0] == "v" else low_ok[part[0]], 2 * j + int(part[1]) + 1)

        def copy_probT(eng, copy, s, n, it, bank, first, last):
            v = s - TRANS_LAG
            if (first and v < 0) or (last and v >= SLOTS):
                return
            half, u = v // 8, v % 8
            if u == 0 and not (first and half < 2):
                eng.wait_ge(pv_ok, 8 * (4 * it + half - 1))
            eng.wait_ge(trans_ok, 2 * (n - TRANS_LAG) + bank + 1)
            copy(probT[:, half % 2, 4 * bank:4 * bank + 4, u // 4, (u % 4) * P:(u % 4 + 1) * P],
                 trans_ps[:, bank, :].rearrange("p (k q) -> p k q", k=4)).then_inc(probT_ok[bank], 1)

        def dve_copies(s):
            return (s - ROWS_LAG) % 8 == 0

        block = ctx.enter_context(nc.Block())

        @block.sync
        def _(sp):
            def weights(par, column0, done):
                for n, w in enumerate((wq[:, bass.ds(column0, P)], wkv[:, bass.ds(column0, P)],
                                       wkv[:, bass.ds(column0 + H * DV, P)])):
                    sp.dma_start(wg[:, par, n, :], w).then_inc(done, 16)

            sp.dma_start(simn[:, :], sim).then_inc(const2_in, 16)
            sp.dma_start(sgate[:, :], gates.rearrange("(a e) -> a e", a=1).to_broadcast([P, E])).then_inc(const2_in, 16)
            for b in range(B):
                sp.dma_start(resid[:, b * NT:(b + 1) * NT, :],
                             x[b].rearrange("(t p) c -> p t c", p=P)).then_inc(x_in[b], 16)
                if b == 0:
                    weights(0, 0, first_weights)
            weights(1, P, first_weights)
            for n, v in enumerate((lq1, lk1, lq2, lk2)):
                sp.dma_start(lam_in[:, n, :], v.rearrange("(a d) -> a d", a=1).to_broadcast([P, D])).then_inc(const_in, 16)
            sp.dma_start(gcol[0:DV, :], gamma.rearrange("(d a) -> d a", a=1)).then_inc(const_in, 16)
            sp.dma_start(gcol[DV:P, :], gamma.rearrange("(d a) -> d a", a=1)).then_inc(const_in, 16)
            sp.dma_start(wo_sb[:, :, :], wout.rearrange("(g p) c -> p g c", p=P)).then_inc(const_in, 16)

            out_rows = out.rearrange("b (t p) c -> p (b t) c", p=P)

            def load_step(par, token0, column0):
                weights(par, column0, step_in[par])
                sp.dma_start(xg[:, par, :], xnT[:, bass.ds(token0, T)]).then_inc(step_in[par], 16)

            def stack_rows(kind, par, subs, done):
                dst, base, order = {"q": (qa, 0, (0, 0, 1, 1)), "k": (ka, 2, (0, 1, 0, 1))}[kind]
                for sub in subs:
                    for row, part in enumerate(order):
                        sp.dma_start(dst[D * row:D * row + D, par, sub, :],
                                     split[D * sub:D * sub + D, base + part, :]).then_inc(done, 16)

            def stack(kind, par, j, scored=None):
                halves, tiles = 2 * (j + 1), None if scored is None else 2 * scored
                sp.wait_ge(low_ok[kind], halves)
                if scored is not None:
                    sp.wait_ge(score_ok, tiles)
                stack_rows(kind, par, range(4), stacked[kind])

            for kind in "qk":
                sp.wait_ge(low_ok[kind], 2)
                stack_rows(kind, 0, (0, 1), first_stacked)
            for kind in "qk":
                stack_rows(kind, 0, (2, 3), stacked[kind])
            for par in range(2):
                sp.dma_start(xg[:, par, :], xnT[:, 0:T]).then_inc(step_in[par], 16)
            stack("q", 1, 1)

            def two_steps(it, first, last):
                for k in range(2):
                    j = 2 * it + k
                    if not last:
                        token0, column0 = (j + 2) // G * T, (j + 2) % G * P
                        sp.wait_ge(filled["v1"], j + 1)
                        load_step(k, token0, column0)
                    if not (last and k == 1):
                        stack("k", (k + 1) % 2, j + 1, None if first and k == 0 else UNITS * j)
                    if not last:
                        stack("q", k, j + 2, UNITS * (j + 1))

            two_steps(0, True, False)
            sp.wait_ge(ln_late, 6)
            with sp.Fori(1, ITERS - 1) as it:
                two_steps(it, False, False)
            two_steps(ITERS - 1, False, True)
            sp.wait_ge(resid_ok, 2 * STEPS)
            for n, w in enumerate((eq, ek, ev)):
                sp.dma_start(ew[:, :, n * DE:(n + 1) * DE], w.rearrange("e c d -> c e d")).then_inc(experts_in, 16)
            for half in range(2):
                sp.dma_start(eow[half * DE:(half + 1) * DE, :, :],
                             eo.rearrange("(g two) d c -> two d g c", two=2)[half]).then_inc(experts_in, 16)

            def store(tile, r):
                sp.wait_ge(y_done, tile + 1)
                sp.dma_start(out_rows[:, bass.ds(tile, 1), :], yo[:, r:r + 1, :]).then_inc(stored[r], 16)

            with sp.Fori(0, B * NT // 2) as pair:
                store(2 * pair, 0)
                store(2 * pair + 1, 1)
            for r in range(2):
                sp.wait_ge(stored[r], 16 * B * NT // 2)

        @block.gpsimd
        def _(pool):
            pool.memset(ident[:, :], 0.0).then_inc(ident_ok, 1)
            pool.wait_ge(ident_ok, 1)
            pool.affine_select(out=ident[:, :], in_=ident[:, :], compare_op=ALU.not_equal, fill=1.0, base=0,
                               pattern=[[-1, P]], channel_multiplier=1).then_inc(ident_ok, 1)

            pool.memset(rms_const[:, 0:1], 0.5).then_inc(rms_const_ok, 1)
            pool.memset(rms_const[:, 1:2], RMS_EPS).then_inc(rms_const_ok, 1)
            pool.wait_ge(rms_const_ok, 2)
            pool.memset(ones[:, :], 1.0).then_inc(iota_ok, 1)
            for e in range(E):
                pool.memset(iota[:, e:e + 1], float(e)).then_inc(iota_ok, 1)
            pool.memset(causal[:, :], 0.0).then_inc(mask_ok, 1)
            pool.wait_ge(mask_ok, 1)
            pool.affine_select(out=causal[:, :], in_=causal[:, :], compare_op=ALU.is_ge, fill=MASKED, base=0,
                               pattern=[[-1, P]], channel_multiplier=1).then_inc(mask_ok, 1)
            for i in (identb, identh):
                pool.memset(i[:, :], 0.0).then_inc(mask_ok, 1)
            pool.wait_ge(mask_ok, 4)
            for i in (identb, identh):
                pool.affine_select(out=i[:, :], in_=i[:, :], compare_op=ALU.not_equal, fill=1.0, base=0,
                                   pattern=[[-1, P]], channel_multiplier=1).then_inc(mask_ok, 1)

            def tokens(ap):
                return ap.unsqueeze(2).to_broadcast([P, NT, C])

            def tiles(ap):
                return ap.rearrange("p (t c) -> p t c", t=NT)

            pool.wait_ge(ln_mean, 1)
            for b in range(1, B):
                pool.tensor_tensor(tiles(xc[b]), resid[:, b * NT:(b + 1) * NT, :],
                                   tokens(stat[:, 1, b * NT:(b + 1) * NT]), ALU.add).then_inc(ln_centred, 1)
            pool.wait_ge(ln_centred, B - 1)
            pool.wait_ge(ln_scale, 1)
            for b in range(1, B):
                pool.tensor_tensor(tiles(xn[b]), tiles(xc[b]), tokens(stat[:, 7, b * NT:(b + 1) * NT]),
                                   ALU.mult).then_inc(ln_normed, 1)

            def mix(n, u):
                pool.wait_ge(c_ok, n + 1)
                pool.tensor_tensor(prob2[:, u, SCALE_V:T], prob2[:, u, SCALE_V:T],
                                   ccol[:, u:u + 1].to_broadcast([P, T - SCALE_V]), ALU.mult).then_inc(scaled_P, 1)
                pool.wait_ge(scaled_P, n + 1)
                pool.wait_ge(scaled_V, n + 1)
                pool.tensor_tensor(prob1[:, u, :], prob1[:, u, :], prob2[:, u, :], ALU.add).then_inc(mix_ok, 1)

            def rms(h):
                pool.wait_ge(stat_ok, 2 * (h + 1))
                pool.tensor_tensor(tl[:, 2, :], tl[:, 1, :], tl[:, 1, :], ALU.mult).then_inc(rms_v, 1)
                pool.wait_ge(rms_v, 4 * h + 1)
                pool.tensor_tensor(tl[:, 3, :], tl[:, 2, :], tl[:, 0, :], ALU.mult).then_inc(rms_v, 1)
                pool.wait_ge(rms_v, 4 * h + 2)
                pool.tensor_tensor(tl[:, 4, :], tl[:, 3, :], rms_const[:, 0:1].to_broadcast([P, 8]), ALU.pow).then_inc(rms_v, 1)
                pool.wait_ge(rms_v, 4 * h + 3)
                pool.tensor_tensor(tl[:, 5, :], tl[:, 4, :], rms_const[:, 1:2].to_broadcast([P, 8]), ALU.add).then_inc(rms_v, 1)

            def units(h, tail):
                for u in range(8):
                    mix(8 * h + u, u % 4)
                    if tail and u == RMS_AFTER:
                        rms(h - 2)

            with pool.Fori(0, 2) as h:
                units(h, False)
            with pool.Fori(2, 2 * STEPS) as h:
                units(h, True)
            pool.wait_ge(g_mean, 1)
            pool.wait_ge(mix_ok, STEPS * UNITS)
            for b in POOL_BATCHES:
                pool.tensor_tensor(x2c[:, b * NT:(b + 1) * NT, :], resid[:, b * NT:(b + 1) * NT, :],
                                   tokens(gs[:, 1, b * NT:(b + 1) * NT]), ALU.add).then_inc(g_cP, 1)
            rms(2 * STEPS - 2)
            pool.wait_ge(g_cP, 2)
            pool.wait_ge(g_scale, 1)
            for b in POOL_BATCHES:
                pool.tensor_tensor(x2n[:, b * NT:(b + 1) * NT, :], x2c[:, b * NT:(b + 1) * NT, :],
                                   tokens(gs[:, 6, b * NT:(b + 1) * NT]), ALU.mult).then_inc(g_nP, 1)
            rms(2 * STEPS - 1)

            pool.wait_ge(resid_ok, 2 * STEPS)
            for n, (w, split_w) in enumerate(((ew, ew_split), (eow, eow_split))):
                pool.wait_ge(w_hi, n + 1)
                pool.tensor_tensor(split_w[:, 1, :, :], w[:, :, :], split_w[:, 0, :, :], ALU.subtract).then_inc(w_lo, 1)
            pool.wait_ge(g_nP, 2)
            pool.wait_ge(g_nV, 2)
            pool.wait_ge(rw_ok, 1)

            def scale_by_experts(m, r, peeled):
                if not peeled:
                    pool.wait_ge(xT_ps, 4 * (m - 1))
                pool.tensor_tensor(xs[:, r, :, :], x2n[:, bass.ds(m, 1), :].to_broadcast([P, E, C]),
                                   rw_all[:, bass.ds(m, 1), :].rearrange("p a e -> p e a").to_broadcast([P, E, C]),
                                   ALU.mult).then_inc(xs_ok, 1)

            scale_by_experts(0, 0, True)
            scale_by_experts(1, 1, True)
            with pool.Fori(1, B * NT // 2) as pair:
                scale_by_experts(2 * pair, 0, False)
                scale_by_experts(2 * pair + 1, 1, False)

        @block.tensor
        def _(pe):
            pe.wait_ge(ident_ok, 2)

            pe.wait_ge(c2_v, 1)
            pe.wait_ge(iota_ok, 1)
            pe.matmul(misc_ps[:, 0:E], ones[:, :], small[:, 0, :], start=True, stop=True).then_inc(c2_p, 1)

            pe.wait_ge(ln_v, 10)
            for t in range(NT):
                mm = pe.transpose(trans_ps[:, t // 4, t % 4 * P:(t % 4 + 1) * P], xn[0][:, t * P:(t + 1) * P], ident[:, :])
                if t % 4 == 3:
                    mm.then_inc(ln_T, 1)

            def proj_fill(part, into, x, par):
                half = int(part[1])
                if part[0] != "v":
                    mm = pe.matmul(into, wg[:, par, "qk".index(part[0]), :],
                                   x[:, half * HALF:(half + 1) * HALF], start=True, stop=True)
                else:
                    for t in range(4):
                        tile = half * 4 + t
                        mm = pe.matmul(into[:, t * P:(t + 1) * P], x[:, tile * P:(tile + 1) * P],
                                       wg[:, par, 2, :], start=True, stop=True)
                mm.then_inc(filled[part], 1)

            pe.wait_ge(first_weights, 96)
            pe.wait_ge(ln_A, 1)
            pe.wait_ge(ln_V, 1)
            for n, part in enumerate(AHEAD):
                proj_fill(part, ahead_ps[n], xnT[:, 0:T], 0)

            def scores(n, s, sub, peeled):
                j, par, half, head, qt, _ = unit_of(s)
                if not (peeled and n < 1):
                    pe.wait_ge(exp_ok, 2 * n - 1 + sub)
                q0 = (half * 4 + qt) * P
                for kh in range(2):
                    mm = pe.matmul(score_ps[:, sub, kh * HALF:(kh + 1) * HALF],
                                   qa[:, par, head * 2 + sub, q0:q0 + P],
                                   ka[:, par, head * 2 + sub, kh * HALF:(kh + 1) * HALF], start=True, stop=True)
                mm.then_inc(score_ok, 1)

            def slots(it, first, last):
                end = SLOTS - 8 + TAIL_SLOTS if last else SLOTS
                if first:
                    pe.wait_ge(first_stacked, 256)
                    scores(0, 0, 0, True)
                for s in range(end):
                    n = SLOTS * it + s
                    if s < SLOTS:
                        scores(n, s, 1, first and s == 0)
                    u = s - TRANS_LAG
                    if not (first and u < 0) and not (last and u >= SLOTS):
                        pe.wait_ge(mix_ok, n - TRANS_LAG + 1)
                        for kb in range(2):
                            if not (first and u == 0):
                                pe.wait_ge(probT_ok[kb], n - TRANS_LAG)
                            for t in range(4):
                                k0 = (kb * 4 + t) * P
                                mm = pe.transpose(trans_ps[:, kb, t * P:(t + 1) * P], prob1[:, u % 4, k0:k0 + P], ident[:, :])
                            mm.then_inc(trans_ok, 1)
                    half, kt = divmod(s - PV_LAG, 8)

                    def values(head):
                        return pe.matmul(attn_ps[head * DV:(head + 1) * DV, :],
                                         v_sb[:, (half // 2) % 2, kt, head * DV:(head + 1) * DV],
                                         probT[:, half % 2, kt, head, :], start=kt == 0, stop=kt == 7)

                    if present(half, first, last):
                        if kt == 0:
                            pe.wait_ge(probT_ok[0], 8 * (4 * it + half + 1))
                            pe.wait_ge(probT_ok[1], 8 * (4 * it + half + 1))
                            if not (first and half == 0):
                                pe.wait_ge(attnT_ok, 4 * it + half)
                        if half % 2 == 0 and kt in (0, 4):
                            pe.wait_ge(v_ok, 2 * (2 * it + half // 2) + kt // 4 + 1)
                        values(0)
                    if s + 1 < SLOTS or not last:
                        if (s + 1) % UNITS == 0 or (first and s + 1 == 4):
                            j = 2 * it + (s + 1) // UNITS
                            pe.wait_ge(stacked["q"], 256 * j + 128)
                            pe.wait_ge(stacked["k"], 256 * j + 128)
                        scores(n + 1, s + 1, 0, False)
                    if present(half, first, last):
                        values(1).then_inc(pv_ok, 1)
                    fill = misc_fill(s, first, last)
                    if fill:
                        misc_free(pe, s, it, first, last)
                        kind, which = fill
                        if kind in PARTS:
                            pe.wait_ge(step_in[which % 2], 64 * (it + which // 2) + 16)
                            proj_fill(kind, misc_ps[:, :], xg[:, which % 2, :], which % 2)
                        elif kind == "ln":
                            b = 1 + which // 2
                            pe.wait_ge(ln_normed, b)
                            for t in range(4):
                                c0 = (which % 2 * 4 + t) * P
                                mm = pe.transpose(misc_ps[:, t * P:(t + 1) * P], xn[b][:, c0:c0 + P], ident[:, :])
                            mm.then_inc(ln_T, 1)
                        elif kind == "rows":
                            pe.wait_ge(attnT_ok, 4 * it + which + 1)
                            for t in range(4):
                                mm = pe.transpose(misc_ps[:, t * P:(t + 1) * P], attnT[:, t * P:(t + 1) * P], ident[:, :])
                            mm.then_inc(rows_ok, 1)
                        elif kind == "cols":
                            pe.wait_ge(norm_v, 3 * (4 * it + which + 1))
                            for t in range(4):
                                mm = pe.transpose(misc_ps[:, t * P:(t + 1) * P],
                                                  attn_n[:, t, :, :].rearrange("p h d -> p (h d)"), ident[:, :])
                            mm.then_inc(cols_ok, 1)
                        else:
                            pe.wait_ge(attn_nT_ok, 4 * it + which + 1)
                            if which == 0 and first:
                                pe.wait_ge(wo_ok, 1)
                            step = 2 * it + which // 2
                            wo_g = wo_sb[:, bass.ds(step % G, 1), :].rearrange("p a c -> p (a c)")
                            for t in range(4):
                                mm = pe.matmul(misc_ps[:, t * P:(t + 1) * P], attn_nT[:, t, :], wo_g,
                                               start=True, stop=True)
                            mm.then_inc(out_ok, 1)

            slots(0, True, False)
            with pe.Fori(1, ITERS - 1) as it:
                slots(it, False, False)
            slots(ITERS - 1, False, True)

            pe.wait_ge(resid_ok, 2 * STEPS)
            pe.wait_ge(mask_ok, 6)

            def gate_logits(n):
                pe.wait_ge(g_V, 2 * (n + 1))
                if n == 0:
                    pe.wait_ge(c2_v, C2V)
                for t in range(NT):
                    for k, (x_part, w_part) in enumerate(SPLIT_PRODUCTS):
                        mm = pe.matmul(qkv_ps[:, (n * NT + t) * E:(n * NT + t + 1) * E], x2T[:, n % 2, x_part, t * P:(t + 1) * P],
                                       simn_split[:, w_part, :], start=k == 0, stop=k == 2)
                mm.then_inc(g_lg, 1)

            for n in range(B):
                pe.wait_ge(*((g_nP, n + 1) if n in POOL_BATCHES else (g_nV, n - 1)))
                if n >= 2:
                    pe.wait_ge(g_V, 2 * (n - 1))
                for t in range(NT):
                    mm = pe.transpose(gate_ps(n, t // 4)[:, t % 4 * P:(t % 4 + 1) * P], x2n[:, n * NT + t, :], ident[:, :])
                    if t % 4 == 3:
                        mm.then_inc(g_T, 1)
                if n:
                    gate_logits(n - 1)
            gate_logits(B - 1)
            pe.wait_ge(w_lo, 2)
            pe.wait_ge(rw_ok, 1)
            pe.wait_ge(g_V, 2 * B)

            def tiles2(it, first, last):
                for t in range(NT + PART2_LAG if last else NT):
                    m = NT * it + t

                    def live(lag):
                        return not (first and t < lag) and not (last and t - lag >= NT)

                    def bank_read(bank, before):
                        pT = (pT_A, pT_V)[bank]
                        for what in before:
                            if what == "x0" and live(0):
                                return pe.wait_ge(xT_lo, 4 * m + bank + 1)
                            if what == "x1" and live(0):
                                return pe.wait_ge(xT_lo, 4 * m + 2 + bank + 1)
                            if what == "x1 of m - 1" and live(1):
                                return pe.wait_ge(xT_lo, 4 * (m - 1) + 2 + bank + 1)
                            if what == "p" and live(2):
                                return pe.wait_ge(pT, m - 1)
                            if what == "y of m - 1" and live(4):
                                return pe.wait_ge(mT_lo, 2 * (m - 4) + bank + 1)

                    def x_transposes(group, bank):
                        if not live(0):
                            return
                        if group == 0:
                            pe.wait_ge(xs_ok, m + 1)
                        bank_read(bank, ("y of m - 1", "x1 of m - 1") if group < 2 else ("p", "x0"))
                        for e in range(4):
                            mm = pe.transpose(t_ps[:, bank, e * P:(e + 1) * P], xs[:, t % 2, 4 * group + e, :], ident[:, :])
                        mm.then_inc(xT_ps, 1)

                    def experts(group):
                        if not live(0):
                            return
                        pe.wait_ge(xT_lo, 4 * m + group + 1)
                        if group == 0 and not (first and t == 0):
                            pe.wait_ge(hi2, 2 * m)
                            pe.wait_ge(lo2, 2 * m)
                            pe.wait_ge(kv_read, m)
                        for e in range(4 * group, 4 * group + 4):
                            for n, (x_part, w_part) in enumerate(SPLIT_PRODUCTS):
                                mm = pe.matmul(qkv_ps[:, 0:3 * DE], xsT[:, t % 2, x_part, e, :], ew_split[:, w_part, e, :],
                                               start=e == 0 and n == 0, stop=e == E - 1 and n == 2)
                        if group == 3:
                            mm.then_inc(qkv_ok, 1)

                    def p_transposes(bank):
                        v = (t - 2) % NT
                        if not live(2):
                            return
                        if bank == 0:
                            pe.wait_ge(exp2, m - 1)
                        if 4 * bank > v:
                            return
                        bank_read(bank, ("x0", "y of m - 1"))
                        for kb in range(4 * bank, min(v, 4 * bank + 3) + 1):
                            mm = pe.transpose(t_ps[:, bank, kb % 4 * P:(kb % 4 + 1) * P],
                                              p2[:, v % 2, kb * P:(kb + 1) * P], ident[:, :])
                        mm.then_inc(pT_ps, 2 if v < 4 else 1)

                    def m_transposes(bank):
                        if not live(3):
                            return
                        v = (t - 3) % NT
                        if bank == 0:
                            pe.wait_ge(mx_ok, m - 2)
                        bank_read(bank, ("x1", "p", "y of m - 1"))
                        for g in range(4):
                            e = 8 * bank + 2 * g
                            mm = pe.transpose(t_ps[:, bank, g * P:(g + 1) * P],
                                              mx[:, v % 2, e:e + 2, :].rearrange("p e d -> p (e d)"), ident[:, :])
                        mm.then_inc(mT_ps, 1)

                    x_transposes(0, 0)
                    x_transposes(1, 1)
                    if live(4):
                        pe.wait_ge(mT_lo, 2 * (m - 3))
                        if not (first and t == 4):
                            pe.wait_ge(y_done, m - 4)
                        for g in range(8):
                            for n, (x_part, w_part) in enumerate(SPLIT_PRODUCTS):
                                mm = pe.matmul(y_ps[:, 0:C], mxT[:, x_part, g, :], eow_split[:, w_part, g, :],
                                               start=g == 0 and n == 0, stop=g == 7 and n == 2)
                        mm.then_inc(y_ok, 1)
                    if live(1):
                        v = (t - 1) % NT
                        pe.wait_ge(hi2, 2 * m)
                        pe.wait_ge(lo2, 2 * m)
                        if not (first and t == 1):
                            pe.wait_ge(qkt_ok, m - 1)
                        for n in range(3):
                            mm = pe.transpose(qk_ps[:, n * P:(n + 1) * P], qs[:, v % 2, n, :], identh[:, :])
                        mm.then_inc(qkt_ps, 1)
                    experts(0)
                    p_transposes(0)
                    p_transposes(1)
                    if live(1):
                        v = (t - 1) % NT
                        pe.wait_ge(qkt_ok, m)
                        if not (first and t == 1):
                            pe.wait_ge(exp2, m - 1)
                        keys = (v + 1) * P
                        for k0 in range(0, keys, 512):
                            k1 = min(k0 + 512, keys)
                            diag = k1 == keys
                            pe.matmul(s2_ps[:, k0:k1], qkT[:, 0, v * P:(v + 1) * P], qkT[:, 1, k0:k1], start=True, stop=False)
                            mm = pe.matmul(s2_ps[:, k0:k1], qkT[:, 0, v * P:(v + 1) * P], qkT[:, 2, k0:k1], start=False, stop=not diag)
                            if diag:
                                mm = pe.matmul(s2_ps[:, k1 - P:k1], identb[:, :], causal[:, :], start=False, stop=True)
                        mm.then_inc(s2_ok, 1)
                    experts(1)
                    x_transposes(2, 0)
                    x_transposes(3, 1)
                    if live(2):
                        v = (t - 2) % NT
                        pe.wait_ge(pT_A, m - 1)
                        pe.wait_ge(pT_V, m - 1)
                        pe.wait_ge(kv_read, m - 1)
                        pe.wait_ge(kv_first_ok, it + 1 if t >= 2 else it)
                        if not (first and t == 2):
                            pe.wait_ge(mx_ok, m - 2)
                        for kb in range(v + 1):
                            mm = pe.matmul(o2_ps[:, 0:2 * DE], p2T[:, kb, :], kv2[:, kb, :], start=kb == 0, stop=kb == v)
                        mm.then_inc(pv2, 1)
                    m_transposes(0)
                    m_transposes(1)
                    experts(2)
                    experts(3)

            tiles2(0, True, False)
            with pe.Fori(1, B - 1) as it:
                tiles2(it, False, False)
            tiles2(B - 1, False, True)

        @block.scalar
        def _(act):
            def act_copy(dst, src):
                return act.activation(dst, src, ACT.Copy)

            act.preload_act_table_set("natural_log_exp_and_others")

            def rsqrt_seed(y, l, v, ready, n, done_sem, k):
                act.wait_ge(ready, n)
                act.activation(l, v, ACT.Ln).then_inc(done_sem, 1)
                act.wait_ge(done_sem, k + 1)
                act.activation(y, l, ACT.Exp, scale=-0.5).then_inc(done_sem, 1)

            act.wait_ge(const2_in, 16 * 2)
            act.activation(small[:, 6, :], sgate[:, :], ACT.Exp, scale=-1.0).then_inc(c2_a, 1)
            rsqrt_seed(small[:, 3, :], small[:, 2, :], small[:, 1, :], c2_v, 2, c2_a, 1)

            act.wait_ge(ln_v, 3)
            act.activation(xsq[0], xc[0], ACT.Square).then_inc(ln_sq, 1)
            act.wait_ge(ln_v, 5)
            act.activation(stat[:, 3, 0:NT], stat[:, 2, 0:NT], ACT.Ln).then_inc(ln_y, 1)
            act.wait_ge(ln_y, 1)
            act.activation(stat[:, 4, 0:NT], stat[:, 3, 0:NT], ACT.Exp, scale=-0.5).then_inc(ln_y, 1)
            act.wait_ge(ln_T, 1)
            act.activation(xnT[:, 0:HALF], trans_ps[:, 0, :], ACT.Copy).then_inc(ln_A, 1)

            def proj_copy(part, j, par, wait_old, src):
                act.wait_ge(filled[part], j + 1)
                kind, half = part[0], int(part[1])
                if kind != "v":
                    if half == 0 and wait_old:
                        act.wait_ge(stacked[kind], 256 * j - 128)
                    if half == 0 and wait_old == "first":
                        act.wait_ge(first_stacked, 256)
                    act.activation(split[:, 2 * "qk".index(kind), half * HALF:(half + 1) * HALF], src,
                                   ACT.Copy, scale=QSCALE if kind == "q" else 1.0).then_inc(high_ok[kind], 1)
                else:
                    act.activation(v_sb[:, par, half * 4:(half + 1) * 4, :],
                                   src.rearrange("p (t d) -> p t d", t=4), ACT.Copy).then_inc(v_ok, 1)

            for n, part in enumerate(AHEAD):
                proj_copy(part, 0, 0, None, ahead_ps[n])
            act.wait_ge(lam_chain, 3)
            act.activation(lam[:, 2:4], lam[:, 0:2], ACT.Exp).then_inc(lam_exp, 1)
            for b in range(1, B):
                act.wait_ge(ln_centred, b)
                act.activation(xsq[b], xc[b], ACT.Square).then_inc(ln_sq, 1)
            act.wait_ge(ln_v, 14)
            act.activation(stat[:, 3, NT:], stat[:, 2, NT:], ACT.Ln).then_inc(ln_y, 1)
            act.wait_ge(ln_y, 3)
            act.activation(stat[:, 4, NT:], stat[:, 3, NT:], ACT.Exp, scale=-0.5).then_inc(ln_y, 1)

            def ln2_squares(b):
                act.wait_ge(*((g_cP, b + 1) if b in POOL_BATCHES else (g_cV, b - 1)))
                if b == 0:
                    act.wait_ge(trans_ok, 2 * STEPS * UNITS)
                act.activation(x2sq[:, b, :], x2c[:, b * NT:(b + 1) * NT, :].rearrange("p t c -> p (t c)"),
                               ACT.Square).then_inc(g_sq, 1)

            def slots(it, first, last):
                end = SLOTS - 8 + TAIL_SLOTS if last else SLOTS
                for s in range(end):
                    n = SLOTS * it + s

                    def softmax(sub):
                        act.wait_ge(max_ok, 2 * n + sub + 1)
                        if sub == 0 and not (first and s < 4):
                            act.wait_ge(trans_ok, 2 * (n - 3))
                        if sub == 1 and not (first and s < 4):
                            act.wait_ge(mix_ok, n - 3)
                        act.activation(prob2[:, s % 4, :] if sub else prob1[:, s % 4, :], score_ps[:, sub, :], ACT.Exp,
                                       bias=negmax[:, s % 2, sub:sub + 1],
                                       accum_out=sums[:, s // 8, sub, s % 8:s % 8 + 1]).then_inc(exp_ok, 1)

                    if s < SLOTS:
                        softmax(0)
                    copy_probT(act, act_copy, s, n, it, 0, first, last)
                    if s < SLOTS:
                        softmax(1)
                    if not dve_copies(s):
                        copy_probT(act, act_copy, s, n, it, 1, first, last)
                    half = half_at(s, COPY_LAG, first, last)
                    if half is not None:
                        act.wait_ge(pv_ok, 8 * (4 * it + half + 1))
                        if not (first and half == 0):
                            act.wait_ge(rows_ok, 4 * it + half)
                        act.activation(attnT[:, :], attn_ps[:, :], ACT.Copy).then_inc(attnT_ok, 1)
                    fill = misc_fill(s, first, last)
                    if fill and fill[0] in PARTS:
                        part, step = fill
                        proj_copy(part, 2 * it + step, step % 2, "first" if first and step == 1 else "later", misc_ps[:, :])
                    elif fill and fill[0] == "ln":
                        act.wait_ge(ln_T, 2 + fill[1] + 1)
                        act.activation(xnT[:, T + fill[1] * HALF:T + (fill[1] + 1) * HALF], misc_ps[:, :],
                                       ACT.Copy).then_inc(ln_late, 1)
                    elif fill and fill[0] == "rows":
                        act.wait_ge(rows_ok, 4 * it + fill[1] + 1)
                        act.activation(attn[:, :, :, :].rearrange("p t h d -> p (t h d)"), misc_ps[:, :],
                                       ACT.Copy).then_inc(attn_copied, 1)
                        act.activation(attn_sq[:, :, :, :].rearrange("p t h d -> p (t h d)"), misc_ps[:, :],
                                       ACT.Square, scale=DV ** -0.5).then_inc(attn_copied, 1)
                    elif fill and fill[0] == "cols":
                        act.wait_ge(cols_ok, 4 * it + fill[1] + 1)
                        act.activation(attn_nT[:, :, :].rearrange("p t q -> p (t q)"), misc_ps[:, :],
                                       ACT.Copy).then_inc(attn_nT_ok, 1)
                    if last and s - LN2_SLOT - 3 in range(EARLY):
                        ln2_squares(s - LN2_SLOT - 3)
                    if last and s == LN2_SLOT + 7:
                        rsqrt_seed(gs[:, 4, 0:BT], gs[:, 3, 0:BT], gs[:, 2, 0:BT], g_v, 1, g_y, 0)

            slots(0, True, False)
            with act.Fori(1, ITERS - 1) as it:
                slots(it, False, False)
            slots(ITERS - 1, False, True)

            def empty_gate(n):
                if n >= 2:
                    act.wait_ge(g_lg, n - 1)
                for half in range(2):
                    act.wait_ge(g_T, 2 * n + half + 1)
                    act.activation(x2T[:, n % 2, 0, half * HALF:(half + 1) * HALF], gate_ps(n, half), ACT.Copy).then_inc(g_A, 1)

            empty_gate(0)
            empty_gate(1)
            ln2_squares(B - 1)
            rsqrt_seed(gs[:, 4, BT:], gs[:, 3, BT:], gs[:, 2, BT:], g_v, GLATE, g_y, 2)
            empty_gate(2)
            rsqrt_seed(gs[:, 4, :], gs[:, 3, :], gs[:, 2, :], g_v, GNORM, g_y, 4)
            empty_gate(3)
            act.wait_ge(experts_in, 16 * 5)
            for w in (ew, eow):
                act.activation(w[:, :, :], w[:, :, :], ACT.Copy, scale=WSCALE).then_inc(w_scaled, 1)
            for n, (w, split_w) in enumerate(((ew, ew_split), (eow, eow_split))):
                act.wait_ge(w_scaled, n + 1)
                act.activation(split_w[:, 0, :, :], w[:, :, :], ACT.Copy).then_inc(w_hi, 1)
            act.wait_ge(g_v, GEXP)
            act.activation(gl[:, 8, :, :], gl[:, 7, :, :], ACT.Exp).then_inc(g_exp, 1)

            def tiles2(it, first, last):
                for t in range(NT + PART2_LAG if last else NT):
                    m = NT * it + t

                    def live(lag):
                        return not (first and t < lag) and not (last and t - lag >= NT)

                    def x_copy(group):
                        if not live(0):
                            return
                        act.wait_ge(xT_ps, 4 * m + group + 1)
                        if group == 0 and not (first and t < 2):
                            act.wait_ge(qkv_ok, m - 1)
                        act.activation(xsT[:, t % 2, 0, 4 * group:4 * group + 4, :],
                                       t_ps[:, group % 2, :].rearrange("p (e q) -> p e q", e=4), ACT.Copy).then_inc(xT_hi, 1)

                    x_copy(0)
                    x_copy(1)
                    if live(1):
                        v = (t - 1) % NT
                        act.wait_ge(qkt_ps, m)
                        if not (first and t == 1):
                            act.wait_ge(s2_ok, m - 1)
                        act.activation(qkT[:, :, v * P:(v + 1) * P], qk_ps[:, 0:3 * P].rearrange("p (n q) -> p n q", n=3),
                                       ACT.Copy).then_inc(qkt_ok, 1)
                    if live(2):
                        v = (t - 2) % NT
                        act.wait_ge(pT_ps, 2 * (m - 2) + 1)
                        if not (first and t == 2):
                            act.wait_ge(pv2, m - 2)
                        blocks = min(v + 1, 4)
                        act.activation(p2T[:, 0:blocks, :], t_ps[:, 0, 0:blocks * P].rearrange("p (k q) -> p k q", k=blocks),
                                       ACT.Copy).then_inc(pT_A, 1)
                    x_copy(2)
                    x_copy(3)
                    if live(1):
                        v = (t - 1) % NT
                        keys = (v + 1) * P
                        act.wait_ge(max2, m)
                        if not (first and t < 3):
                            act.wait_ge(pT_ps, 2 * (m - 2))
                            act.wait_ge(rec2_ok, m - 2)
                        act.activation(p2[:, v % 2, 0:keys], s2_ps[:, 0:keys], ACT.Exp, bias=nm2[:, v % 2:v % 2 + 1],
                                       accum_out=sum2[:, v % 2:v % 2 + 1]).then_inc(exp2, 1)
                    if live(3):
                        for bank in range(2):
                            act.wait_ge(mT_ps, 2 * (m - 3) + bank + 1)
                            if bank == 0 and not (first and t == 3):
                                act.wait_ge(y_ok, m - 3)
                            act.activation(mxT[:, 0, 4 * bank:4 * bank + 4, :],
                                           t_ps[:, bank, :].rearrange("p (g q) -> p g q", g=4), ACT.Copy).then_inc(mT_hi, 1)
                    if live(0):
                        if t == 1:
                            if not first:
                                act.wait_ge(pv2, m - 1)
                            act.wait_ge(kv_read, m)
                            act.activation(kv2[:, 0, :], kv_first[:, :], ACT.Copy).then_inc(kv_first_ok, 1)
                        act.wait_ge(qkv_ok, m + 1)
                        if not (first and t < 2):
                            act.wait_ge(qkt_ps, m - 1)
                        act.activation(qs[:, t % 2, 0, 0:DE], qkv_ps[:, 0:DE], ACT.Copy, scale=DE ** -0.5 / WSCALE).then_inc(hi2, 1)
                        act.activation(qs[:, t % 2, 1, :].rearrange("p (n d) -> p n d", n=2),
                                       qkv_ps[:, DE:2 * DE].unsqueeze(1).to_broadcast([P, 2, DE]), ACT.Copy,
                                       scale=1.0 / WSCALE).then_inc(hi2, 1)
                        if t == 0 and not first:
                            act.wait_ge(kv_first_ok, it)
                        act.activation(kv_first[:, :] if t == 0 else kv2[:, t, :], qkv_ps[:, DE:3 * DE],
                                       ACT.Copy, scale=1.0 / WSCALE).then_inc(kv_read, 1)

            tiles2(0, True, False)
            with act.Fori(1, B - 1) as it:
                tiles2(it, False, False)
            tiles2(B - 1, False, True)

        @block.vector
        def _(dve):
            def newton(y, v, t, u, sm, base):
                dve.tensor_tensor(t, v, y, ALU.mult).then_inc(sm, 1)
                dve.wait_ge(sm, base + 1)
                dve.tensor_tensor(u, t, y, ALU.mult).then_inc(sm, 1)
                dve.wait_ge(sm, base + 2)
                dve.tensor_scalar(u, u, -0.5, 1.5, ALU.mult, ALU.add).then_inc(sm, 1)
                dve.wait_ge(sm, base + 3)

            def tiles(ap):
                return ap.rearrange("p (t c) -> p t c", t=NT)

            def tokens(ap):
                return ap.unsqueeze(2).to_broadcast([P, NT, C])

            links = {}

            def link(ins, sm):
                links[sm.name] = links.get(sm.name, 0) + 1
                ins.then_inc(sm, 1)
                dve.wait_ge(sm, links[sm.name])

            def polished(y, v, t, u, sm):
                link(dve.tensor_tensor(t, v, y, ALU.mult), sm)
                link(dve.tensor_tensor(t, t, y, ALU.mult), sm)
                link(dve.tensor_scalar(t, t, -0.5, 1.5, ALU.mult, ALU.add), sm)
                link(dve.tensor_tensor(u, t, y, ALU.mult), sm)

            dve.wait_ge(const2_in, 16 * 2)
            dve.wait_ge(iota_ok, 1 + E)
            link(dve.tensor_tensor(small[:, 0, :], simn[:, :], simn[:, :], ALU.mult), c2_v)
            dve.wait_ge(c2_p, 1)
            link(dve.tensor_scalar(small[:, 1, :], misc_ps[:, 0:E], RSQ_SHIFT, RSQ_LEAST, ALU.mult, ALU.max), c2_v)
            dve.wait_ge(c2_a, 3)
            link(dve.tensor_scalar(small[:, 6, :], small[:, 6, :], 1.0, None, ALU.add), c2_v)
            link(dve.reciprocal(sgate[:, :], small[:, 6, :]), c2_v)
            polished(small[:, 3, :], small[:, 1, :], small[:, 4, :], small[:, 5, :], c2_v)
            link(dve.tensor_scalar(small[:, 5, :], small[:, 5, :], RSQ_SHIFT ** 0.5, 1.0 / GATE_LEAST, ALU.mult, ALU.min), c2_v)
            link(dve.tensor_tensor(simn[:, :], simn[:, :], small[:, 5, :], ALU.mult), c2_v)
            link(dve.tensor_copy(simn_split[:, 0, :], simn[:, :]), c2_v)
            link(dve.tensor_tensor(simn_split[:, 1, :], simn[:, :], simn_split[:, 0, :], ALU.subtract), c2_v)
            assert links[c2_v.name] == C2V

            def batch_sums(b):
                dve.wait_ge(x_in[b], 16)
                return dve.tensor_reduce(stat[:, 0, b * NT:(b + 1) * NT], resid[:, b * NT:(b + 1) * NT, :], AX.X, ALU.add)

            batch_sums(0).then_inc(ln_v, 1)
            dve.wait_ge(ln_v, 1)
            dve.tensor_scalar(stat[:, 1, 0:NT], stat[:, 0, 0:NT], -1.0 / C, None, ALU.mult).then_inc(ln_v, 1)
            dve.wait_ge(ln_v, 2)
            dve.tensor_tensor(tiles(xc[0]), resid[:, 0:NT, :], tokens(stat[:, 1, 0:NT]), ALU.add).then_inc(ln_v, 1)
            batch_sums(1).then_inc(ln_mean_v, 1)
            dve.wait_ge(ln_sq, 1)
            dve.tensor_reduce(stat[:, 0, 0:NT], tiles(xsq[0]), AX.X, ALU.add).then_inc(ln_v, 1)
            dve.wait_ge(ln_v, 4)
            dve.tensor_scalar(stat[:, 2, 0:NT], stat[:, 0, 0:NT], 1.0 / C, LN_EPS, ALU.mult, ALU.add).then_inc(ln_v, 1)
            dve.wait_ge(ln_y, 2)
            newton(stat[:, 4, 0:NT], stat[:, 2, 0:NT], stat[:, 5, 0:NT], stat[:, 6, 0:NT], ln_v, 5)
            dve.tensor_tensor(stat[:, 7, 0:NT], stat[:, 4, 0:NT], stat[:, 6, 0:NT], ALU.mult).then_inc(ln_v, 1)
            dve.wait_ge(ln_v, 9)
            dve.tensor_tensor(tiles(xn[0]), tiles(xc[0]), tokens(stat[:, 7, 0:NT]), ALU.mult).then_inc(ln_v, 1)
            batch_sums(2).then_inc(ln_mean_v, 1)
            dve.wait_ge(ln_T, 2)
            dve.tensor_copy(xnT[:, HALF:T], trans_ps[:, 1, :]).then_inc(ln_V, 1)
            batch_sums(3).then_inc(ln_mean_v, 1)
            dve.wait_ge(ln_mean_v, B - 1)
            dve.tensor_scalar(stat[:, 1, NT:], stat[:, 0, NT:], -1.0 / C, None, ALU.mult).then_inc(ln_mean, 1)

            def proj_low(part, j, src):
                kind, half = part[0], int(part[1])
                dve.wait_ge(high_ok[kind], 2 * j + half + 1)
                cols = slice(half * HALF, (half + 1) * HALF)
                row = 2 * "qk".index(kind)
                dve.scalar_tensor_tensor(out=split[:, row + 1, cols], in0=src,
                                         scalar=QSCALE if kind == "q" else 1.0, in1=split[:, row, cols],
                                         op0=ALU.mult, op1=ALU.subtract).then_inc(low_ok[kind], 1)

            for n, part in enumerate(AHEAD):
                if part[0] != "v":
                    proj_low(part, 0, ahead_ps[n])
            dve.wait_ge(const_in, 7 * 16)
            for n in range(2):
                dve.tensor_tensor(lam_pr[:, n, :], lam_in[:, 2 * n, :], lam_in[:, 2 * n + 1, :], ALU.mult).then_inc(lam_chain, 1)
            dve.wait_ge(lam_chain, 2)
            dve.tensor_reduce(lam[:, 0:2], lam_pr[:, :, :], AX.X, ALU.add).then_inc(lam_chain, 1)
            dve.tensor_scalar(wo_sb[:, :, :], wo_sb[:, :, :], gcol[:, :], 1.0 - LAMBDA_INIT, ALU.mult, ALU.mult).then_inc(wo_ok, 1)
            dve.wait_ge(lam_exp, 1)
            dve.tensor_tensor(lam[:, 4:5], lam[:, 3:4], lam[:, 2:3], ALU.subtract).then_inc(lam_chain, 1)
            dve.wait_ge(lam_chain, 4)
            dve.tensor_scalar(lam[:, 5:6], lam[:, 4:5], LAMBDA_INIT, None, ALU.subtract).then_inc(lam_ok, 1)
            dve.wait_ge(lam_ok, 1)
            for b in range(1, B):
                dve.wait_ge(ln_sq, b + 1)
                dve.tensor_reduce(stat[:, 0, b * NT:(b + 1) * NT], tiles(xsq[b]), AX.X, ALU.add).then_inc(ln_v, 1)
            dve.wait_ge(ln_v, 13)
            dve.tensor_scalar(stat[:, 2, NT:], stat[:, 0, NT:], 1.0 / C, LN_EPS, ALU.mult, ALU.add).then_inc(ln_v, 1)
            dve.wait_ge(ln_y, 4)
            newton(stat[:, 4, NT:], stat[:, 2, NT:], stat[:, 5, NT:], stat[:, 6, NT:], ln_v, 14)
            dve.tensor_tensor(stat[:, 7, NT:], stat[:, 4, NT:], stat[:, 6, NT:], ALU.mult).then_inc(ln_scale, 1)

            def rows(x, b):
                return x[:, b * NT:(b + 1) * NT, :]

            def per_tile(k, b):
                return gs[:, k, b * NT:(b + 1) * NT]

            def ln2_sum(b):
                dve.tensor_reduce(per_tile(0, b), rows(resid, b), AX.X, ALU.add).then_inc(g_sum, 1)

            def ln2_centre(b):
                dve.tensor_tensor(rows(x2c, b), rows(resid, b), tokens(per_tile(1, b)), ALU.add).then_inc(g_cV, 1)

            def ln2_square_sums(b):
                dve.wait_ge(g_sq, b + 1)
                dve.tensor_reduce(per_tile(7, b), tiles(x2sq[:, b, :]), AX.X, ALU.add).then_inc(g_ss, 1)

            def ln2_scale(b):
                dve.tensor_tensor(rows(x2n, b), rows(x2c, b), tokens(per_tile(0, b)), ALU.mult).then_inc(g_nV, 1)

            def ln2_early(step):
                if step == 0:
                    dve.wait_ge(resid_ok, 2 * G * EARLY)
                    for b in range(EARLY):
                        ln2_sum(b)
                    dve.wait_ge(g_sum, EARLY)
                    dve.tensor_scalar(gs[:, 1, 0:BT], gs[:, 0, 0:BT], -1.0 / C, None, ALU.mult).then_inc(g_mean, 1)
                elif step == 2:
                    dve.wait_ge(g_mean, 1)
                    dve.wait_ge(mix_ok, STEPS * UNITS)
                    for b in range(len(POOL_BATCHES), EARLY):
                        ln2_centre(b)
                elif step - 4 in range(EARLY):
                    ln2_square_sums(step - 4)
                    if step - 4 == EARLY - 1:
                        dve.wait_ge(g_ss, EARLY)
                        link(dve.tensor_scalar(gs[:, 2, 0:BT], gs[:, 7, 0:BT], 1.0 / C, LN_EPS, ALU.mult, ALU.add), g_v)
                elif step == 8:
                    dve.wait_ge(g_y, 2)
                    polished(gs[:, 4, 0:BT], gs[:, 2, 0:BT], gs[:, 5, 0:BT], gs[:, 0, 0:BT], g_v)
                    dve.tensor_copy(gs[:, 6, 0:BT], gs[:, 0, 0:BT]).then_inc(g_scale, 1)
                elif step == 10:
                    for b in range(len(POOL_BATCHES), EARLY):
                        ln2_scale(b)

            def slots(it, first, last):
                end = SLOTS - 8 + TAIL_SLOTS if last else SLOTS
                for s in range(end):
                    n = SLOTS * it + s

                    def row_max(n, s, sub):
                        dve.wait_ge(score_ok, 2 * n + sub + 1)
                        dve.tensor_reduce(negmax[:, s % 2, sub:sub + 1], score_ps[:, sub, :], AX.X, ALU.max,
                                          negate=True).then_inc(max_ok, 1)

                    if first and s == 0:
                        row_max(0, 0, 0)
                    r = (s - 1) % 2
                    last_unit = not (first and s < 1) and not (last and s > SLOTS)
                    if last_unit:
                        half, u = ((s - 1) // 8) % 4, (s - 1) % 8
                        dve.wait_ge(exp_ok, 2 * n)
                        dve.reciprocal(recip2[:, r:r + 1], sums[:, half, 1, u:u + 1]).then_inc(rec_ok, 1)
                        dve.wait_ge(rec_ok, n)
                        dve.scalar_tensor_tensor(out=ccol[:, (s - 1) % 4:(s - 1) % 4 + 1], in0=recip2[:, r:r + 1], scalar=lam[:, 5:6],
                                                 in1=sums[:, half, 0, u:u + 1], op0=ALU.mult,
                                                 op1=ALU.mult).then_inc(c_ok, 1)
                    norm = half_at(s, NORM_LAG, first, last)
                    if norm is not None:
                        k = 3 * (4 * it + norm)
                        dve.wait_ge(rms_v, 4 * (4 * it + norm + 1))
                        dve.reciprocal(tl[:, 6, :], tl[:, 5, :]).then_inc(norm_v, 1)
                    if s < SLOTS:
                        row_max(n, s, 1)
                    if norm is not None:
                        dve.wait_ge(norm_v, k + 1)
                        dve.tensor_tensor(tl[:, 7, :], tl[:, 6, :], tl[:, 1, :], ALU.mult).then_inc(norm_v, 1)
                    fill = None if first and s < 1 else misc_fill(s - 1, first, last)
                    if fill and fill[0] in PARTS and fill[0][0] != "v":
                        proj_low(fill[0], 2 * it + fill[1], misc_ps[:, :])
                    half = half_at(s, PROJECT_LAG + 1, first, last)
                    if half is not None:
                        step = 2 * it + half // 2
                        tile0 = (step // G) * NT + (half % 2) * 4
                        dve.wait_ge(out_ok, 4 * it + half + 1)
                        rows = resid[:, bass.ds(tile0, 4), :]
                        dve.tensor_tensor(rows, rows, misc_ps[:, :].rearrange("p (t c) -> p t c", t=4),
                                          ALU.add).then_inc(resid_ok, 1)
                    if last_unit:
                        dve.wait_ge(c_ok, n)
                        dve.tensor_scalar(prob2[:, (s - 1) % 4, 0:SCALE_V], prob2[:, (s - 1) % 4, 0:SCALE_V],
                                          ccol[:, (s - 1) % 4:(s - 1) % 4 + 1], None, ALU.mult).then_inc(scaled_V, 1)
                    if s + 1 < SLOTS or not last:
                        row_max(n + 1, s + 1, 0)
                    if dve_copies(s):
                        copy_probT(dve, dve.tensor_copy, s, n, it, 1, first, last)
                    half = half_at(s, STAT_LAG, first, last)
                    if half is not None:
                        if not (first and half == 0):
                            dve.wait_ge(norm_v, 3 * (4 * it + half))
                        dve.reciprocal(tl[:, 1, :], sums[:, half % 4, 0, :]).then_inc(stat_ok, 1)
                        dve.wait_ge(attn_copied, 2 * (4 * it + half + 1))
                        dve.tensor_reduce(tl[:, 0, :].rearrange("p (h t) -> p h t", h=2),
                                          attn_sq[:, :, :, :].rearrange("p t h d -> p h t d"), AX.X, ALU.add).then_inc(stat_ok, 1)
                    if norm is not None:
                        dve.wait_ge(norm_v, k + 2)
                        dve.tensor_tensor(attn_n[:, :, :, :], attn[:, :, :, :],
                                          tl[:, 7, :].rearrange("p (h t) -> p t h", h=2).unsqueeze(3).to_broadcast([P, 4, 2, DV]),
                                          ALU.mult).then_inc(norm_v, 1)
                    if last and s >= LN2_SLOT:
                        ln2_early(s - LN2_SLOT)

            slots(0, True, False)
            with dve.Fori(1, ITERS - 1) as it:
                slots(it, False, False)
            slots(ITERS - 1, False, True)

            def empty_gate(n):
                for half in range(2):
                    dve.wait_ge(g_A, 2 * n + half + 1)
                    cols = slice(half * HALF, (half + 1) * HALF)
                    dve.tensor_tensor(x2T[:, n % 2, 1, cols], gate_ps(n, half), x2T[:, n % 2, 0, cols],
                                      ALU.subtract).then_inc(g_V, 1)

            last_b = B - 1
            dve.wait_ge(resid_ok, 2 * STEPS)
            ln2_sum(last_b)
            dve.wait_ge(g_sum, B)
            dve.tensor_scalar(gs[:, 1, BT:], gs[:, 0, BT:], -1.0 / C, None, ALU.mult).then_inc(g_mean, 1)
            dve.wait_ge(g_mean, 2)
            ln2_centre(last_b)
            empty_gate(0)
            ln2_square_sums(last_b)
            dve.wait_ge(g_ss, B)
            link(dve.tensor_scalar(gs[:, 2, BT:], gs[:, 7, BT:], 1.0 / C, LN_EPS, ALU.mult, ALU.add), g_v)
            assert links[g_v.name] == GLATE
            dve.wait_ge(g_y, 4)
            polished(gs[:, 4, BT:], gs[:, 2, BT:], gs[:, 5, BT:], gs[:, 0, BT:], g_v)
            ln2_scale(last_b)
            empty_gate(1)
            link(dve.tensor_tensor(gs[:, 5, :], gs[:, 0, :], gs[:, 0, :], ALU.mult), g_v)
            link(dve.tensor_tensor(gs[:, 5, :], gs[:, 5, :], gs[:, 7, :], ALU.mult), g_v)
            link(dve.tensor_scalar(gs[:, 2, :], gs[:, 5, :], RSQ_SHIFT, RSQ_LEAST, ALU.mult, ALU.max), g_v)
            assert links[g_v.name] == GNORM

            dve.wait_ge(g_y, 6)
            polished(gs[:, 4, :], gs[:, 2, :], gs[:, 5, :], gs[:, 3, :], g_v)
            link(dve.tensor_scalar(gs[:, 3, :], gs[:, 3, :], RSQ_SHIFT ** 0.5, 1.0 / GATE_LEAST, ALU.mult, ALU.min), g_v)
            for n in range(2, B):
                empty_gate(n)

            NTB = B * NT

            def per_token(ap):
                return ap.unsqueeze(2).to_broadcast([P, NTB, E])

            def per_expert(ap):
                return ap.unsqueeze(1).to_broadcast([P, NTB, E])

            dve.wait_ge(g_lg, B)
            lg = gl[:, 0, :, :]
            link(dve.tensor_tensor(gl[:, 1, :, :], qkv_ps[:, :].rearrange("p (t e) -> p t e", t=NTB),
                                   per_token(gs[:, 3, :]), ALU.mult), g_v)
            link(dve.tensor_tensor(lg, gl[:, 1, :, :], per_expert(sgate[:, :]), ALU.subtract), g_v)
            for t in range(NTB):
                dve.max(out=top8[:, t, :], in_=lg[:, t, :]).then_inc(g_top, 1)
            dve.wait_ge(g_top, NTB)
            for t in range(NTB):
                dve.max_index(out=top8i[:, t, :], in_max=top8[:, t, :], in_values=lg[:, t, :]).then_inc(g_top, 1)
            best = top8[:, :, 0:1].rearrange("p t a -> p (t a)")
            link(dve.tensor_scalar(gs[:, 1, :], best, 0.0, None, ALU.max), g_v)
            link(dve.scalar_tensor_tensor(out=gl[:, 7, :, :], in0=lg, scalar=0.0, in1=per_token(gs[:, 1, :]),
                                          op0=ALU.max, op1=ALU.subtract), g_v)
            assert links[g_v.name] == GEXP, links
            dve.tensor_scalar(gs[:, 0, :], best, 0.0, float(E), ALU.is_gt, ALU.mult).then_inc(g_top, 1)
            dve.wait_ge(g_top, 2 * NTB + 1)
            link(dve.tensor_copy(top2f[:, :, :], top8i[:, :, 0:2]), g_v)
            link(dve.tensor_tensor(top2f[:, :, :], top2f[:, :, :], gs[:, 0, :].unsqueeze(2).to_broadcast([P, NTB, 2]), ALU.add), g_v)
            for n in range(2):
                dve.tensor_tensor(gl[:, 2 + n, :, :], per_expert(iota[:, :]),
                                  top2f[:, :, n:n + 1].to_broadcast([P, NTB, E]), ALU.is_equal).then_inc(g_top, 1)
            dve.wait_ge(g_top, 2 * NTB + 3)
            link(dve.tensor_tensor(gl[:, 4, :, :], gl[:, 2, :, :], gl[:, 3, :, :], ALU.add), g_v)
            link(dve.scalar_tensor_tensor(out=gl[:, 5, :, :], in0=lg, scalar=0.0, in1=gl[:, 4, :, :],
                                          op0=ALU.is_gt, op1=ALU.add), g_v)
            dve.wait_ge(g_exp, 1)
            link(dve.tensor_tensor(gl[:, 9, :, :], gl[:, 8, :, :], gl[:, 5, :, :], ALU.mult), g_v)
            link(dve.tensor_reduce(gs[:, 0, :], gl[:, 9, :, :], AX.X, ALU.add), g_v)
            link(dve.reciprocal(gs[:, 1, :], gs[:, 0, :]), g_v)
            link(dve.tensor_tensor(rw_all[:, :, :], gl[:, 9, :, :], per_token(gs[:, 1, :]), ALU.mult), rw_ok)

            def tiles2(it, first, last):
                for t in range(NT + PART2_LAG if last else NT):
                    m = NT * it + t

                    def live(lag):
                        return not (first and t < lag) and not (last and t - lag >= NT)

                    def x_copy(group):
                        if not live(0):
                            return
                        dve.wait_ge(xT_hi, 4 * m + group + 1)
                        dve.tensor_tensor(xsT[:, t % 2, 1, 4 * group:4 * group + 4, :],
                                          t_ps[:, group % 2, :].rearrange("p (e q) -> p e q", e=4),
                                          xsT[:, t % 2, 0, 4 * group:4 * group + 4, :], ALU.subtract).then_inc(xT_lo, 1)

                    x_copy(0)
                    x_copy(1)
                    if live(4):
                        v = (t - 4) % NT
                        dve.wait_ge(y_ok, m - 3)
                        if not (first and t < 6):
                            dve.wait_ge(stored[v % 2], 16 * (4 * it + (t - 6) // 2 + 1))
                        dve.scalar_tensor_tensor(out=yo[:, v % 2:v % 2 + 1, :], in0=y_ps[:, 0:C].unsqueeze(1), scalar=1.0 / WSCALE,
                                                 in1=resid[:, bass.ds(m - 4, 1), :], op0=ALU.mult, op1=ALU.add).then_inc(y_done, 1)
                    if live(2):
                        v = (t - 2) % NT
                        if v >= 4:
                            dve.wait_ge(pT_ps, 2 * (m - 1))
                            if not (first and t == 2):
                                dve.wait_ge(pv2, m - 2)
                            dve.tensor_copy(p2T[:, 4:v + 1, :],
                                            t_ps[:, 1, 0:(v - 3) * P].rearrange("p (k q) -> p k q", k=v - 3)).then_inc(pT_V, 1)
                        else:
                            dve.sem_inc(pT_V, 1)
                    if live(1):
                        v = (t - 1) % NT
                        dve.wait_ge(s2_ok, m)
                        dve.tensor_reduce(nm2[:, v % 2:v % 2 + 1], s2_ps[:, 0:(v + 1) * P], AX.X, ALU.max, negate=True).then_inc(max2, 1)
                    x_copy(2)
                    x_copy(3)
                    if live(2):
                        v = (t - 2) % NT
                        dve.wait_ge(exp2, m - 1)
                        dve.reciprocal(rec2[:, v % 2:v % 2 + 1], sum2[:, v % 2:v % 2 + 1]).then_inc(rec2_ok, 1)
                        dve.wait_ge(pv2, m - 1)
                        dve.wait_ge(rec2_ok, m - 1)
                        if not (first and t < 4):
                            dve.wait_ge(mT_ps, 2 * (m - 3))
                        dve.scalar_tensor_tensor(out=mx[:, v % 2, :, :], in0=o2_ps[:, DE:2 * DE].unsqueeze(1).to_broadcast([P, E, DE]),
                                                 scalar=rec2[:, v % 2:v % 2 + 1],
                                                 in1=rw_all[:, bass.ds(m - 2, 1), :].rearrange("p a e -> p e a").to_broadcast([P, E, DE]),
                                                 op0=ALU.mult, op1=ALU.mult).then_inc(mx_ok, 1)
                    if live(3):
                        for bank in range(2):
                            dve.wait_ge(mT_hi, 2 * (m - 3) + bank + 1)
                            dve.tensor_tensor(mxT[:, 1, 4 * bank:4 * bank + 4, :],
                                              t_ps[:, bank, :].rearrange("p (g q) -> p g q", g=4),
                                              mxT[:, 0, 4 * bank:4 * bank + 4, :], ALU.subtract).then_inc(mT_lo, 1)
                    if live(0):
                        dve.wait_ge(hi2, 2 * (m + 1))
                        dve.wait_ge(kv_read, m + 1)
                        dve.scalar_tensor_tensor(out=qs[:, t % 2, 0, DE:2 * DE], in0=qkv_ps[:, 0:DE], scalar=DE ** -0.5 / WSCALE,
                                                 in1=qs[:, t % 2, 0, 0:DE], op0=ALU.mult, op1=ALU.subtract).then_inc(lo2, 1)
                        dve.scalar_tensor_tensor(out=qs[:, t % 2, 2, :].rearrange("p (n d) -> p n d", n=2),
                                                 in0=qkv_ps[:, DE:2 * DE].unsqueeze(1).to_broadcast([P, 2, DE]), scalar=1.0 / WSCALE,
                                                 in1=qs[:, t % 2, 1, :].rearrange("p (n d) -> p n d", n=2),
                                                 op0=ALU.mult, op1=ALU.subtract).then_inc(lo2, 1)

            tiles2(0, True, False)
            with dve.Fori(1, B - 1) as it:
                tiles2(it, False, False)
            tiles2(B - 1, False, True)


_INS = ["L0_attn_x", "L0_attn_Wq", "L0_attn_Wkv", "L0_attn_Wout", "L0_attn_lambda_q1", "L0_attn_lambda_k1",
        "L0_attn_lambda_q2", "L0_attn_lambda_k2", "L0_attn_gamma", "L0_ffn_sim_matrix", "L0_ffn_gates",
        "L0_ffn_q_proj", "L0_ffn_k_proj", "L0_ffn_v_proj", "L0_ffn_o_proj"]


def kernel(**inputs):
    import concourse.bacc as bacc
    from concourse.bass_utils import run_bass_kernel_spmd

    nc = bacc.Bacc("TRN2", target_bir_lowering=False, num_devices=1)
    arrays, args = {}, []
    for name in _INS:
        a = np.ascontiguousarray(inputs[name])
        arrays[f"in_{name}"] = a
        args.append(nc.dram_tensor(f"in_{name}", a.shape, mybir.dt.from_np(a.dtype), kind="ExternalInput").ap())
    out = nc.dram_tensor("out_0", (B, T, C), F32, kind="ExternalOutput").ap()
    block_kernel(nc, *args, out)
    r = run_bass_kernel_spmd(nc, [arrays], core_ids=[0])
    return r.results[0]["out_0"]
```
